# Optimizing a Trainium2 kernel written in Bass

```python
import numpy as np
import jax
import jax.numpy as jnp

def _softmax(x, axis=-1):
    return jax.nn.softmax(x, axis=axis)

def _gelu(x):
    return jax.nn.gelu(x, approximate=True)

def _silu(x):
    return jax.nn.silu(x)

def _sigmoid(x):
    return jax.nn.sigmoid(x)

def _layernorm(x, axis=-1, eps=1e-05):
    m = jnp.mean(x, axis=axis, keepdims=True)
    v = jnp.var(x, axis=axis, keepdims=True)
    return (x - m) / jnp.sqrt(v + eps)

def _scatter_add(tgt, idx, src, axis=0):
    return tgt.at[idx].add(src)

def _segment_sum(src, seg, n):
    return jax.ops.segment_sum(src, seg, n)
kernel_name = 'mk_early_fusion_d1_tok_img4096_r4_9874d1'

def setup_inputs(seed: int=0):
    np.random.seed(seed)
    _w = jnp.asarray

    def _rec_inputs():
        import jax
        import jax.numpy as jnp
        _rk = jax.random.key(seed)
        x = -0.00348982 + 0.707501 * jax.random.normal(jax.random.fold_in(_rk, 1), (16, 128, 64, 2), jnp.float32)
        txt = 6.73332e-06 + 0.02 * jax.random.normal(jax.random.fold_in(_rk, 2), (16, 128, 1024), jnp.float32)
        return (x, txt)
    x, txt = _rec_inputs()

    def _L0_tok_setup():
        import jax, jax.numpy as jnp
        import numpy as np
        H, N, S, CH, LEN = (128, 64, 128, 1, 1024)

        def _s4d_kernel(log_dt, C, B, inv_A_real, A_imag, L):
            dt = jnp.exp(log_dt)
            Cc = C[..., 0] + 1j * C[..., 1]
            Bc = B[..., 0] + 1j * B[..., 1]
            A = -jnp.exp(inv_A_real) + 1j * A_imag
            rep = H // A.shape[0]
            A = jnp.tile(A, (rep, 1))
            Bc = jnp.tile(Bc, (rep, 1))
            dtA = A * dt[:, None]
            Cc = Bc[None, :, :] * Cc
            Cc = Cc * (jnp.exp(dtA) - 1.0) / A
            ell = jnp.arange(L, dtype=jnp.float32)
            V = jnp.exp(dtA[:, :, None] * ell)
            K = 2.0 * jnp.einsum('chn,hnl->chl', Cc, V).real
            return K.astype(jnp.float32)
        key = jax.random.key(seed)
        k1, k2 = jax.random.split(key, 2)
        log_dt = jax.random.uniform(k1, (H,), minval=float(np.log(0.001)), maxval=float(np.log(0.1))).astype(jnp.float32)
        inv_A_real = jnp.full((S, N), float(np.log(0.5)), dtype=jnp.float32)
        A_imag = jnp.tile((np.pi * jnp.arange(N, dtype=jnp.float32))[None, :], (S, 1))
        B = jnp.stack([jnp.ones((S, N), jnp.float32), jnp.zeros((S, N), jnp.float32)], axis=-1)
        C = (jax.random.normal(k2, (CH, H, N, 2)) * 0.5 ** 0.5).astype(jnp.float32)
        return {'log_dt': log_dt, 'C': C, 'B': B, 'inv_A_real': inv_A_real, 'A_imag': A_imag, 'L': LEN}
    _L0_tok_all = _L0_tok_setup()
    _L0_tok_in = {k: v for k, v in _L0_tok_all.items() if k in ('log_dt', 'B', 'inv_A_real', 'A_imag')}
    del _L0_tok_all

    def _L0_attn_setup():
        import jax, jax.numpy as jnp
        import numpy as np
        DEPTH, DIM, DFF, VOCAB = (4, 128, 512, 1024)
        EPS = 1e-05

        def layernorm(x, w, b):
            mu = jnp.mean(x, axis=-1, keepdims=True)
            var = jnp.mean((x - mu) ** 2, axis=-1, keepdims=True)
            return (x - mu) * jax.lax.rsqrt(var + EPS) * w + b

        def sconv(x, phazor_c, last_conv_c):
            B, L, D = x.shape
            r = jnp.abs(phazor_c)
            p = jnp.tanh(r) * jnp.exp(1j * jnp.angle(phazor_c))
            prog = p[None, :] ** jnp.arange(L, dtype=jnp.float32)[:, None]
            filt_fft = jnp.fft.fft(prog, n=2 * L, axis=0)
            x_fft = jnp.fft.fft(x.astype(jnp.complex64), n=2 * L, axis=1)
            conv = jnp.fft.ifft(filt_fft[None] * x_fft, axis=1)[:, :L]
            conv = conv + last_conv_c[None, None, :] * prog[None] * p[None, None, :]
            return conv.real.astype(x.dtype)

        def _forward(x, Win, bin, ln1_w, ln1_b, phz_re, phz_im, lc_re, lc_im, sc_lin, ln2_w, ln2_b, W1, b1, W2, b2, lnl_w, lnl_b, Wout, bout):
            h = jnp.einsum('blv,dv->bld', x, Win) + bin

            def body(h, p):
                l1w, l1b, pr, pi, lr, li, scl, l2w, l2b, w1, b1_, w2, b2_ = p
                y = jax.nn.silu(layernorm(h, l1w, l1b))
                y = sconv(y, pr + 1j * pi, lr + 1j * li)
                h = h + y * scl
                y = layernorm(h, l2w, l2b)
                y = jax.nn.silu(jnp.einsum('bld,fd->blf', y, w1) + b1_)
                y = jnp.einsum('blf,df->bld', y, w2) + b2_
                return (h + y, None)
            xs = (ln1_w, ln1_b, phz_re, phz_im, lc_re, lc_im, sc_lin, ln2_w, ln2_b, W1, b1, W2, b2)
            h, _ = jax.lax.scan(body, h, xs)
            h = layernorm(h, lnl_w, lnl_b)
            return jnp.einsum('bld,vd->blv', h, Wout) + bout
        key = jax.random.key(seed)
        ks = jax.random.split(key, 20)
        f32 = jnp.float32
        inp = {}
        inp['x'] = jax.random.normal(ks[0], (2, 1024, VOCAB), dtype=f32)
        inp['Win'] = jax.random.normal(ks[1], (DIM, VOCAB), dtype=f32) * VOCAB ** (-0.5)
        inp['bin'] = jnp.zeros((DIM,), f32)
        inp['ln1_w'] = jnp.ones((DEPTH, DIM), f32)
        inp['ln1_b'] = jnp.zeros((DEPTH, DIM), f32)
        ang = 2 * np.pi * jnp.arange(DIM, dtype=f32) / DIM
        mag = jnp.abs(jax.random.normal(ks[2], (DEPTH, DIM), dtype=f32))
        inp['phz_re'] = mag * jnp.cos(ang)[None]
        inp['phz_im'] = mag * jnp.sin(ang)[None]
        inp['lc_re'] = jax.random.normal(ks[3], (DEPTH, DIM), dtype=f32)
        inp['lc_im'] = jax.random.normal(ks[4], (DEPTH, DIM), dtype=f32)
        inp['sc_lin'] = jnp.ones((DEPTH, DIM), f32)
        inp['ln2_w'] = jnp.ones((DEPTH, DIM), f32)
        inp['ln2_b'] = jnp.zeros((DEPTH, DIM), f32)
        inp['W1'] = jax.random.normal(ks[5], (DEPTH, DFF, DIM), dtype=f32) * DIM ** (-0.5)
        inp['b1'] = jnp.zeros((DEPTH, DFF), f32)
        inp['W2'] = jax.random.normal(ks[6], (DEPTH, DIM, DFF), dtype=f32) * DFF ** (-0.5)
        inp['b2'] = jnp.zeros((DEPTH, DIM), f32)
        inp['lnl_w'] = jnp.ones((DIM,), f32)
        inp['lnl_b'] = jnp.zeros((DIM,), f32)
        inp['Wout'] = jax.random.normal(ks[7], (VOCAB, DIM), dtype=f32) * DIM ** (-0.5)
        inp['bout'] = jnp.zeros((VOCAB,), f32)
        return inp
    _L0_attn_all = _L0_attn_setup()
    _L0_attn_in = {k: v for k, v in _L0_attn_all.items() if k in ('Win', 'bin', 'ln1_w', 'ln1_b', 'phz_re', 'phz_im', 'lc_re', 'lc_im', 'sc_lin', 'ln2_w', 'ln2_b', 'W1', 'b1', 'W2', 'b2', 'lnl_w', 'lnl_b', 'Wout', 'bout')}
    del _L0_attn_all

    def _L0_ffn_setup():
        import jax, jax.numpy as jnp
        import numpy as np
        B, S, D_IN, D_OUT = (2, 512, 1024, 1024)
        E, K, R = (8, 2, 16)
        SCALING = 32.0 / 16.0
        key = jax.random.key(seed)
        ks = jax.random.split(key, 6)
        x = jax.random.normal(ks[0], (B, S, D_IN), dtype=jnp.float32)
        gate_w = jax.random.normal(ks[1], (E, D_IN), dtype=jnp.float32) * 0.02
        base_w = jax.random.normal(ks[2], (D_OUT, D_IN), dtype=jnp.float32) * 0.02
        base_b = jax.random.normal(ks[3], (D_OUT,), dtype=jnp.float32) * 0.02
        lora_A = jax.random.normal(ks[4], (E, R, D_IN), dtype=jnp.float32) * 0.02
        lora_B = jax.random.normal(ks[5], (E, D_OUT, R), dtype=jnp.float32) * 0.02
        return {'x': x, 'gate_w': gate_w, 'base_w': base_w, 'base_b': base_b, 'lora_A': lora_A, 'lora_B': lora_B}
    _L0_ffn_all = _L0_ffn_setup()
    _L0_ffn_in = {k: v for k, v in _L0_ffn_all.items() if k in ('gate_w', 'base_w', 'base_b', 'lora_A', 'lora_B')}
    del _L0_ffn_all
    return {'x': x, 'txt': txt, 'L0_tok_log_dt': _L0_tok_in['log_dt'], 'L0_tok_B': _L0_tok_in['B'], 'L0_tok_inv_A_real': _L0_tok_in['inv_A_real'], 'L0_tok_A_imag': _L0_tok_in['A_imag'], 'L0_attn_Win': _L0_attn_in['Win'], 'L0_attn_bin': _L0_attn_in['bin'], 'L0_attn_ln1_w': _L0_attn_in['ln1_w'], 'L0_attn_ln1_b': _L0_attn_in['ln1_b'], 'L0_attn_phz_re': _L0_attn_in['phz_re'], 'L0_attn_phz_im': _L0_attn_in['phz_im'], 'L0_attn_lc_re': _L0_attn_in['lc_re'], 'L0_attn_lc_im': _L0_attn_in['lc_im'], 'L0_attn_sc_lin': _L0_attn_in['sc_lin'], 'L0_attn_ln2_w': _L0_attn_in['ln2_w'], 'L0_attn_ln2_b': _L0_attn_in['ln2_b'], 'L0_attn_W1': _L0_attn_in['W1'], 'L0_attn_b1': _L0_attn_in['b1'], 'L0_attn_W2': _L0_attn_in['W2'], 'L0_attn_b2': _L0_attn_in['b2'], 'L0_attn_lnl_w': _L0_attn_in['lnl_w'], 'L0_attn_lnl_b': _L0_attn_in['lnl_b'], 'L0_attn_Wout': _L0_attn_in['Wout'], 'L0_attn_bout': _L0_attn_in['bout'], 'L0_ffn_gate_w': _L0_ffn_in['gate_w'], 'L0_ffn_base_w': _L0_ffn_in['base_w'], 'L0_ffn_base_b': _L0_ffn_in['base_b'], 'L0_ffn_lora_A': _L0_ffn_in['lora_A'], 'L0_ffn_lora_B': _L0_ffn_in['lora_B']}

def reference(x, txt, L0_tok_log_dt, L0_tok_B, L0_tok_inv_A_real, L0_tok_A_imag, L0_attn_Win, L0_attn_bin, L0_attn_ln1_w, L0_attn_ln1_b, L0_attn_phz_re, L0_attn_phz_im, L0_attn_lc_re, L0_attn_lc_im, L0_attn_sc_lin, L0_attn_ln2_w, L0_attn_ln2_b, L0_attn_W1, L0_attn_b1, L0_attn_W2, L0_attn_b2, L0_attn_lnl_w, L0_attn_lnl_b, L0_attn_Wout, L0_attn_bout, L0_ffn_gate_w, L0_ffn_base_w, L0_ffn_base_b, L0_ffn_lora_A, L0_ffn_lora_B):
    import jax
    import jax.numpy as jnp

    def _L0_tok_ref(log_dt, C, B, inv_A_real, A_imag, L):
        import jax, jax.numpy as jnp
        import numpy as np
        H, N, S, CH, LEN = (128, 64, 128, 1, 1024)

        def _s4d_kernel(log_dt, C, B, inv_A_real, A_imag, L):
            dt = jnp.exp(log_dt)
            Cc = C[..., 0] + 1j * C[..., 1]
            Bc = B[..., 0] + 1j * B[..., 1]
            A = -jnp.exp(inv_A_real) + 1j * A_imag
            rep = H // A.shape[0]
            A = jnp.tile(A, (rep, 1))
            Bc = jnp.tile(Bc, (rep, 1))
            dtA = A * dt[:, None]
            Cc = Bc[None, :, :] * Cc
            Cc = Cc * (jnp.exp(dtA) - 1.0) / A
            ell = jnp.arange(L, dtype=jnp.float32)
            V = jnp.exp(dtA[:, :, None] * ell)
            K = 2.0 * jnp.einsum('chn,hnl->chl', Cc, V).real
            return K.astype(jnp.float32)
        return _s4d_kernel(log_dt, C, B, inv_A_real, A_imag, L)

    def _L0_attn_ref(x, Win, bin, ln1_w, ln1_b, phz_re, phz_im, lc_re, lc_im, sc_lin, ln2_w, ln2_b, W1, b1, W2, b2, lnl_w, lnl_b, Wout, bout):
        import jax, jax.numpy as jnp
        import numpy as np
        DEPTH, DIM, DFF, VOCAB = (4, 128, 512, 1024)
        EPS = 1e-05

        def layernorm(x, w, b):
            mu = jnp.mean(x, axis=-1, keepdims=True)
            var = jnp.mean((x - mu) ** 2, axis=-1, keepdims=True)
            return (x - mu) * jax.lax.rsqrt(var + EPS) * w + b

        def sconv(x, phazor_c, last_conv_c):
            B, L, D = x.shape
            r = jnp.abs(phazor_c)
            p = jnp.tanh(r) * jnp.exp(1j * jnp.angle(phazor_c))
            prog = p[None, :] ** jnp.arange(L, dtype=jnp.float32)[:, None]
            filt_fft = jnp.fft.fft(prog, n=2 * L, axis=0)
            x_fft = jnp.fft.fft(x.astype(jnp.complex64), n=2 * L, axis=1)
            conv = jnp.fft.ifft(filt_fft[None] * x_fft, axis=1)[:, :L]
            conv = conv + last_conv_c[None, None, :] * prog[None] * p[None, None, :]
            return conv.real.astype(x.dtype)

        def _forward(x, Win, bin, ln1_w, ln1_b, phz_re, phz_im, lc_re, lc_im, sc_lin, ln2_w, ln2_b, W1, b1, W2, b2, lnl_w, lnl_b, Wout, bout):
            h = jnp.einsum('blv,dv->bld', x, Win) + bin

            def body(h, p):
                l1w, l1b, pr, pi, lr, li, scl, l2w, l2b, w1, b1_, w2, b2_ = p
                y = jax.nn.silu(layernorm(h, l1w, l1b))
                y = sconv(y, pr + 1j * pi, lr + 1j * li)
                h = h + y * scl
                y = layernorm(h, l2w, l2b)
                y = jax.nn.silu(jnp.einsum('bld,fd->blf', y, w1) + b1_)
                y = jnp.einsum('blf,df->bld', y, w2) + b2_
                return (h + y, None)
            xs = (ln1_w, ln1_b, phz_re, phz_im, lc_re, lc_im, sc_lin, ln2_w, ln2_b, W1, b1, W2, b2)
            h, _ = jax.lax.scan(body, h, xs)
            h = layernorm(h, lnl_w, lnl_b)
            return jnp.einsum('bld,vd->blv', h, Wout) + bout
        return _forward(x, Win, bin, ln1_w, ln1_b, phz_re, phz_im, lc_re, lc_im, sc_lin, ln2_w, ln2_b, W1, b1, W2, b2, lnl_w, lnl_b, Wout, bout)

    def _L0_ffn_ref(x, gate_w, base_w, base_b, lora_A, lora_B):
        import jax, jax.numpy as jnp
        import numpy as np
        B, S, D_IN, D_OUT = (2, 512, 1024, 1024)
        E, K, R = (8, 2, 16)
        SCALING = 32.0 / 16.0
        gate_logits = jnp.einsum('bsd,ed->bse', x, gate_w)
        weights, selected = jax.lax.top_k(gate_logits, K)
        weights = jax.nn.softmax(weights.astype(jnp.float32), axis=2).astype(x.dtype)
        result = jnp.einsum('bsd,od->bso', x, base_w) + base_b
        w_full = jnp.sum(jax.nn.one_hot(selected, E, dtype=x.dtype) * weights[..., None], axis=2)
        low = jnp.einsum('bsd,erd->ebsr', x, lora_A)
        lora_out = jnp.einsum('ebsr,eor,bse->bso', low, lora_B, w_full)
        result = result + SCALING * lora_out
        return result
    h = _L0_tok_ref(L0_tok_log_dt, x, L0_tok_B, L0_tok_inv_A_real, L0_tok_A_imag, 1024)
    h = jnp.concatenate([h, txt], axis=1)
    h = h + _L0_attn_ref(_layernorm(h, axis=-1), L0_attn_Win, L0_attn_bin, L0_attn_ln1_w, L0_attn_ln1_b, L0_attn_phz_re, L0_attn_phz_im, L0_attn_lc_re, L0_attn_lc_im, L0_attn_sc_lin, L0_attn_ln2_w, L0_attn_ln2_b, L0_attn_W1, L0_attn_b1, L0_attn_W2, L0_attn_b2, L0_attn_lnl_w, L0_attn_lnl_b, L0_attn_Wout, L0_attn_bout)
    h = h + _L0_ffn_ref(_layernorm(h, axis=-1), L0_ffn_gate_w, L0_ffn_base_w, L0_ffn_base_b, L0_ffn_lora_A, L0_ffn_lora_B)
    return h

_drawn_inputs = setup_inputs


def setup_inputs(seed=0):
    import zlib

    import numpy as np

    out = dict(_drawn_inputs(seed))
    spreads = {'L0_tok_inv_A_real': (-0.6931471824645996, 0.2),
     'L0_attn_bin': (0.0, 0.1),
     'L0_attn_ln1_w': (1.0, 0.2),
     'L0_attn_ln1_b': (0.0, 0.1),
     'L0_attn_sc_lin': (1.0, 0.2),
     'L0_attn_ln2_w': (1.0, 0.2),
     'L0_attn_ln2_b': (0.0, 0.1),
     'L0_attn_b1': (0.0, 0.1),
     'L0_attn_b2': (0.0, 0.1),
     'L0_attn_lnl_w': (1.0, 0.2),
     'L0_attn_lnl_b': (0.0, 0.1),
     'L0_attn_bout': (0.0, 0.1)}
    factors = {'L0_ffn_base_b': 3.523}
    for name, (base, spread) in spreads.items():
        noise = np.random.default_rng([zlib.crc32(name.encode()), seed]).standard_normal(out[name].shape)
        drawn = base * np.exp(spread * noise) if base else spread * noise
        out[name] = jnp.asarray(drawn.astype(out[name].dtype))
    for name, factor in factors.items():
        out[name] = (out[name] * factor).astype(out[name].dtype)
    return out
```

```python
from contextlib import ExitStack

import numpy as np

import concourse.bass as bass
from concourse import mybir

F32 = mybir.dt.float32
F32R = mybir.dt.float32r
BF16 = mybir.dt.bfloat16
U32 = mybir.dt.uint32
ALU = mybir.AluOpType
ACT = mybir.ActivationFunctionType
AX = mybir.AxisListType

P = 128
BATCH = 16
SEQ = 256
TOK = 128
VOC = 1024
KC = VOC // P
STATES = 64
DIM = 128
DFF = 512
FC = DFF // P
DEPTH = 4
EXPERTS = 8
RANK = 16
EPS = 1e-5

NA, NB1, NB0 = 8, 8, 16
NJ = NA + NB1 + NB0
H_CHUNK = 32
H_BLOCK = 8
N_CHUNK = TOK // H_CHUNK
BLOCKS = H_CHUNK // H_BLOCK
N_PAIR = BATCH

TWO_PI = 2.0 * np.pi
INV_2PI = float(np.float32(1.0 / TWO_PI))
PI2_A = 6.28125
PI2_B = float(np.float32(round((TWO_PI - PI2_A) * 2**21) / 2**21))
PI2_C = float(np.float32(TWO_PI - PI2_A - PI2_B))
ROUND = 1.5 * 2**23
TURN = float(np.nextafter(np.float32(TWO_PI), np.float32(0)))
PI_IN = float(np.nextafter(np.float32(np.pi), np.float32(0)))

LN1_W, LN1_B, PHZ_RE, PHZ_IM, LC_RE, LC_IM, SC_LIN, LN2_W, LN2_B, B2, LNL_W, LNL_B = range(12)
N_VEC = 12
AG = EXPERTS * RANK + EXPERTS
WF_BASE, WF_AG = 0, KC * VOC
WF_OUT = WF_AG + KC * AG
WF_B = WF_OUT + VOC
N_WF = WF_B + VOC
GROUPS = BATCH // 2
UNIT = 2 * SEQ
WF_PIECE = N_WF // ((DEPTH - 1) * GROUPS)
assert WF_PIECE * (DEPTH - 1) * GROUPS == N_WF

RING = 2


def made(n, ring=RING):
    return n + (1 + ring)


def free(n):
    return n + 1


def build(nc, log_dt, tok_a, tok_c, txt, win_t, bin_, vecs, b1, w1_t, w2_t, experts, row_bias, out):
    with ExitStack() as whole:
        def sb(ctx, name, shape, dt=F32):
            return ctx.enter_context(nc.sbuf_tensor(name, shape, dt))

        def psum(ctx, name, shape, dt=F32):
            return ctx.enter_context(nc.psum_tensor(name, shape, dt))

        def sem(ctx, name):
            return ctx.enter_context(nc.semaphore(name))

        tok_rows = nc.dram_tensor("tok_rows", (TOK, BATCH, VOC), F32, kind="Internal").ap()

        hT = sb(whole, "hT", [P, BATCH, SEQ])
        ident = sb(whole, "ident", [P, P])
        center = sb(whole, "center", [P, P])
        minus_half = sb(whole, "minus_half", [P, 4])
        eps = sb(whole, "eps", [P, 1])
        vec = sb(whole, "vec", [P, DEPTH, N_VEC])
        b1_sb = sb(whole, "b1_sb", [P, DEPTH, FC])
        w1 = sb(whole, "w1", [P, DFF])
        w2 = sb(whole, "w2", [P, FC, DIM])
        rot = sb(whole, "rot", [P, 2, DEPTH, SEQ])
        rot_scaled = sb(whole, "rot_scaled", [P, 2, DEPTH, SEQ])
        rate = sb(whole, "rate", [P, DEPTH])
        state0 = sb(whole, "state0", [P, 2, DEPTH])
        tokens_and_projection(nc, sb, psum, sem, log_dt, tok_a, tok_c, txt, win_t, bin_, vecs, b1, w1_t, w2_t,
                              tok_rows, hT, ident, center, minus_half, eps, vec, b1_sb, w1, w2,
                              rot, rot_scaled, rate, state0)
        with ExitStack() as late:
            wf = sb(late, "wf", [P, 2, N_WF], F32R)
            mixer(nc, sb, psum, sem, w1_t, w2_t, experts, hT, ident, center, minus_half, vec, b1_sb, w1, w2,
                  rot, rot_scaled, rate, state0, wf)
            experts_stage(nc, sb, psum, sem, txt, row_bias, tok_rows, hT, ident, minus_half, vec, wf, out)


def tokens_and_projection(nc, sb, psum, sem, log_dt, tok_a, tok_c, txt, win_t, bin_, vecs, b1, w1_t, w2_t,
                          tok_rows, hT, ident, center, minus_half, eps, vec, b1_sb, w1, w2,
                          rot, rot_scaled, rate, state0):
    with ExitStack() as ctx:
        ldt = sb(ctx, "ldt", [P, TOK])
        par = sb(ctx, "par", [P, 4, TOK])
        c_re = sb(ctx, "c_re", [P, TOK, BATCH])
        c_im = sb(ctx, "c_im", [P, TOK, BATCH])
        small = sb(ctx, "small", [P, 24, TOK])
        half = sb(ctx, "half", [P, DEPTH])
        ph = sb(ctx, "ph", [P, 5, DEPTH])
        half_pi = sb(ctx, "half_pi", [P, 1])
        alpha = sb(ctx, "alpha", [P, TOK])
        beta = sb(ctx, "beta", [P, TOK])
        powers = sb(ctx, "powers", [P, NJ])
        turns = sb(ctx, "turns", [P, H_CHUNK, NJ])
        whole_turns = sb(ctx, "whole_turns", [P, H_CHUNK, NJ])
        mag = sb(ctx, "decay", [P, H_CHUNK, NJ])
        sin = sb(ctx, "sin", [P, H_CHUNK, NJ])
        cos = sb(ctx, "cos", [P, H_CHUNK, NJ])
        w_re = sb(ctx, "w_re", [P, H_CHUNK, NA + NB1])
        w_im = sb(ctx, "w_im", [P, H_CHUNK, NA + NB1])
        n1 = sb(ctx, "n1", [P, H_CHUNK, NB0])
        n2 = sb(ctx, "n2", [P, H_CHUNK, NB0])
        pt = sb(ctx, "pt", [P, 4, H_CHUNK, NA])
        p1 = sb(ctx, "p1", [P, H_CHUNK, NA])
        p2 = sb(ctx, "p2", [P, H_CHUNK, NA])
        x1 = sb(ctx, "x1", [P, RING, H_BLOCK, BATCH, NA])
        x2 = sb(ctx, "x2", [P, RING, H_BLOCK, BATCH, NA])
        y1 = sb(ctx, "y1", [P, RING, H_BLOCK, NB1, NB0])
        y2 = sb(ctx, "y2", [P, RING, H_BLOCK, NB1, NB0])
        vv = sb(ctx, "vv", [P, RING, H_BLOCK, NB1 * NB0])
        rows_out = sb(ctx, "rows_out", [P, RING, H_BLOCK, P])
        wts = sb(ctx, "win_sb", [P, KC, DIM])
        bin_sb = sb(ctx, "bin_sb", [P, 1])
        raw = sb(ctx, "raw", [P, RING, 2, VOC])
        stats = sb(ctx, "stats", [P, RING, 2, 2, 6])
        mv = sb(ctx, "mv", [P, RING, 2, 2])
        var_eps = sb(ctx, "var_eps", [P, RING, 2])
        rstd = sb(ctx, "rstd", [P, RING, 2])
        xhat = sb(ctx, "xhat", [P, RING, 2, VOC])
        xT = sb(ctx, "xT", [P, RING, KC, 2 * P])

        k_ps = [psum(ctx, f"k_ps{i}", [P, 4, P]) for i in range(2)]
        t_ps = [psum(ctx, f"t_ps{i}", [P, 4, P]) for i in range(4)]
        w_ps = [psum(ctx, f"w_ps{i}", [P, 2, P]) for i in range(2)]

        vec_in = sem(ctx, "vec_in")
        ffn_in = sem(ctx, "ffn_in")
        pool_small = sem(ctx, "pool_small")
        par_in = sem(ctx, "par_in")
        c_in = sem(ctx, "c_in")
        win_in = sem(ctx, "win_in")
        consts = sem(ctx, "consts")
        act_small = sem(ctx, "act_small")
        dve_small = sem(ctx, "dve_small")
        decay_made = sem(ctx, "decay_made")
        mag_made = sem(ctx, "mag_made")
        chunk_steps = sem(ctx, "chunk_steps")
        sincos_made = sem(ctx, "sincos_made")
        coef_made = sem(ctx, "coef_made")
        x1_made = sem(ctx, "x1_made")
        x2_made = sem(ctx, "x2_made")
        y1_made = sem(ctx, "y1_made")
        y2_made = sem(ctx, "y2_made")
        vv_made = sem(ctx, "vv_made")
        k_done = sem(ctx, "k_done")
        k_moved = sem(ctx, "k_moved")
        rows_stored = [sem(ctx, f"rows_stored{i}") for i in range(RING)]
        raw_in = [sem(ctx, f"raw_in{i}") for i in range(RING)]
        stats_made = sem(ctx, "stats_made")
        waited = sem(ctx, "waited")
        mv_made = sem(ctx, "mv_made")
        ve_made = sem(ctx, "ve_made")
        rstd_made = sem(ctx, "rstd_made")
        xhat_made = sem(ctx, "xhat_made")
        xT_done = sem(ctx, "xT_done")
        xT_moved = sem(ctx, "xT_moved")
        win_done = sem(ctx, "win_done")
        win_moved = sem(ctx, "win_moved")
        block = ctx.enter_context(nc.Block())

        N_BLOCK = N_CHUNK * BLOCKS
        CONSTS = 9
        CHUNK_STEPS = 15

        @block.sync
        def _(sp):
            sp.dma_start(ldt[:], log_dt.to_broadcast([P, TOK])).then_inc(par_in, 16)
            for slot in range(2):
                sp.dma_start(par[slot * STATES:(slot + 1) * STATES], tok_a).then_inc(par_in, 16)
            for part, dst in enumerate((c_re, c_im)):
                for slot in range(2):
                    sp.dma_start(dst[slot * STATES:(slot + 1) * STATES], tok_c[part]).then_inc(c_in, 16)
            sp.dma_start(vec[:], vecs).then_inc(vec_in, 16)
            sp.dma_start(b1_sb[:], b1).then_inc(ffn_in, 16)
            sp.dma_start(w1[:], w1_t[0]).then_inc(ffn_in, 16)
            sp.dma_start(w2[:], w2_t[0]).then_inc(ffn_in, 16)
            sp.dma_start(wts[:], win_t).then_inc(win_in, 16)
            sp.dma_start(bin_sb[:], bin_).then_inc(win_in, 16)
            sp.wait_ge(ffn_in, 48)
            for first, src in ((0, txt.rearrange("c s v -> s c v")), (N_PAIR // 2, tok_rows)):
                if first:
                    for r in range(RING):
                        sp.wait_ge(rows_stored[r], 16 * (N_BLOCK // RING + 1))
                with sp.Fori(0, N_PAIR // 4) as i:
                    for p in range(RING):
                        sp.wait_ge(xhat_made, 2 * (2 * i + (first + p)) + 2)
                        sp.dma_start(raw[:, p], src[:, bass.ds(4 * i + 2 * p, 2), :]).then_inc(raw_in[p], 16)

        def mixer_tables(pool):
            count = [0]

            def step(ins):
                count[0] += 1
                ins.then_inc(pool_small, 1)
                pool.wait_ge(pool_small, count[0])

            def mul(o, a, b):
                step(pool.tensor_tensor(o, a, b, ALU.mult))

            rt = y2[:].rearrange("p r h a b -> p (r h a b)").rearrange("p (n l t) -> p n l t", n=4, l=DEPTH)
            v = lambda k: vec[:, :, k]
            t = lambda k: ph[:, k]
            pool.wait_ge(vec_in, 16)
            mul(t(0), v(PHZ_RE), v(PHZ_RE))
            mul(t(1), v(PHZ_IM), v(PHZ_IM))
            step(pool.tensor_tensor(t(0), t(0), t(1), ALU.add))
            step(pool.tensor_tensor(t(2), t(0), half[:], ALU.pow))
            step(pool.tensor_scalar(t(1), t(0), 1e-37, None, ALU.max))
            step(pool.tensor_tensor(t(1), t(1), minus_half[:], ALU.pow))
            step(pool.tensor_scalar(t(3), t(2), 0.0, None, ALU.is_equal))
            mul(t(4), v(PHZ_RE), t(1))
            step(pool.tensor_tensor(rot[:, 0, :, 1], t(4), t(3), ALU.add))
            mul(rot[:, 1, :, 1], v(PHZ_IM), t(1))
            step(pool.memset(rot[:, 0, :, 0], 1.0))
            step(pool.memset(rot[:, 1, :, 0], 0.0))
            m = 1
            while m < SEQ:
                k = min(m, SEQ - 1 - m)
                here = lambda part: rot[:, part, :, 1:1 + k]
                turn = lambda part: rot[:, part, :, m:m + 1].to_broadcast([P, DEPTH, k])
                if k:
                    for n, (a, b) in enumerate(((0, 0), (1, 1), (0, 1), (1, 0))):
                        mul(rt[:, n, :, 0:k], here(a), turn(b))
                    step(pool.tensor_tensor(rot[:, 0, :, m + 1:m + 1 + k], rt[:, 0, :, 0:k], rt[:, 1, :, 0:k], ALU.subtract))
                    step(pool.tensor_tensor(rot[:, 1, :, m + 1:m + 1 + k], rt[:, 2, :, 0:k], rt[:, 3, :, 0:k], ALU.add))
                m *= 2
            for part in range(2):
                mul(rot_scaled[:, part], rot[:, part], v(SC_LIN).unsqueeze(2).to_broadcast([P, DEPTH, SEQ]))
            c, s_ = rot[:, 0, :, 1], rot[:, 1, :, 1]
            mul(t(0), c, v(LC_RE))
            mul(t(1), s_, v(LC_IM))
            step(pool.tensor_tensor(state0[:, 0], t(0), t(1), ALU.subtract))
            mul(t(0), s_, v(LC_RE))
            mul(t(1), c, v(LC_IM))
            step(pool.tensor_tensor(t(0), t(0), t(1), ALU.add))
            step(pool.tensor_scalar(state0[:, 1], t(0), -1.0, None, ALU.mult))

        @block.gpsimd
        def _(pool):
            pool.memset(half[:], 0.5).then_inc(consts, 1)
            pool.memset(ident[:], 0.0).then_inc(consts, 1)
            pool.memset(minus_half[:], -0.5).then_inc(consts, 1)
            pool.iota(powers[:, 0:NA], pattern=[[P, NA]], base=0, channel_multiplier=0,
                      allow_small_or_imprecise_dtypes=True).then_inc(consts, 1)
            pool.iota(powers[:, NA:NA + NB1], pattern=[[NB0, NB1]], base=0, channel_multiplier=0,
                      allow_small_or_imprecise_dtypes=True).then_inc(consts, 1)
            pool.iota(powers[:, NA + NB1:NJ], pattern=[[1, NB0]], base=0, channel_multiplier=0,
                      allow_small_or_imprecise_dtypes=True).then_inc(consts, 1)
            pool.memset(eps[:], EPS).then_inc(consts, 1)
            pool.memset(half_pi[:], 0.5 * np.pi).then_inc(consts, 1)
            pool.wait_ge(consts, 2)
            pool.affine_select(out=ident[:], in_=ident[:], compare_op=ALU.not_equal, fill=1.0, base=0,
                               pattern=[[-1, P]], channel_multiplier=1).then_inc(consts, 1)
            pool.sem_inc(x2_made, 1)
            pool.sem_inc(y2_made, 1)
            pool.wait_ge(consts, CONSTS)
            mixer_tables(pool)
            pool.wait_ge(dve_small, 2)
            pool.wait_ge(c_in, 64)
            with pool.Fori(0, N_CHUNK) as q:
                pool.wait_ge(coef_made, free(q))
                pool.tensor_tensor(
                    mag[:], small[:, 0, bass.ds(q * H_CHUNK, H_CHUNK)].unsqueeze(2).to_broadcast([P, H_CHUNK, NJ]),
                    powers[:].unsqueeze(1).to_broadcast([P, H_CHUNK, NJ]), ALU.mult).then_inc(decay_made, 1)
                pool.wait_ge(coef_made, made(q, 1))
                for b in range(BLOCKS):
                    n = q * BLOCKS + b
                    r = b % RING
                    hs = slice(b * H_BLOCK, (b + 1) * H_BLOCK)
                    pool.wait_ge(k_done, 2 * free(n))
                    pool.tensor_tensor(
                        x2[:, r], c_im[:, bass.ds(q * H_CHUNK + b * H_BLOCK, H_BLOCK)].unsqueeze(3).to_broadcast([P, H_BLOCK, BATCH, NA]),
                        p2[:, hs].unsqueeze(2).to_broadcast([P, H_BLOCK, BATCH, NA]), ALU.mult).then_inc(x2_made, 1)
                    pool.wait_ge(vv_made, free(n))
                    pool.tensor_tensor(
                        y2[:, r], w_im[:, hs, NA:].unsqueeze(3).to_broadcast([P, H_BLOCK, NB1, NB0]),
                        n2[:, hs].unsqueeze(2).to_broadcast([P, H_BLOCK, NB1, NB0]), ALU.mult).then_inc(y2_made, 1)
            with pool.Fori(0, N_PAIR // RING) as i:
                for p in range(RING):
                    for j in range(2):
                        t = 2 * (RING * i + p) + j
                        pool.wait_ge(mv_made, t + 1)
                        pool.wait_ge(xhat_made, t + 1)
                        pool.tensor_tensor(var_eps[:, p, j:j + 1], mv[:, p, j, 1:2], eps[:], ALU.add).then_inc(ve_made, 1)
                        pool.wait_ge(ve_made, t + 1)
                        pool.tensor_tensor(rstd[:, p, j:j + 1], var_eps[:, p, j:j + 1], minus_half[:, 0:1],
                                           ALU.pow).then_inc(rstd_made, 1)

        @block.vector
        def _(dve):
            count = [0]

            def step(ins):
                count[0] += 1
                ins.then_inc(dve_small, 1)
                dve.wait_ge(dve_small, count[0])

            S = lambda k: small[:, k]
            X, THETA, K, R, RHO, DT, EAR, T, OMT, EM1, E, S2, ER, EI, NR, NI, A2, Q, GR, GI, TA, TB, AR = range(23)
            dve.wait_ge(consts, CONSTS)
            step(dve.tensor_scalar(center[:], ident[:], -1.0 / DIM, None, ALU.add))
            dve.wait_ge(act_small, 2)
            step(dve.scalar_tensor_tensor(S(X), S(EAR), -1.0, S(DT), ALU.mult, ALU.mult))
            step(dve.tensor_tensor(S(THETA), par[:, 1], S(DT), ALU.mult))
            step(dve.tensor_scalar(S(K), S(THETA), INV_2PI, ROUND, ALU.mult, ALU.add))
            step(dve.tensor_scalar(S(K), S(K), ROUND, None, ALU.subtract))
            step(dve.scalar_tensor_tensor(S(R), S(K), -PI2_A, S(THETA), ALU.mult, ALU.add))
            step(dve.scalar_tensor_tensor(S(R), S(K), -PI2_B, S(R), ALU.mult, ALU.add))
            step(dve.scalar_tensor_tensor(S(R), S(K), -PI2_C, S(R), ALU.mult, ALU.add))
            step(dve.tensor_scalar(S(RHO), S(R), INV_2PI, None, ALU.mult))
            step(dve.tensor_scalar(S(R), S(R), PI_IN, -PI_IN, ALU.min, ALU.max))
            dve.wait_ge(act_small, 5)
            step(dve.tensor_scalar(S(OMT), S(T), -1.0, 1.0, ALU.mult, ALU.add))
            step(dve.reciprocal(S(Q), S(OMT)))
            step(dve.scalar_tensor_tensor(S(EM1), S(T), 2.0, S(Q), ALU.mult, ALU.mult))
            step(dve.tensor_scalar(S(E), S(EM1), 1.0, None, ALU.add))
            step(dve.tensor_tensor(S(TA), S(S2), S(S2), ALU.mult))
            step(dve.tensor_tensor(S(TA), S(TA), S(E), ALU.mult))
            step(dve.scalar_tensor_tensor(S(ER), S(TA), -2.0, S(EM1), ALU.mult, ALU.add))
            step(dve.tensor_tensor(S(EI), S(EI), S(E), ALU.mult))
            step(dve.tensor_scalar(S(AR), S(EAR), -1.0, None, ALU.mult))

            def complex_times(re, im, a_re, a_im, b_re, b_im, conj):
                one, two = (ALU.add, ALU.subtract) if conj else (ALU.subtract, ALU.add)
                step(dve.tensor_tensor(S(TA), a_re, b_re, ALU.mult))
                step(dve.tensor_tensor(S(TB), a_im, b_im, ALU.mult))
                step(dve.tensor_tensor(re, S(TA), S(TB), one))
                step(dve.tensor_tensor(S(TA), a_im, b_re, ALU.mult))
                step(dve.tensor_tensor(S(TB), a_re, b_im, ALU.mult))
                step(dve.tensor_tensor(im, S(TA), S(TB), two))

            complex_times(S(NR), S(NI), S(ER), S(EI), S(AR), par[:, 1], True)
            complex_times(S(GR), S(GI), S(NR), S(NI), par[:, 2], par[:, 3], False)
            step(dve.tensor_tensor(S(TA), S(AR), S(AR), ALU.mult))
            step(dve.tensor_tensor(S(TB), par[:, 1], par[:, 1], ALU.mult))
            step(dve.tensor_tensor(S(A2), S(TA), S(TB), ALU.add))
            step(dve.reciprocal(S(Q), S(A2)))
            step(dve.tensor_tensor(S(GR), S(GR), S(Q), ALU.mult))
            step(dve.tensor_tensor(S(GI), S(GI), S(Q), ALU.mult))
            for slot, (dst, src, f) in enumerate(((alpha, GR, 2.0), (alpha, GI, -2.0), (beta, GI, -2.0), (beta, GR, -2.0))):
                ps = slice(slot % 2 * STATES, (slot % 2 + 1) * STATES)
                step(dve.tensor_scalar(dst[ps], small[ps, src], f, None, ALU.mult))
            dve.sem_inc(vv_made, RING)
            dve.sem_inc(coef_made, 1)
            dve.sem_inc(xhat_made, 2 * RING)

            with dve.Fori(0, N_CHUNK) as q:
                hq = bass.ds(q * H_CHUNK, H_CHUNK)
                dve.wait_ge(sincos_made, 2 * free(q))
                dve.tensor_tensor(turns[:], small[:, RHO, hq].unsqueeze(2).to_broadcast([P, H_CHUNK, NJ]),
                                  powers[:].unsqueeze(1).to_broadcast([P, H_CHUNK, NJ]), ALU.mult).then_inc(chunk_steps, 1)
                base = q * CHUNK_STEPS
                dve.wait_ge(chunk_steps, base + 1)
                dve.tensor_scalar(whole_turns[:], turns[:], ROUND, ROUND, ALU.add, ALU.subtract).then_inc(chunk_steps, 1)
                dve.wait_ge(chunk_steps, base + 2)
                dve.tensor_tensor(turns[:], turns[:], whole_turns[:], ALU.subtract).then_inc(chunk_steps, 1)
                dve.wait_ge(chunk_steps, base + 3)
                dve.scalar_tensor_tensor(whole_turns[:], turns[:], -1.0, turns[:], ALU.mult, ALU.max).then_inc(chunk_steps, 1)
                dve.wait_ge(mag_made, made(q, 1))
                dve.wait_ge(sincos_made, 2 * made(q, 1))
                dve.wait_ge(x2_made, free(q * BLOCKS))
                dve.wait_ge(y2_made, free(q * BLOCKS))
                ab = slice(0, NA + NB1)
                b0 = slice(NA + NB1, NJ)
                re, im = slice(0, STATES), slice(STATES, P)
                dve.tensor_tensor(w_re[:], mag[:, :, ab], cos[:, :, ab], ALU.mult).then_inc(chunk_steps, 1)
                dve.tensor_tensor(w_im[:], mag[:, :, ab], sin[:, :, ab], ALU.mult).then_inc(chunk_steps, 1)
                dve.tensor_tensor(n1[re], mag[re, :, b0], cos[re, :, b0], ALU.mult).then_inc(chunk_steps, 1)
                dve.tensor_tensor(n1[im], mag[im, :, b0], sin[im, :, b0], ALU.mult).then_inc(chunk_steps, 1)
                dve.scalar_tensor_tensor(n2[re], mag[re, :, b0], -1.0, sin[re, :, b0], ALU.mult, ALU.mult).then_inc(chunk_steps, 1)
                dve.tensor_tensor(n2[im], mag[im, :, b0], cos[im, :, b0], ALU.mult).then_inc(chunk_steps, 1)
                dve.wait_ge(chunk_steps, base + 6)
                al = alpha[:, hq].unsqueeze(2).to_broadcast([P, H_CHUNK, NA])
                be = beta[:, hq].unsqueeze(2).to_broadcast([P, H_CHUNK, NA])
                for k, (w, c) in enumerate(((w_re, al), (w_im, be), (w_re, be), (w_im, al))):
                    dve.tensor_tensor(pt[:, k], w[:, :, 0:NA], c, ALU.mult).then_inc(chunk_steps, 1)
                dve.wait_ge(chunk_steps, base + 14)
                dve.tensor_tensor(p1[:], pt[:, 0], pt[:, 1], ALU.add).then_inc(chunk_steps, 1)
                dve.tensor_tensor(p2[:], pt[:, 2], pt[:, 3], ALU.subtract).then_inc(coef_made, 1)
                dve.wait_ge(chunk_steps, base + 15)
                for b in range(BLOCKS):
                    n = q * BLOCKS + b
                    r = b % RING
                    hs = slice(b * H_BLOCK, (b + 1) * H_BLOCK)
                    dve.wait_ge(k_done, 2 * free(n))
                    dve.tensor_tensor(
                        y1[:, r], w_re[:, hs, NA:].unsqueeze(3).to_broadcast([P, H_BLOCK, NB1, NB0]),
                        n1[:, hs].unsqueeze(2).to_broadcast([P, H_BLOCK, NB1, NB0]), ALU.mult).then_inc(y1_made, 1)
                    dve.tensor_tensor(
                        x1[:, r], c_re[:, bass.ds(q * H_CHUNK + b * H_BLOCK, H_BLOCK)].unsqueeze(3).to_broadcast([P, H_BLOCK, BATCH, NA]),
                        p1[:, hs].unsqueeze(2).to_broadcast([P, H_BLOCK, BATCH, NA]), ALU.mult).then_inc(x1_made, 1)
                    dve.wait_ge(y1_made, n + 1)
                    dve.wait_ge(y2_made, made(n, 1))
                    dve.tensor_tensor(vv[:, r], y1[:, r].rearrange("p h a b -> p h (a b)"),
                                      y2[:, r].rearrange("p h a b -> p h (a b)"), ALU.add).then_inc(vv_made, 1)

            with dve.Fori(0, N_PAIR // RING) as i:
                for p in range(RING):
                    m = RING * i + p
                    dve.wait_ge(raw_in[p], 16 * i + 16)
                    for j in range(2):
                        for k in range(2):
                            dve.bn_stats(stats[:, p, j, k], raw[:, p, j, k * 512:(k + 1) * 512]).then_inc(stats_made, 1)
                        dve.wait_ge(stats_made, 4 * m + 2 * j + 2)
                        dve.sem_inc(waited, 1)
                        dve.bn_aggr(mv[:, p, j], stats[:, p, j].rearrange("p a b -> p (a b)")).then_inc(mv_made, 1)
                    for j in range(2):
                        dve.wait_ge(rstd_made, 2 * m + j + 1)
                        dve.wait_ge(xT_done, 4 * m + 2 * j + 2)
                        dve.tensor_scalar(xhat[:, p, j], raw[:, p, j], mv[:, p, j, 0:1], rstd[:, p, j:j + 1],
                                          ALU.subtract, ALU.mult).then_inc(xhat_made, 1)

        @block.scalar
        def _(act):
            X, THETA, K, R, RHO, DT, EAR, T, OMT, EM1, E, S2, ER, EI = range(14)
            act.sem_inc(mag_made, 1)
            act.sem_inc(sincos_made, 2)
            for r in range(RING):
                act.sem_inc(rows_stored[r], 16)
            act.sem_inc(k_moved, RING)
            act.sem_inc(xT_moved, 4)
            act.sem_inc(win_moved, RING)
            act.wait_ge(consts, CONSTS)
            act.wait_ge(par_in, 48)
            act.activation(small[:, DT], ldt[:], ACT.Exp).then_inc(act_small, 1)
            act.activation(small[:, EAR], par[:, 0], ACT.Exp).then_inc(act_small, 1)
            act.wait_ge(dve_small, 10)
            act.activation(small[:, T], small[:, X], ACT.Tanh, scale=0.5).then_inc(act_small, 1)
            act.activation(small[:, EI], small[:, R], ACT.Sin).then_inc(act_small, 1)
            act.activation(small[:, S2], small[:, R], ACT.Sin, scale=0.5).then_inc(act_small, 1)
            act.wait_ge(pool_small, 4)
            act.activation(rate[:], ph[:, 2], ACT.Tanh).then_inc(act_small, 1)
            with act.Fori(0, N_CHUNK) as q:
                act.wait_ge(decay_made, q + 1)
                act.wait_ge(coef_made, free(q))
                act.activation(mag[:], mag[:], ACT.Exp).then_inc(mag_made, 1)
                act.wait_ge(chunk_steps, q * CHUNK_STEPS + 4)
                act.activation(sin[:], turns[:], ACT.Sin, scale=TURN).then_inc(sincos_made, 1)
                act.activation(cos[:], whole_turns[:], ACT.Sin, scale=-TURN, bias=half_pi[:]).then_inc(sincos_made, 1)
                for b in range(BLOCKS):
                    n = q * BLOCKS + b
                    r = b % RING
                    act.wait_ge(rows_stored[r], q * (8 * BLOCKS) + 8 * (b - r + RING))
                    for k in range(2):
                        act.wait_ge(k_done, 2 * n + (k + 1 + 2 * RING))
                        act.activation(rows_out[:, r, 4 * k:4 * k + 4], k_ps[k][:], ACT.Copy).then_inc(k_moved, 1)
                    act.wait_ge(k_moved, 2 * n + (2 + RING))
                    act.dma_start(tok_rows[bass.ds(q * H_CHUNK + b * H_BLOCK, H_BLOCK)].rearrange("h c (a l) -> (c a) h l", l=P),
                                  rows_out[:, r]).then_inc(rows_stored[r], 16)

            def move_transposed(m, p):
                for j in range(2):
                    for k in range(2):
                        n = 2 * j + k
                        act.wait_ge(xT_done, 4 * m + (n + 1 + 8))
                        act.wait_ge(win_done, free(m))
                        act.activation(xT[:, p, 4 * k:4 * k + 4, j * P:(j + 1) * P], t_ps[n][:], ACT.Copy).then_inc(xT_moved, 1)

            def move_projected(m, p, sample, half):
                act.wait_ge(win_done, made(m))
                act.activation(hT[:, bass.ds(sample, 2), half * P:(half + 1) * P], w_ps[p][:], ACT.Identity,
                               bias=bin_sb[:]).then_inc(win_moved, 1)

            act.wait_ge(win_in, 32)
            move_transposed(0, 0)
            with act.Fori(0, N_PAIR // 4) as i:
                for p in range(RING):
                    move_transposed(2 * i + (p + 1), 1 - p)
                    move_projected(2 * i + p, p, 4 * i + 2 * p, 1)
            with act.Fori(0, N_PAIR // 4 - 1) as i:
                for p in range(RING):
                    move_transposed(2 * i + (p + 1 + N_PAIR // 2), 1 - p)
                    move_projected(2 * i + (p + N_PAIR // 2), p, 4 * i + 2 * p, 0)
            move_transposed(N_PAIR - 1, 1)
            move_projected(N_PAIR - 2, 0, BATCH - 4, 0)
            move_projected(N_PAIR - 1, 1, BATCH - 2, 0)

        @block.tensor
        def _(pe):
            pe.sem_inc(k_done, 2 * RING)
            pe.sem_inc(xT_done, 4 * RING)
            pe.sem_inc(win_done, RING)
            with pe.Fori(0, N_CHUNK) as q:
                for b in range(BLOCKS):
                    n = q * BLOCKS + b
                    r = b % RING
                    pe.wait_ge(x1_made, n + 1)
                    pe.wait_ge(x2_made, made(n, 1))
                    pe.wait_ge(vv_made, made(n))
                    for k in range(2):
                        pe.wait_ge(k_moved, 2 * n + k + 1)
                        for g in range(4):
                            h = 4 * k + g
                            for x in (x1, x2):
                                mm = pe.matmul(k_ps[k][:, g], x[:, r, h].rearrange("p c a -> p (c a)"), vv[:, r, h],
                                               start=(x is x1), stop=(x is x2))
                        mm.then_inc(k_done, 1)

            def transpose(m, p):
                for j in range(2):
                    pe.wait_ge(xhat_made, 2 * m + (j + 1 + 2 * RING))
                    for k in range(2):
                        pe.wait_ge(xT_moved, 4 * m + (2 * j + k + 1))
                        for c in range(4):
                            mm = pe.transpose(t_ps[2 * j + k][:, c], xhat[:, p, j, (4 * k + c) * P:(4 * k + c + 1) * P], ident[:])
                        mm.then_inc(xT_done, 1)

            def project(m, p):
                pe.wait_ge(xT_moved, 4 * m + 8)
                pe.wait_ge(win_moved, free(m))
                for c in range(KC):
                    mm = pe.matmul(w_ps[p][:].rearrange("p a b -> p (a b)"), wts[:, c], xT[:, p, c], start=(c == 0), stop=(c == KC - 1))
                mm.then_inc(win_done, 1)

            pe.wait_ge(win_in, 32)
            transpose(0, 0)
            with pe.Fori(0, N_PAIR // RING - 1) as i:
                for p in range(RING):
                    transpose(RING * i + (p + 1), 1 - p)
                    project(RING * i + p, p)
            transpose(N_PAIR - 1, 1)
            project(N_PAIR - 2, 0)
            project(N_PAIR - 1, 1)


def mixer(nc, sb, psum, sem, w1_t, w2_t, experts, hT, ident, center, minus_half, vec, b1_sb, w1, w2,
          rot, rot_scaled, rate, state0, wf):
    with ExitStack() as ctx:
        def buf(name, shape, dt=F32):
            return sb(ctx, name, shape, dt)

        sq = [buf(f"sq{n}", [P, 4, P]) for n in (1, 2)]
        ss = [buf(f"ss{n}", [P, 4]) for n in (1, 2)]
        ve = [buf(f"ve{n}", [P, 4]) for n in (1, 2)]
        rstd = [buf(f"l_rstd{n}", [P, 4]) for n in (1, 2)]
        xn = [buf(f"xn{n}", [P, 4, P]) for n in (1, 2)]
        y = buf("y", [P, 2, SEQ])
        u_re = buf("u_re", [P, 2, SEQ])
        u_im = buf("u_im", [P, 2, SEQ])
        z_re = buf("z_re", [P, 2, SEQ])
        z_im = buf("z_im", [P, 2, SEQ])
        c_re = buf("conv_re", [P, 2, SEQ])
        c_im = buf("conv_im", [P, 2, SEQ])
        h_mid = buf("h_mid", [P, 2, SEQ])
        y2 = buf("y2l", [P, UNIT])
        s = buf("s", [P, FC, UNIT])
        wf_raw = buf("wf_raw", [P, RING, WF_PIECE])

        c_ps = [psum(ctx, f"c_ps{n}", [P, 4, P]) for n in (1, 2)]
        t_ps = [psum(ctx, f"tl_ps{n}", [P, 4 * P]) for n in (1, 2)]
        m_ps = [psum(ctx, f"m_ps{n}", [P, UNIT]) for n in range(2)]
        o_ps = [psum(ctx, f"o_ps{n}", [P, UNIT]) for n in range(2)]

        centered = [sem(ctx, f"centered{n}") for n in (1, 2)]
        squared = [sem(ctx, f"squared{n}") for n in (1, 2)]
        summed = [sem(ctx, f"summed{n}") for n in (1, 2)]
        ve_made = [sem(ctx, f"lve_made{n}") for n in (1, 2)]
        rstd_made = [sem(ctx, f"lrstd_made{n}") for n in (1, 2)]
        xn_made = [sem(ctx, f"xn_made{n}") for n in (1, 2)]
        turned = [sem(ctx, f"turned{n}") for n in (1, 2)]
        y_made = sem(ctx, "y_made")
        u_re_made = sem(ctx, "u_re_made")
        u_im_made = sem(ctx, "u_im_made")
        z_re_made = sem(ctx, "z_re_made")
        z_im_made = sem(ctx, "z_im_made")
        c_re_made = sem(ctx, "c_re_made")
        c_im_made = sem(ctx, "c_im_made")
        h_mid_made = sem(ctx, "h_mid_made")
        h1_made = sem(ctx, "h1_made")
        y2_made = sem(ctx, "y2l_made")
        m_done = sem(ctx, "m_done")
        s_made = sem(ctx, "s_made")
        o_done = sem(ctx, "o_done")
        res_made = sem(ctx, "res_made")
        waited = sem(ctx, "l_waited")
        w1_in = sem(ctx, "w1_in")
        w2_in = sem(ctx, "w2_in")
        piece_in = [sem(ctx, f"piece_in{r}") for r in range(RING)]
        hi_made = sem(ctx, "hi_made")
        lo_made = sem(ctx, "lo_made")
        block = ctx.enter_context(nc.Block())

        def slots(eng, slot):
            slot(-2, 0, -2, True, False, False)
            slot(-1, 0, -1, True, True, False)
            with eng.Fori(0, DEPTH - 1) as l:
                for g in range(GROUPS):
                    slot(GROUPS * l + g, l, g, True, True, True)
            for g in range(GROUPS):
                slot(GROUPS * (DEPTH - 1) + g, DEPTH - 1, g, g + 2 < GROUPS, g + 1 < GROUPS, True)

        def carry(eng):
            eng.sem_inc(waited, 1)

        def at(l, g, ahead):
            return l + (g + ahead) // GROUPS, (g + ahead) % GROUPS

        def of(l):
            return bass.ds(l, 1)

        def rows(g):
            return hT[:, 2 * g:2 * g + 2, :]

        @block.sync
        def _(sp):
            with sp.Fori(0, DEPTH - 1) as l:
                for g in range(GROUPS):
                    n = GROUPS * l + g
                    sp.wait_ge(lo_made, free(n))
                    sp.dma_start(wf_raw[:, g % RING], experts[:, bass.ds(n * WF_PIECE, WF_PIECE)]).then_inc(piece_in[g % RING], 16)
                sp.wait_ge(m_done, FC * GROUPS * l + (FC * GROUPS + FC))
                sp.dma_start(w1[:], w1_t[bass.ds(l + 1, 1)].rearrange("o p f -> (o p) f")).then_inc(w1_in, 16)
                sp.wait_ge(o_done, GROUPS * l + (GROUPS + 1))
                sp.dma_start(w2[:], w2_t[bass.ds(l + 1, 1)].rearrange("o p c f -> (o p) c f")).then_inc(w2_in, 16)

        @block.gpsimd
        def _(pool):
            for k in range(2):
                pool.sem_inc(rstd_made[k], 1)
            pool.sem_inc(u_im_made, 1)
            pool.sem_inc(c_im_made, 1)
            pool.sem_inc(lo_made, RING)

            def rstd_of(k, u):
                pool.wait_ge(summed[k], made(u, 1))
                carry(pool)
                pool.tensor_scalar(ve[k][:], ss[k][:], 1.0 / DIM, EPS, ALU.mult, ALU.add).then_inc(ve_made[k], 1)
                pool.wait_ge(ve_made[k], u + 1)
                pool.wait_ge(xn_made[k], free(u))
                pool.tensor_tensor(rstd[k][:], ve[k][:], minus_half[:], ALU.pow).then_inc(rstd_made[k], 1)

            def slot(i, l, g, a, b, m):
                if a:
                    rstd_of(0, i + 2)
                if b:
                    rstd_of(1, i + 1)
                if m and not isinstance(l, int):
                    pool.wait_ge(hi_made, i + 1)
                    carry(pool)
                    pool.tensor_tensor(wf[:, 1, bass.ds(i * WF_PIECE, WF_PIECE)], wf_raw[:, g % RING],
                                       wf[:, 0, bass.ds(i * WF_PIECE, WF_PIECE)].bitcast(F32), ALU.subtract).then_inc(lo_made, 1)
                if a:
                    u = i + 2
                    la, _ = at(l, g, 2)
                    pool.wait_ge(y_made, made(u, 1))
                    pool.wait_ge(z_im_made, 2 * free(u))
                    carry(pool)
                    pool.tensor_tensor(u_im[:], y[:], rot[:, 1, of(la)].to_broadcast([P, 2, SEQ]), ALU.mult).then_inc(u_im_made, 1)
                    pool.wait_ge(z_im_made, 2 * made(u, 1))
                    pool.wait_ge(h1_made, free(u))
                    carry(pool)
                    pool.tensor_tensor(c_im[:], z_im[:], rot_scaled[:, 1, of(la)].to_broadcast([P, 2, SEQ]), ALU.mult).then_inc(c_im_made, 1)

            slots(pool, slot)

        @block.vector
        def _(dve):
            for k in range(2):
                dve.sem_inc(summed[k], 1)
                dve.sem_inc(xn_made[k], 1)
            dve.sem_inc(u_re_made, 1)
            dve.sem_inc(z_im_made, 2)
            dve.sem_inc(h1_made, 1)
            dve.sem_inc(res_made, GROUPS)

            def sum_squares(k, u):
                dve.wait_ge(squared[k], made(u, 1))
                dve.wait_ge(rstd_made[k], free(u))
                dve.tensor_reduce(ss[k][:], sq[k][:], AX.X, ALU.add).then_inc(summed[k], 1)

            def normalize(k, u):
                dve.wait_ge(rstd_made[k], made(u, 1))
                dve.wait_ge(turned[k], free(u))
                dve.tensor_tensor(xn[k][:], c_ps[k][:], rstd[k][:].unsqueeze(2).to_broadcast([P, 4, P]), ALU.mult).then_inc(xn_made[k], 1)

            def scans(u, dst, src, part, la, done):
                for n in range(2):
                    dve.tensor_tensor_scan(dst[:, n], rate[:, of(la)].to_broadcast([P, SEQ]), src[:, n],
                                           state0[:, part, of(la)], ALU.mult, ALU.add).then_inc(done, 1)

            def slot(i, l, g, a, b, m):
                if a:
                    sum_squares(0, i + 2)
                if b:
                    sum_squares(1, i + 1)
                if a:
                    normalize(0, i + 2)
                if b:
                    normalize(1, i + 1)
                if a:
                    u = i + 2
                    la, ga = at(l, g, 2)
                    dve.wait_ge(y_made, made(u, 1))
                    dve.tensor_tensor(u_re[:], y[:], rot[:, 0, of(la)].to_broadcast([P, 2, SEQ]), ALU.mult).then_inc(u_re_made, 1)
                    dve.wait_ge(u_re_made, made(u, 1))
                    scans(u, z_re, u_re, 0, la, z_re_made)
                    dve.wait_ge(u_im_made, made(u, 1))
                    dve.wait_ge(c_im_made, free(u))
                    scans(u, z_im, u_im, 1, la, z_im_made)
                    dve.wait_ge(z_re_made, 2 * u + 2)
                    dve.tensor_tensor(c_re[:], z_re[:], rot_scaled[:, 0, of(la)].to_broadcast([P, 2, SEQ]), ALU.mult).then_inc(c_re_made, 1)
                    dve.wait_ge(c_re_made, u + 1)
                    dve.tensor_tensor(h_mid[:], rows(ga), c_re[:], ALU.add).then_inc(h_mid_made, 1)
                    dve.wait_ge(h_mid_made, u + 1)
                    dve.wait_ge(c_im_made, made(u, 1))
                    dve.tensor_tensor(rows(ga), h_mid[:], c_im[:], ALU.add).then_inc(h1_made, 1)
                if m:
                    dve.wait_ge(o_done, made(i, 1))
                    flat = rows(g).rearrange("p n t -> p (n t)")
                    dve.scalar_tensor_tensor(flat, o_ps[g % 2][:], vec[:, of(l), B2], flat, ALU.add, ALU.add).then_inc(res_made, 1)

            slots(dve, slot)

        @block.scalar
        def _(act):
            for k in range(2):
                act.sem_inc(squared[k], 1)
            act.sem_inc(y_made, 1)
            act.sem_inc(y2_made, 1)
            act.sem_inc(s_made, 2)

            def square(k, u):
                act.wait_ge(centered[k], made(u, 1))
                act.wait_ge(summed[k], free(u))
                act.activation(sq[k][:], c_ps[k][:], ACT.Square).then_inc(squared[k], 1)

            def hidden(i, l, j):
                act.wait_ge(m_done, FC * i + (j + 1 + FC))
                act.wait_ge(o_done, free(i))
                carry(act)
                act.activation(s[:, j], m_ps[j % 2][:], ACT.Silu, bias=b1_sb[:, of(l), j]).then_inc(s_made, 1)

            def slot(i, l, g, a, b, m):
                if a:
                    square(0, i + 2)
                if m:
                    hidden(i, l, 0)
                    hidden(i, l, 1)
                    if not isinstance(l, int):
                        act.wait_ge(piece_in[g % RING], 16 * (GROUPS // RING) * l + 16 * (g // RING + 1))
                        carry(act)
                        act.activation(wf[:, 0, bass.ds(i * WF_PIECE, WF_PIECE)], wf_raw[:, g % RING], ACT.Copy).then_inc(hi_made, 1)
                    hidden(i, l, 2)
                if b:
                    square(1, i + 1)
                if m:
                    hidden(i, l, 3)
                if a:
                    u = i + 2
                    la, _ = at(l, g, 2)
                    act.wait_ge(turned[0], made(u, 1))
                    act.wait_ge(u_re_made, free(u))
                    act.wait_ge(u_im_made, free(u))
                    carry(act)
                    act.activation(y[:].rearrange("p n t -> p (n t)"), t_ps[0][:], ACT.Silu, bias=vec[:, of(la), LN1_B],
                                   scale=vec[:, of(la), LN1_W]).then_inc(y_made, 1)
                if b:
                    u = i + 1
                    lb, _ = at(l, g, 1)
                    act.wait_ge(turned[1], made(u, 1))
                    act.wait_ge(m_done, FC * free(u))
                    carry(act)
                    act.activation(y2[:], t_ps[1][:], ACT.Identity, bias=vec[:, of(lb), LN2_B],
                                   scale=vec[:, of(lb), LN2_W]).then_inc(y2_made, 1)

            slots(act, slot)

        @block.tensor
        def _(pe):
            for k in range(2):
                pe.sem_inc(centered[k], 1)
                pe.sem_inc(turned[k], 1)
            pe.sem_inc(m_done, FC)
            pe.sem_inc(o_done, 1)
            pe.sem_inc(w1_in, 16)
            pe.sem_inc(w2_in, 16)

            def center_rows(k, u, g):
                if k == 0:
                    pe.wait_ge(res_made, free(u))
                else:
                    pe.wait_ge(h1_made, made(u, 1))
                pe.wait_ge(xn_made[k], free(u))
                flat = rows(g).rearrange("p n t -> p (n t)")
                for c in range(4):
                    mm = pe.matmul(c_ps[k][:, c], flat[:, c * P:(c + 1) * P], center[:], start=True, stop=True)
                mm.then_inc(centered[k], 1)

            def turn_rows(k, u):
                pe.wait_ge(xn_made[k], made(u, 1))
                pe.wait_ge((y_made, y2_made)[k], free(u))
                for c in range(4):
                    mm = pe.transpose(t_ps[k][:, c * P:(c + 1) * P], xn[k][:, c], ident[:])
                mm.then_inc(turned[k], 1)

            def first(i, j):
                if j == 0:
                    pe.wait_ge(y2_made, made(i, 1))
                pe.wait_ge(s_made, FC * i + (j + 1))
                pe.matmul(m_ps[j % 2][:], w1[:, j * P:(j + 1) * P], y2[:], start=True, stop=True).then_inc(m_done, 1)

            def second(i, g, k):
                if k == 0:
                    pe.wait_ge(res_made, i + (GROUPS - 1))
                pe.wait_ge(s_made, FC * i + (k + 3))
                mm = pe.matmul(o_ps[g % 2][:], w2[:, k], s[:, k], start=(k == 0), stop=(k == FC - 1))
                if k == FC - 1:
                    mm.then_inc(o_done, 1)

            def slot(i, l, g, a, b, m):
                if a:
                    center_rows(0, i + 2, at(l, g, 2)[1])
                if m:
                    if g == 0:
                        pe.wait_ge(w1_in, 16 * l + 16)
                    for j in range(3):
                        first(i, j)
                if b:
                    center_rows(1, i + 1, at(l, g, 1)[1])
                if m:
                    first(i, 3)
                    if g == 0:
                        pe.wait_ge(w2_in, 16 * l + 16)
                    second(i, g, 0)
                if a:
                    turn_rows(0, i + 2)
                if m:
                    second(i, g, 1)
                    second(i, g, 2)
                if b:
                    turn_rows(1, i + 1)
                if m:
                    second(i, g, 3)

            slots(pe, slot)


def experts_stage(nc, sb, psum, sem, txt, row_bias, tok_rows, hT, ident, minus_half, vec, wf, out):
    with ExitStack() as ctx:
        def buf(name, shape, dt=F32):
            return sb(ctx, name, shape, dt)

        ER = EXPERTS * RANK
        mixed = buf("mixed", [P, RING, P])
        row = buf("row", [P, RING, VOC])
        bias = buf("bias", [P, 2, VOC])
        f_stats = buf("f_stats", [P, 6])
        f_mv = buf("f_mv", [P, 2])
        f_ve = buf("f_ve", [P, 1])
        f_rstd = buf("f_rstd", [P, 1])
        zn = buf("zn", [P, P])
        z = buf("z", [P, P])
        z_hi = buf("z_hi", [P, P], F32R)
        z_lo = buf("z_lo", [P, P], F32R)
        row_b = buf("row_b", [P, VOC])
        h2 = buf("h2", [P, VOC])
        h2_b = buf("h2_b", [P, RING, VOC])
        r_stats = buf("r_stats", [P, 2, 6])
        r_mv = buf("r_mv", [P, 2])
        r_ve = buf("r_ve", [P, 1])
        r_rstd = buf("r_rstd", [P, 1])
        xhat = buf("x2hat", [P, VOC])
        x_hi = buf("x_hi", [P, RING, VOC], F32R)
        x_lo = buf("x_lo", [P, RING, VOC], F32R)
        top = buf("top", [P, EXPERTS])
        top_at = buf("top_at", [P, EXPERTS], U32)
        top_at_f = buf("top_at_f", [P, 2])
        gap = buf("gap", [P, 1])
        ratio = buf("ratio", [P, 1])
        total = buf("total", [P, 1])
        share = buf("share", [P, 2])
        picked = buf("picked", [P, 2, EXPERTS])
        weight = buf("weight", [P, EXPERTS])
        number = buf("number", [P, EXPERTS])
        ag = buf("ag", [P, AG])
        low = buf("low", [P, ER])
        low_hi = buf("low_hi", [P, P], F32R)
        low_lo = buf("low_lo", [P, P], F32R)
        result = buf("result", [P, RING, VOC])

        f_ps = psum(ctx, "f_ps", [P, 4, P])
        ag_bank = psum(ctx, "ag_bank", [P, 512])
        ag_ps = ag_bank[:, 0:2 * AG].rearrange("p (k n) -> p k n", k=2)
        y_ps = psum(ctx, "y_ps", [P, VOC])
        x_ps = psum(ctx, "x_ps", [P, VOC])
        r_ps = psum(ctx, "r_ps", [P, VOC])

        mixed_turned = sem(ctx, "x_mixed_turned")
        f_counted = sem(ctx, "x_f_counted")
        f_aggregated = sem(ctx, "x_f_aggregated")
        f_ve_made = sem(ctx, "x_f_ve_made")
        f_rstd_made = sem(ctx, "x_f_rstd_made")
        zn_made = sem(ctx, "x_zn_made")
        zn_turned = sem(ctx, "x_zn_turned")
        z_made = sem(ctx, "x_z_made")
        z_hi_made = sem(ctx, "x_z_hi_made")
        z_lo_made = sem(ctx, "x_z_lo_made")
        row_b_made = sem(ctx, "x_row_b_made")
        y_done = sem(ctx, "x_y_done")
        h2_made = sem(ctx, "x_h2_made")
        h2_b_made = sem(ctx, "x_h2_b_made")
        r_counted = sem(ctx, "x_r_counted")
        r_aggregated = sem(ctx, "x_r_aggregated")
        r_ve_made = sem(ctx, "x_r_ve_made")
        r_rstd_made = sem(ctx, "x_r_rstd_made")
        xhat_made = sem(ctx, "x_xhat_made")
        x_turned = sem(ctx, "x_x_turned")
        x_hi_made = sem(ctx, "x_x_hi_made")
        x_lo_made = sem(ctx, "x_x_lo_made")
        ag_done = sem(ctx, "x_ag_done")
        ag_base_done = sem(ctx, "x_ag_base_done")
        weight_made = sem(ctx, "x_weight_made")
        ag_half_made = sem(ctx, "x_ag_half_made")
        ag_added = sem(ctx, "x_ag_added")
        gate_steps = sem(ctx, "x_gate_steps")
        ratio_made = sem(ctx, "x_ratio_made")
        low_made = sem(ctx, "x_low_made")
        low_turned = sem(ctx, "x_low_turned")
        low_hi_made = sem(ctx, "x_low_hi_made")
        low_lo_made = sem(ctx, "x_low_lo_made")
        r_done = sem(ctx, "x_r_done")
        result_made = sem(ctx, "x_result_made")
        x_constants = sem(ctx, "x_x_constants")
        x_waited = sem(ctx, "x_x_waited")
        bias_in = sem(ctx, "x_bias_in")
        mixed_in = [sem(ctx, f"mixed_in{r}") for r in range(RING)]
        row_in = [sem(ctx, f"row_in{r}") for r in range(RING)]
        stored = [sem(ctx, f"stored{r}") for r in range(RING)]
        block = ctx.enter_context(nc.Block())
        TILES = 2 * BATCH
        GATE_STEPS = 10

        def slots(eng, slot):
            with eng.Fori(0, BATCH - 1) as c:
                for p in range(RING):
                    slot(2 * c + p, p, c, 2)
            slot(TILES - 2, 0, BATCH - 1, 1)
            slot(TILES - 1, 1, BATCH - 1, 0)

        def carry(eng):
            eng.sem_inc(x_waited, 1)

        @block.sync
        def _(sp):
            def load(t, p, c):
                sp.wait_ge(mixed_turned, free(t))
                sp.dma_start(mixed[:, p], hT[:, bass.ds(c, 1), p * P:(p + 1) * P].rearrange("d o t -> d (o t)")).then_inc(mixed_in[p], 16)
                sp.wait_ge(row_b_made, free(t))
                src = tok_rows[:, bass.ds(c, 1)] if p == 0 else txt[bass.ds(c, 1)].rearrange("o s v -> s o v")
                sp.dma_start(row[:, p], src.rearrange("s o v -> s (o v)")).then_inc(row_in[p], 16)

            def store(t, p, c):
                sp.wait_ge(result_made, made(t))
                sp.dma_start(out[bass.ds(c, 1), p * P:(p + 1) * P].rearrange("o s v -> (o s) v"), result[:, p]).then_inc(stored[p], 16)

            for k in range(2):
                sp.dma_start(bias[:, k], row_bias[k:k + 1].to_broadcast([P, VOC])).then_inc(bias_in, 16)
            for p in range(RING):
                load(p, p, 0)
            with sp.Fori(0, BATCH - 1) as c:
                for p in range(RING):
                    load(2 * c + (p + 2), p, c + 1)
                    store(2 * c + p, p, c)
            for p in range(RING):
                store(TILES - 2 + p, p, BATCH - 1)
            for p in range(RING):
                sp.wait_ge(stored[p], 16 * (BATCH + 1))

        @block.gpsimd
        def _(pool):
            pool.iota(number[:], pattern=[[1, EXPERTS]], base=0, channel_multiplier=0,
                      allow_small_or_imprecise_dtypes=True).then_inc(x_constants, 1)
            pool.sem_inc(row_b_made, RING)
            pool.sem_inc(h2_b_made, RING)
            pool.sem_inc(f_rstd_made, 1)
            pool.sem_inc(r_rstd_made, 1)
            pool.wait_ge(bias_in, 32)

            def rstd_of(t, mv, ve, rstd, aggregated, ve_made, rstd_made, used):
                pool.wait_ge(aggregated, t + 1)
                pool.wait_ge(used, free(t))
                carry(pool)
                pool.tensor_scalar(ve[:], mv[:, 1:2], EPS, None, ALU.add).then_inc(ve_made, 1)
                pool.wait_ge(ve_made, t + 1)
                pool.tensor_tensor(rstd[:], ve[:], minus_half[:, 0:1], ALU.pow).then_inc(rstd_made, 1)

            def mixed_part(t, p, c):
                pool.wait_ge(row_in[p], 16 * (c + 1))
                pool.wait_ge(h2_made, free(t))
                pool.tensor_tensor(row_b[:], row[:, p], bias[:, 0], ALU.add).then_inc(row_b_made, 1)
                rstd_of(t, f_mv, f_ve, f_rstd, f_aggregated, f_ve_made, f_rstd_made, zn_made)

            def row_part(t, p):
                rstd_of(t, r_mv, r_ve, r_rstd, r_aggregated, r_ve_made, r_rstd_made, xhat_made)
                pool.wait_ge(h2_made, made(t, 1))
                pool.wait_ge(result_made, free(t))
                pool.tensor_tensor(h2_b[:, p], h2[:], bias[:, 1], ALU.add).then_inc(h2_b_made, 1)

            def slot(t, p, c, after):
                if after > 0:
                    row_part(t + 1, 1 - p)
                if after > 1:
                    mixed_part(t + 2, p, c + 1)

            mixed_part(0, 0, 0)
            row_part(0, 0)
            mixed_part(1, 1, 0)
            slots(pool, slot)

        @block.vector
        def _(dve):
            for n in (zn_made, z_lo_made, h2_made, xhat_made, ag_added, low_made, low_lo_made):
                dve.sem_inc(n, 1)
            dve.sem_inc(x_lo_made, RING)
            dve.sem_inc(result_made, RING)
            dve.wait_ge(x_constants, 1)

            def gate_pick(t):
                g = t * GATE_STEPS
                dve.wait_ge(ag_done, made(t, 1))
                dve.wait_ge(low_made, free(t))
                dve.tensor_copy(ag[:], ag_ps[:, 1]).then_inc(ag_half_made, 1)
                dve.wait_ge(ag_half_made, t + 1)
                dve.tensor_tensor(ag[:], ag_ps[:, 0], ag[:], ALU.add).then_inc(ag_added, 1)
                dve.wait_ge(ag_added, made(t, 1))
                carry(dve)
                dve.max(top[:], ag[:, ER:AG]).then_inc(gate_steps, 1)
                dve.wait_ge(gate_steps, g + 1)
                dve.tensor_tensor(gap[:], top[:, 1:2], top[:, 0:1], ALU.subtract).then_inc(gate_steps, 1)
                dve.max_index(top_at[:], top[:], ag[:, ER:AG]).then_inc(gate_steps, 1)
                dve.wait_ge(gate_steps, g + 3)
                dve.tensor_copy(top_at_f[:], top_at[:, 0:2]).then_inc(gate_steps, 1)
                dve.wait_ge(gate_steps, g + 4)
                for k in range(2):
                    dve.tensor_scalar(picked[:, k], number[:], top_at_f[:, k:k + 1], None, ALU.is_equal).then_inc(gate_steps, 1)

            def gate_weigh(t):
                g = t * GATE_STEPS
                dve.wait_ge(ratio_made, t + 1)
                dve.tensor_scalar(total[:], ratio[:], 0.5, 0.5, ALU.mult, ALU.add).then_inc(gate_steps, 1)
                dve.wait_ge(gate_steps, g + 7)
                dve.reciprocal(share[:, 0:1], total[:]).then_inc(gate_steps, 1)
                dve.wait_ge(gate_steps, g + 8)
                dve.tensor_tensor(share[:, 1:2], share[:, 0:1], ratio[:], ALU.mult).then_inc(gate_steps, 1)
                dve.wait_ge(gate_steps, g + 9)
                dve.tensor_scalar(weight[:], picked[:, 0], share[:, 0:1], None, ALU.mult).then_inc(gate_steps, 1)

            def low_rank(t):
                g = t * GATE_STEPS
                dve.wait_ge(gate_steps, g + 10)
                dve.scalar_tensor_tensor(weight[:], picked[:, 1], share[:, 1:2], weight[:], ALU.mult, ALU.add).then_inc(weight_made, 1)
                dve.wait_ge(weight_made, t + 1)
                dve.wait_ge(low_turned, t + 1)
                dve.tensor_tensor(low[:].rearrange("p (e r) -> p e r", e=EXPERTS), ag[:, 0:ER].rearrange("p (e r) -> p e r", e=EXPERTS),
                                  weight[:].unsqueeze(2).to_broadcast([P, EXPERTS, RANK]), ALU.mult).then_inc(low_made, 1)

            def finish(t, p):
                dve.wait_ge(r_done, made(t, 1))
                dve.wait_ge(stored[p], 8 * t + (16 - 8 * p))
                dve.wait_ge(h2_b_made, made(t))
                dve.tensor_tensor(result[:, p], r_ps[:], h2_b[:, p], ALU.add).then_inc(result_made, 1)

            def mixed_stats(t):
                dve.wait_ge(mixed_turned, made(t))
                dve.bn_stats(f_stats[:], f_ps[:, 0]).then_inc(f_counted, 1)
                dve.wait_ge(f_counted, t + 1)
                dve.wait_ge(f_rstd_made, free(t))
                carry(dve)
                dve.bn_aggr(f_mv[:], f_stats[:]).then_inc(f_aggregated, 1)

            def mixed_normal(t):
                dve.wait_ge(f_rstd_made, made(t, 1))
                dve.wait_ge(zn_turned, free(t))
                dve.tensor_scalar(zn[:], f_ps[:, 0], f_mv[:, 0:1], f_rstd[:], ALU.subtract, ALU.mult).then_inc(zn_made, 1)

            def mixed_low(t):
                dve.wait_ge(z_hi_made, t + 1)
                dve.wait_ge(y_done, free(t))
                dve.tensor_tensor(z_lo[:], z[:], z_hi[:].bitcast(F32), ALU.subtract).then_inc(z_lo_made, 1)

            def residual(t):
                dve.wait_ge(y_done, made(t, 1))
                dve.wait_ge(row_b_made, made(t))
                dve.wait_ge(h2_b_made, t + RING)
                dve.tensor_tensor(h2[:], y_ps[:], row_b[:], ALU.add).then_inc(h2_made, 1)
                dve.wait_ge(h2_made, made(t, 1))
                for k in range(2):
                    dve.bn_stats(r_stats[:, k], h2[:, k * 512:(k + 1) * 512]).then_inc(r_counted, 1)
                dve.wait_ge(r_counted, 2 * t + 2)
                dve.wait_ge(r_rstd_made, free(t))
                carry(dve)
                dve.bn_aggr(r_mv[:], r_stats[:].rearrange("p a b -> p (a b)")).then_inc(r_aggregated, 1)

            def row_normal(t):
                dve.wait_ge(r_rstd_made, made(t, 1))
                dve.wait_ge(x_turned, free(t))
                dve.tensor_scalar(xhat[:], h2[:], r_mv[:, 0:1], r_rstd[:], ALU.subtract, ALU.mult).then_inc(xhat_made, 1)

            def row_low(t, p):
                dve.wait_ge(x_hi_made, made(t))
                dve.tensor_tensor(x_lo[:, p], x_ps[:], x_hi[:, p].bitcast(F32), ALU.subtract).then_inc(x_lo_made, 1)

            def low_low(t):
                dve.wait_ge(low_hi_made, t + 1)
                dve.tensor_tensor(low_lo[:], f_ps[:, 2], low_hi[:].bitcast(F32), ALU.subtract).then_inc(low_lo_made, 1)

            def slot(t, p, c, after):
                if after > 0:
                    mixed_normal(t + 1)
                gate_pick(t)
                if after > 0:
                    mixed_low(t + 1)
                gate_weigh(t)
                low_rank(t)
                if after > 0:
                    residual(t + 1)
                low_low(t)
                if after > 0:
                    row_normal(t + 1)
                    row_low(t + 1, 1 - p)
                if after > 1:
                    mixed_stats(t + 2)
                finish(t, p)

            mixed_stats(0)
            mixed_normal(0)
            mixed_low(0)
            residual(0)
            row_normal(0)
            row_low(0, 0)
            mixed_stats(1)
            slots(dve, slot)

        @block.scalar
        def _(act):
            act.sem_inc(z_made, 1)
            act.sem_inc(x_hi_made, RING)
            for p in range(RING):
                act.sem_inc(stored[p], 16)

            def ahead_z(t):
                act.wait_ge(zn_turned, made(t, 1))
                act.wait_ge(z_lo_made, free(t))
                act.activation(z[:], f_ps[:, 1], ACT.Identity, bias=vec[:, 0, LNL_B:LNL_B + 1],
                               scale=vec[:, 0, LNL_W:LNL_W + 1]).then_inc(z_made, 1)
                act.wait_ge(z_made, made(t, 1))
                act.wait_ge(y_done, free(t))
                act.activation(z_hi[:], z[:], ACT.Copy).then_inc(z_hi_made, 1)

            def ahead_x(t, p):
                act.wait_ge(x_turned, made(t, 1))
                act.wait_ge(ag_base_done, free(t))
                act.activation(x_hi[:, p], x_ps[:], ACT.Copy).then_inc(x_hi_made, 1)

            def slot(t, p, c, after):
                if after > 0:
                    ahead_z(t + 1)
                act.wait_ge(gate_steps, t * GATE_STEPS + 2)
                act.activation(ratio[:], gap[:], ACT.Exp).then_inc(ratio_made, 1)
                act.wait_ge(low_turned, made(t, 1))
                act.wait_ge(r_done, free(t))
                act.activation(low_hi[:], f_ps[:, 2], ACT.Copy).then_inc(low_hi_made, 1)
                if after > 0:
                    ahead_x(t + 1, 1 - p)

            ahead_z(0)
            ahead_x(0, 0)
            slots(act, slot)

        @block.tensor
        def _(pe):
            pe.sem_inc(mixed_turned, RING)
            for n in (zn_turned, y_done, x_turned, ag_done, low_turned, r_done):
                pe.sem_inc(n, 1)
            pe.sem_inc(ag_base_done, RING)

            def turn_mixed(t, p, c):
                pe.wait_ge(mixed_in[p], 16 * (c + 1))
                pe.wait_ge(zn_made, free(t))
                pe.wait_ge(z_made, free(t))
                pe.transpose(f_ps[:, 0], mixed[:, p], ident[:]).then_inc(mixed_turned, 1)

            def turn_zn(t):
                pe.wait_ge(zn_made, made(t, 1))
                pe.transpose(f_ps[:, 1], zn[:], ident[:]).then_inc(zn_turned, 1)

            def wide(dst, x_hi_c, x_lo_c, at, start, stop):
                for k, (x, lo) in enumerate(((x_hi_c, False), (x_hi_c, True), (x_lo_c, False))):
                    for n in range(VOC // 512):
                        w = wf[:, int(lo), at + n * 512:at + (n + 1) * 512]
                        mm = pe.matmul(dst[:, n * 512:(n + 1) * 512], x, w, start=(start and k == 0), stop=(stop and k == 2))
                return mm

            def output(t):
                pe.wait_ge(z_lo_made, made(t, 1))
                pe.wait_ge(h2_made, free(t))
                wide(y_ps, z_hi[:], z_lo[:], WF_OUT, True, True).then_inc(y_done, 1)

            def turn_rows(t):
                pe.wait_ge(xhat_made, made(t, 1))
                pe.wait_ge(x_lo_made, t + RING)
                for c in range(KC):
                    mm = pe.transpose(x_ps[:, c * P:(c + 1) * P], xhat[:, c * P:(c + 1) * P], ident[:])
                mm.then_inc(x_turned, 1)

            def low_and_gate(t, p):
                pe.wait_ge(x_lo_made, made(t))
                pe.wait_ge(ag_added, free(t))
                for c in range(KC):
                    cs = slice(c * P, (c + 1) * P)
                    w = wf[:, :, WF_AG + c * AG:WF_AG + (c + 1) * AG]
                    if c == 0:
                        pe.matmul(ag_ps, x_hi[:, p, cs], w, start=True, stop=False)
                    pe.matmul(ag_ps[:, 0], x_lo[:, p, cs], w[:, 0], start=False, stop=False)
                    if c > 0:
                        mm = pe.matmul(ag_ps, x_hi[:, p, cs], w, start=False, stop=c == KC - 1)
                mm.then_inc(ag_done, 1)

            def base(t, p, chunks):
                if chunks[0] == 0:
                    pe.wait_ge(result_made, t + RING)
                for c in chunks:
                    cs = slice(c * P, (c + 1) * P)
                    mm = wide(r_ps, x_hi[:, p, cs], x_lo[:, p, cs], WF_BASE + c * VOC, c == 0, False)
                    if c == KC - 1:
                        mm.then_inc(ag_base_done, 1)

            def turn_low(t, after):
                if after:
                    pe.wait_ge(z_made, made(t + 1, 1))
                pe.wait_ge(low_made, made(t, 1))
                pe.wait_ge(low_lo_made, free(t))
                pe.transpose(f_ps[:, 2], low[:], ident[:]).then_inc(low_turned, 1)

            def low_output(t):
                pe.wait_ge(low_lo_made, made(t, 1))
                wide(r_ps, low_hi[:], low_lo[:], WF_B, False, True).then_inc(r_done, 1)

            def slot(t, p, c, after):
                low_and_gate(t, p)
                if after > 0:
                    turn_zn(t + 1)
                base(t, p, [0, 1])
                if after > 0:
                    output(t + 1)
                base(t, p, [2])
                turn_low(t, after > 0)
                base(t, p, [3, 4, 5])
                if after > 0:
                    turn_rows(t + 1)
                base(t, p, [6, 7])
                if after > 1:
                    pe.wait_ge(low_lo_made, made(t, 1))
                    turn_mixed(t + 2, p, c + 1)
                low_output(t)

            turn_mixed(0, 0, 0)
            turn_zn(0)
            output(0)
            turn_rows(0)
            turn_mixed(1, 1, 0)
            slots(pe, slot)


def kernel(x, txt, L0_tok_log_dt, L0_tok_B, L0_tok_inv_A_real, L0_tok_A_imag, L0_attn_Win, L0_attn_bin,
           L0_attn_ln1_w, L0_attn_ln1_b, L0_attn_phz_re, L0_attn_phz_im, L0_attn_lc_re, L0_attn_lc_im,
           L0_attn_sc_lin, L0_attn_ln2_w, L0_attn_ln2_b, L0_attn_W1, L0_attn_b1, L0_attn_W2, L0_attn_b2,
           L0_attn_lnl_w, L0_attn_lnl_b, L0_attn_Wout, L0_attn_bout, L0_ffn_gate_w, L0_ffn_base_w,
           L0_ffn_base_b, L0_ffn_lora_A, L0_ffn_lora_B):
    import concourse.bacc as bacc
    from concourse.bass_utils import run_bass_kernel_spmd

    arr = np.asarray
    per_layer = [L0_attn_ln1_w, L0_attn_ln1_b, L0_attn_phz_re, L0_attn_phz_im, L0_attn_lc_re, L0_attn_lc_im,
                 L0_attn_sc_lin, L0_attn_ln2_w, L0_attn_ln2_b, L0_attn_b2]
    once = [np.broadcast_to(arr(v), (DEPTH, DIM)) for v in (L0_attn_lnl_w, L0_attn_lnl_b)]

    def chunked(w):
        w = arr(w)
        return w.reshape(-1, P, w.shape[-1]).transpose(1, 0, 2)

    low_rank = np.concatenate([arr(L0_ffn_lora_A).reshape(EXPERTS * RANK, VOC), arr(L0_ffn_gate_w)], axis=0)
    laid_out = {
        "log_dt": arr(L0_tok_log_dt).reshape(1, TOK),
        "tok_a": np.stack([arr(L0_tok_inv_A_real).T, arr(L0_tok_A_imag).T, arr(L0_tok_B)[..., 0].T,
                           arr(L0_tok_B)[..., 1].T], axis=1),
        "tok_c": arr(x).transpose(3, 2, 1, 0),
        "txt": arr(txt),
        "win_t": chunked(arr(L0_attn_Win).T),
        "bin_": arr(L0_attn_bin).reshape(DIM, 1),
        "vecs": np.stack([arr(v) for v in per_layer] + once).transpose(2, 1, 0),
        "b1": arr(L0_attn_b1).reshape(DEPTH, FC, P).transpose(2, 0, 1),
        "w1_t": arr(L0_attn_W1).transpose(0, 2, 1),
        "w2_t": np.stack([chunked(w.T) for w in arr(L0_attn_W2)]),
        "experts": np.concatenate([chunked(w).reshape(P, -1) for w in (
            arr(L0_ffn_base_w).T, low_rank.T, arr(L0_attn_Wout).T,
            arr(L0_ffn_lora_B).transpose(0, 2, 1).reshape(EXPERTS * RANK, VOC))], axis=1),
        "row_bias": np.stack([arr(L0_attn_bout), arr(L0_ffn_base_b)]),
    }
    nc = bacc.Bacc("TRN2", target_bir_lowering=False, num_devices=1)
    arrays, args = {}, []
    for name, a in laid_out.items():
        arrays["in_" + name] = np.ascontiguousarray(a)
        args.append(nc.dram_tensor("in_" + name, a.shape, mybir.dt.from_np(a.dtype), kind="ExternalInput").ap())
    args.append(nc.dram_tensor("out", (BATCH, SEQ, VOC), F32, kind="ExternalOutput").ap())
    build(nc, *args)
    return run_bass_kernel_spmd(nc, [arrays], core_ids=[0]).results[0]["out"]
```

```python
from contextlib import ExitStack

import numpy as np

import concourse.bass as bass
from concourse import mybir

F32 = mybir.dt.float32
F32R = mybir.dt.float32r
BF16 = mybir.dt.bfloat16
U32 = mybir.dt.uint32
ALU = mybir.AluOpType
ACT = mybir.ActivationFunctionType
AX = mybir.AxisListType

P = 128
BATCH = 16
SEQ = 256
TOK = 128
VOC = 1024
KC = VOC // P
STATES = 64
DIM = 128
DFF = 512
FC = DFF // P
DEPTH = 4
EXPERTS = 8
RANK = 16
EPS = 1e-5

NA, NB1, NB0 = 8, 8, 16
NJ = NA + NB1 + NB0
H_CHUNK = 32
H_BLOCK = 8
N_CHUNK = TOK // H_CHUNK
BLOCKS = H_CHUNK // H_BLOCK

TWO_PI = 2.0 * np.pi
INV_2PI = float(np.float32(1.0 / TWO_PI))
PI2_A = 6.28125
PI2_B = float(np.float32(round((TWO_PI - PI2_A) * 2**21) / 2**21))
PI2_C = float(np.float32(TWO_PI - PI2_A - PI2_B))
ROUND = 1.5 * 2**23
TURN = float(np.nextafter(np.float32(TWO_PI), np.float32(0)))
PI_IN = float(np.nextafter(np.float32(np.pi), np.float32(0)))

LN1_W, LN1_B, PHZ_RE, PHZ_IM, LC_RE, LC_IM, SC_LIN, LN2_W, LN2_B, B2, LNL_W, LNL_B = range(12)
N_VEC = 12
AG = EXPERTS * RANK + EXPERTS
WF_BASE, WF_AG = 0, KC * VOC
WF_OUT = WF_AG + KC * AG
WF_B = WF_OUT + VOC
N_WF = WF_B + VOC
GROUPS = BATCH // 2
UNIT = 2 * SEQ
WF_PIECE = N_WF // ((DEPTH - 1) * GROUPS)
assert WF_PIECE * (DEPTH - 1) * GROUPS == N_WF

LONG_RING = 4
RING = 2


def made(n, ring=RING):
    return n + (1 + ring)


def free(n):
    return n + 1


def build(nc, log_dt, tok_a, tok_c, txt, win_t, bin_, vecs, b1, w1_t, w2_t, experts, row_bias, out):
    with ExitStack() as whole:
        def sb(ctx, name, shape, dt=F32):
            return ctx.enter_context(nc.sbuf_tensor(name, shape, dt))

        def psum(ctx, name, shape, dt=F32):
            return ctx.enter_context(nc.psum_tensor(name, shape, dt))

        def sem(ctx, name):
            return ctx.enter_context(nc.semaphore(name))

        tok_rows = nc.dram_tensor("tok_rows", (TOK, BATCH, VOC), F32, kind="Internal").ap()

        hT = sb(whole, "hT", [P, BATCH, SEQ])
        ident = sb(whole, "ident", [P, P])
        center = sb(whole, "center", [P, P])
        minus_half = sb(whole, "minus_half", [P, 4])
        vec = sb(whole, "vec", [P, DEPTH, N_VEC])
        b1_sb = sb(whole, "b1_sb", [P, DEPTH, FC])
        w1 = sb(whole, "w1", [P, DFF])
        w2 = sb(whole, "w2", [P, FC, DIM])
        rot = sb(whole, "rot", [P, 2, DEPTH, SEQ])
        rot_scaled = sb(whole, "rot_scaled", [P, 2, DEPTH, SEQ])
        rate = sb(whole, "rate", [P, DEPTH])
        state0 = sb(whole, "state0", [P, 2, DEPTH])
        tokens_and_projection(nc, sb, psum, sem, log_dt, tok_a, tok_c, txt, win_t, bin_, vecs, b1, w1_t, w2_t,
                              tok_rows, hT, ident, center, minus_half, vec, b1_sb, w1, w2,
                              rot, rot_scaled, rate, state0)
        with ExitStack() as late:
            wf = sb(late, "wf", [P, 2, N_WF], F32R)
            mixer(nc, sb, psum, sem, w1_t, w2_t, experts, hT, ident, center, minus_half, vec, b1_sb, w1, w2,
                  rot, rot_scaled, rate, state0, wf)
            experts_stage(nc, sb, psum, sem, txt, row_bias, tok_rows, hT, ident, minus_half, vec, wf, out)


def tokens_and_projection(nc, sb, psum, sem, log_dt, tok_a, tok_c, txt, win_t, bin_, vecs, b1, w1_t, w2_t,
                          tok_rows, hT, ident, center, minus_half, vec, b1_sb, w1, w2,
                          rot, rot_scaled, rate, state0):
    with ExitStack() as ctx:
        ldt = sb(ctx, "ldt", [P, TOK])
        par = sb(ctx, "par", [P, 4, TOK])
        c_re = sb(ctx, "c_re", [P, TOK, BATCH])
        c_im = sb(ctx, "c_im", [P, TOK, BATCH])
        small = sb(ctx, "small", [P, 24, TOK])
        half = sb(ctx, "half", [P, DEPTH])
        ph = sb(ctx, "ph", [P, 5, DEPTH])
        eps = sb(ctx, "eps", [P, 1])
        half_pi = sb(ctx, "half_pi", [P, 1])
        alpha = sb(ctx, "alpha", [P, TOK])
        beta = sb(ctx, "beta", [P, TOK])
        powers = sb(ctx, "powers", [P, NJ])
        turns = sb(ctx, "turns", [P, H_CHUNK, NJ])
        whole_turns = sb(ctx, "whole_turns", [P, H_CHUNK, NJ])
        mag = sb(ctx, "decay", [P, H_CHUNK, NJ])
        sin = sb(ctx, "sin", [P, H_CHUNK, NJ])
        cos = sb(ctx, "cos", [P, H_CHUNK, NJ])
        w_re = sb(ctx, "w_re", [P, H_CHUNK, NA + NB1])
        w_im = sb(ctx, "w_im", [P, H_CHUNK, NA + NB1])
        n1 = sb(ctx, "n1", [P, H_CHUNK, NB0])
        n2 = sb(ctx, "n2", [P, H_CHUNK, NB0])
        pt = sb(ctx, "pt", [P, 4, H_CHUNK, NA])
        p1 = sb(ctx, "p1", [P, H_CHUNK, NA])
        p2 = sb(ctx, "p2", [P, H_CHUNK, NA])
        x1 = sb(ctx, "x1", [P, RING, H_BLOCK, BATCH, NA])
        x2 = sb(ctx, "x2", [P, RING, H_BLOCK, BATCH, NA])
        y1 = sb(ctx, "y1", [P, RING, H_BLOCK, NB1, NB0])
        y2 = sb(ctx, "y2", [P, RING, H_BLOCK, NB1, NB0])
        vv = sb(ctx, "vv", [P, RING, H_BLOCK, NB1 * NB0])
        rows_out = sb(ctx, "rows_out", [P, RING, H_BLOCK, P])
        wts = sb(ctx, "win_sb", [P, KC, DIM])
        bin_sb = sb(ctx, "bin_sb", [P, 1])
        raw = sb(ctx, "raw", [P, LONG_RING, VOC])
        stats = sb(ctx, "stats", [P, LONG_RING, 2, 6])
        mv = sb(ctx, "mv", [P, LONG_RING, 2])
        var_eps = sb(ctx, "var_eps", [P, LONG_RING])
        rstd = sb(ctx, "rstd", [P, LONG_RING])
        shift = sb(ctx, "shift", [P, LONG_RING])
        xhat = sb(ctx, "xhat", [P, RING, VOC])
        xT = sb(ctx, "xT", [P, RING, KC, P])

        k_ps = [psum(ctx, f"k_ps{i}", [P, 4, P]) for i in range(2)]
        t_ps = [psum(ctx, f"t_ps{i}", [P, 4, P]) for i in range(4)]
        w_ps = [psum(ctx, f"w_ps{i}", [P, 512]) for i in range(RING)]

        vec_in = sem(ctx, "vec_in")
        ffn_in = sem(ctx, "ffn_in")
        first_rotations = sem(ctx, "first_rotations")
        rot_steps = sem(ctx, "rot_steps")
        pool_small = sem(ctx, "pool_small")
        par_in = sem(ctx, "par_in")
        c_in = sem(ctx, "c_in")
        win_in = sem(ctx, "win_in")
        consts = sem(ctx, "consts")
        act_small = sem(ctx, "act_small")
        dve_small = sem(ctx, "dve_small")
        turns_steps = sem(ctx, "turns_steps")
        coef_made = sem(ctx, "coef_made")
        decay_made = sem(ctx, "decay_made")
        mag_made = sem(ctx, "mag_made")
        sincos_made = sem(ctx, "sincos_made")
        dve_tables = sem(ctx, "dve_tables")
        pool_tables = sem(ctx, "pool_tables")
        x1_made = sem(ctx, "x1_made")
        x2_made = sem(ctx, "x2_made")
        y1_made = sem(ctx, "y1_made")
        y2_made = sem(ctx, "y2_made")
        vv_made = sem(ctx, "vv_made")
        k_done = sem(ctx, "k_done")
        k_moved = sem(ctx, "k_moved")
        rows_stored = [sem(ctx, f"rows_stored{i}") for i in range(RING)]
        raw_in = [sem(ctx, f"raw_in{i}") for i in range(LONG_RING)]
        stats_made = sem(ctx, "stats_made")
        waited = sem(ctx, "waited")
        mv_made = sem(ctx, "mv_made")
        ve_made = sem(ctx, "ve_made")
        rstd_made = sem(ctx, "rstd_made")
        shift_made = sem(ctx, "shift_made")
        xhat_made = sem(ctx, "xhat_made")
        xT_done = sem(ctx, "xT_done")
        xT_moved = sem(ctx, "xT_moved")
        win_done = sem(ctx, "win_done")
        win_moved = sem(ctx, "win_moved")
        block = ctx.enter_context(nc.Block())

        N_BLOCK = N_CHUNK * BLOCKS
        TILES = 2 * BATCH
        CONSTS = 9
        TURN_STEPS = 4
        DVE_TABLES = 8
        POOL_TABLES = 4

        def slots(eng, slot):
            def four(q, s4d, n=BLOCKS):
                for b in range(n):
                    slot(q, b, s4d)

            four(0, True)
            with eng.Fori(1, N_CHUNK - 1) as q:
                four(q, True)
            four(N_CHUNK - 1, True)
            four(N_CHUNK, False)
            with eng.Fori(N_CHUNK + 1, TILES // BLOCKS) as q:
                four(q, False)
            four(TILES // BLOCKS, False, 3)

        def scaled_rotations(dve):
            count = [0]

            def step(ins):
                count[0] += 1
                ins.then_inc(rot_steps, 1)
                dve.wait_ge(rot_steps, count[0])

            def mul(o, a, b):
                step(dve.tensor_tensor(o, a, b, ALU.mult))

            rt = y1[:].rearrange("p r h a b -> p (r h a b)").rearrange("p (n l t) -> p n l t", n=4, l=DEPTH)
            dve.wait_ge(first_rotations, 1)
            double(dve, mul, step, rt, EARLY, SEQ)
            for part in range(2):
                mul(rot_scaled[:, part], rot[:, part], vec[:, :, SC_LIN].unsqueeze(2).to_broadcast([P, DEPTH, SEQ]))

        def is_last(q):
            return isinstance(q, int) and q == N_CHUNK - 1

        def tile(q, b, lag):
            t = BLOCKS * q + (b - lag)
            return None if isinstance(t, int) and not 0 <= t < TILES else t

        def place(q, b, t, s4d):
            text = t < BATCH if isinstance(t, int) else s4d
            return hT[:, bass.ds(t if text else t - BATCH, 1), (P if text else 0):(2 * P if text else P)].rearrange("d o t -> d (o t)")

        def carry(eng):
            eng.sem_inc(waited, 1)

        @block.sync
        def _(sp):
            sp.dma_start(ldt[:], log_dt.to_broadcast([P, TOK])).then_inc(par_in, 16)
            for slot in range(2):
                sp.dma_start(par[slot * STATES:(slot + 1) * STATES], tok_a).then_inc(par_in, 16)
            sp.dma_start(vec[:], vecs).then_inc(vec_in, 16)
            for part, dst in enumerate((c_re, c_im)):
                for slot in range(2):
                    sp.dma_start(dst[slot * STATES:(slot + 1) * STATES], tok_c[part]).then_inc(c_in, 16)
            sp.dma_start(wts[:], win_t).then_inc(win_in, 16)
            sp.dma_start(bin_sb[:], bin_).then_inc(win_in, 16)
            def load_text(t, r):
                sp.wait_ge(xhat_made, free(t))
                sp.dma_start(raw[:, r], txt[bass.ds(t, 1)].rearrange("o s v -> (o s) v")).then_inc(raw_in[r], 16)

            def store_block(q, b):
                sp.wait_ge(k_moved, 2 * (BLOCKS * q + b) + 4)
                sp.dma_start(tok_rows[bass.ds(q * H_CHUNK + b * H_BLOCK, H_BLOCK)].rearrange("h c (a l) -> (c a) h l", l=P),
                             rows_out[:, b % RING]).then_inc(rows_stored[b % RING], 16)

            for t in range(LONG_RING - 1):
                load_text(t, t)
            with sp.Fori(0, N_CHUNK - 1) as q:
                for b in range(BLOCKS):
                    load_text(BLOCKS * q + (b + LONG_RING - 1), (b - 1) % LONG_RING)
                    store_block(q, b)
            load_text(BATCH - 1, LONG_RING - 1)
            for b in range(BLOCKS):
                store_block(N_CHUNK - 1, b)
            for r in range(RING):
                sp.wait_ge(rows_stored[r], 16 * (N_BLOCK // RING + 1))
            with sp.Fori(0, BATCH // LONG_RING) as i:
                for b in range(LONG_RING):
                    sp.wait_ge(xhat_made, free(LONG_RING * i + (b + BATCH)))
                    sp.dma_start(raw[:, b], tok_rows[:, bass.ds(LONG_RING * i + b, 1)].rearrange("s o v -> s (o v)")).then_inc(raw_in[b], 16)
            sp.dma_start(b1_sb[:], b1).then_inc(ffn_in, 16)
            sp.dma_start(w1[:], w1_t[0]).then_inc(ffn_in, 16)
            sp.dma_start(w2[:], w2_t[0]).then_inc(ffn_in, 16)
            sp.wait_ge(ffn_in, 48)

        EARLY = 64

        def double(eng, mul, step, rt, m, end):
            while m < end:
                k = min(m, SEQ - 1 - m)
                here = lambda part: rot[:, part, :, 1:1 + k]
                turn = lambda part: rot[:, part, :, m:m + 1].to_broadcast([P, DEPTH, k])
                for n, (a, b) in enumerate(((0, 0), (1, 1), (0, 1), (1, 0))):
                    mul(rt[:, n, :, 0:k], here(a), turn(b))
                step(eng.tensor_tensor(rot[:, 0, :, m + 1:m + 1 + k], rt[:, 0, :, 0:k], rt[:, 1, :, 0:k], ALU.subtract))
                step(eng.tensor_tensor(rot[:, 1, :, m + 1:m + 1 + k], rt[:, 2, :, 0:k], rt[:, 3, :, 0:k], ALU.add))
                m *= 2

        def mixer_tables(pool):
            count = [0]

            def step(ins):
                count[0] += 1
                ins.then_inc(pool_small, 1)
                pool.wait_ge(pool_small, count[0])

            def mul(o, a, b):
                step(pool.tensor_tensor(o, a, b, ALU.mult))

            rt = y2[:].rearrange("p r h a b -> p (r h a b)").rearrange("p (n l t) -> p n l t", n=4, l=DEPTH)
            v = lambda k: vec[:, :, k]
            t = lambda k: ph[:, k]
            pool.wait_ge(vec_in, 16)
            mul(t(0), v(PHZ_RE), v(PHZ_RE))
            mul(t(1), v(PHZ_IM), v(PHZ_IM))
            step(pool.tensor_tensor(t(0), t(0), t(1), ALU.add))
            step(pool.tensor_tensor(t(2), t(0), half[:], ALU.pow))
            step(pool.tensor_scalar(t(1), t(0), 1e-37, None, ALU.max))
            step(pool.tensor_tensor(t(1), t(1), minus_half[:], ALU.pow))
            step(pool.tensor_scalar(t(3), t(2), 0.0, None, ALU.is_equal))
            pool.wait_ge(dve_small, 2)
            chunk_exponents(pool, 0)
            mul(t(4), v(PHZ_RE), t(1))
            step(pool.tensor_tensor(rot[:, 0, :, 1], t(4), t(3), ALU.add))
            mul(rot[:, 1, :, 1], v(PHZ_IM), t(1))
            step(pool.memset(rot[:, 0, :, 0], 1.0))
            step(pool.memset(rot[:, 1, :, 0], 0.0))
            double(pool, mul, step, rt, 1, EARLY)
            c, s_ = rot[:, 0, :, 1], rot[:, 1, :, 1]
            mul(t(0), c, v(LC_RE))
            mul(t(1), s_, v(LC_IM))
            step(pool.tensor_tensor(state0[:, 0], t(0), t(1), ALU.subtract))
            mul(t(0), s_, v(LC_RE))
            mul(t(1), c, v(LC_IM))
            step(pool.tensor_tensor(t(0), t(0), t(1), ALU.add))
            step(pool.tensor_scalar(state0[:, 1], t(0), -1.0, None, ALU.mult))

        def chunk_exponents(pool, q):
            pool.tensor_tensor(
                mag[:], small[:, 0, bass.ds(q * H_CHUNK, H_CHUNK)].unsqueeze(2).to_broadcast([P, H_CHUNK, NJ]),
                powers[:].unsqueeze(1).to_broadcast([P, H_CHUNK, NJ]), ALU.mult).then_inc(decay_made, 1)

        @block.gpsimd
        def _(pool):
            pool.memset(half[:], 0.5).then_inc(consts, 1)
            pool.memset(ident[:], 0.0).then_inc(consts, 1)
            pool.memset(minus_half[:], -0.5).then_inc(consts, 1)
            pool.iota(powers[:, 0:NA], pattern=[[P, NA]], base=0, channel_multiplier=0,
                      allow_small_or_imprecise_dtypes=True).then_inc(consts, 1)
            pool.iota(powers[:, NA:NA + NB1], pattern=[[NB0, NB1]], base=0, channel_multiplier=0,
                      allow_small_or_imprecise_dtypes=True).then_inc(consts, 1)
            pool.iota(powers[:, NA + NB1:NJ], pattern=[[1, NB0]], base=0, channel_multiplier=0,
                      allow_small_or_imprecise_dtypes=True).then_inc(consts, 1)
            pool.memset(eps[:], EPS).then_inc(consts, 1)
            pool.memset(half_pi[:], 0.5 * np.pi).then_inc(consts, 1)
            pool.wait_ge(consts, 2)
            pool.affine_select(out=ident[:], in_=ident[:], compare_op=ALU.not_equal, fill=1.0, base=0,
                               pattern=[[-1, P]], channel_multiplier=1).then_inc(consts, 1)
            pool.sem_inc(x2_made, 1)
            pool.sem_inc(y2_made, 1)
            pool.wait_ge(consts, CONSTS)
            mixer_tables(pool)
            pool.sem_inc(first_rotations, 1)
            pool.wait_ge(c_in, 64)
            pool.wait_ge(coef_made, 1)

            def tables(q):
                hq = bass.ds(q * H_CHUNK, H_CHUNK)
                ab = slice(0, NA + NB1)
                base = q * POOL_TABLES
                pool.wait_ge(mag_made, q + 1)
                pool.wait_ge(sincos_made, 2 * q + 2)
                if not (isinstance(q, int) and q == 0):
                    pool.wait_ge(dve_tables, q * DVE_TABLES)
                pool.tensor_tensor(w_im[:], mag[:, :, ab], sin[:, :, ab], ALU.mult).then_inc(pool_tables, 1)
                pool.wait_ge(pool_tables, base + 1)
                for k, c in ((1, beta), (3, alpha)):
                    pool.tensor_tensor(pt[:, k], w_im[:, :, 0:NA], c[:, hq].unsqueeze(2).to_broadcast([P, H_CHUNK, NA]),
                                       ALU.mult).then_inc(pool_tables, 1)
                pool.wait_ge(pool_tables, base + 3)
                pool.wait_ge(dve_tables, q * DVE_TABLES + 7)
                pool.tensor_tensor(p2[:], pt[:, 2], pt[:, 3], ALU.subtract).then_inc(pool_tables, 1)
                pool.wait_ge(pool_tables, base + 4)

            def slot(q, b, s4d):
                if s4d:
                    n = q * BLOCKS + b
                    r = b % RING
                    hs = slice(b * H_BLOCK, (b + 1) * H_BLOCK)
                    if b == 0:
                        tables(q)
                    pool.wait_ge(k_done, 2 * free(n))
                    pool.tensor_tensor(
                        x2[:, r], c_im[:, bass.ds(q * H_CHUNK + b * H_BLOCK, H_BLOCK)].unsqueeze(3).to_broadcast([P, H_BLOCK, BATCH, NA]),
                        p2[:, hs].unsqueeze(2).to_broadcast([P, H_BLOCK, BATCH, NA]), ALU.mult).then_inc(x2_made, 1)
                    pool.wait_ge(vv_made, free(n))
                    pool.tensor_tensor(
                        y2[:, r], w_im[:, hs, NA:].unsqueeze(3).to_broadcast([P, H_BLOCK, NB1, NB0]),
                        n2[:, hs].unsqueeze(2).to_broadcast([P, H_BLOCK, NB1, NB0]), ALU.mult).then_inc(y2_made, 1)
                t = tile(q, b, 1)
                if t is not None:
                    at = (b - 1) % LONG_RING
                    pool.wait_ge(mv_made, t + 1)
                    pool.tensor_tensor(var_eps[:, at:at + 1], mv[:, at, 1:2], eps[:], ALU.add).then_inc(ve_made, 1)
                    pool.wait_ge(ve_made, t + 1)
                    pool.tensor_tensor(rstd[:, at:at + 1], var_eps[:, at:at + 1], minus_half[:, 0:1], ALU.pow).then_inc(rstd_made, 1)
                    pool.wait_ge(rstd_made, t + 1)
                    carry(pool)
                    pool.tensor_scalar(shift[:, at:at + 1], mv[:, at, 0:1], rstd[:, at:at + 1], -1.0, ALU.mult, ALU.mult).then_inc(shift_made, 1)
                if s4d and b == 0 and not is_last(q):
                    pool.wait_ge(dve_tables, (q + 1) * DVE_TABLES)
                    chunk_exponents(pool, q + 1)

            slots(pool, slot)

        @block.vector
        def _(dve):
            count = [0]

            def step(ins):
                count[0] += 1
                ins.then_inc(dve_small, 1)
                dve.wait_ge(dve_small, count[0])

            def turns_first(q):
                hq = bass.ds(q * H_CHUNK, H_CHUNK)
                dve.tensor_tensor(turns[:], small[:, RHO, hq].unsqueeze(2).to_broadcast([P, H_CHUNK, NJ]),
                                  powers[:].unsqueeze(1).to_broadcast([P, H_CHUNK, NJ]), ALU.mult).then_inc(turns_steps, 1)
                dve.wait_ge(turns_steps, q * TURN_STEPS + 1)
                dve.tensor_scalar(whole_turns[:], turns[:], ROUND, ROUND, ALU.add, ALU.subtract).then_inc(turns_steps, 1)

            def turns_second(q):
                dve.wait_ge(turns_steps, q * TURN_STEPS + 2)
                dve.tensor_tensor(turns[:], turns[:], whole_turns[:], ALU.subtract).then_inc(turns_steps, 1)
                dve.wait_ge(turns_steps, q * TURN_STEPS + 3)
                dve.scalar_tensor_tensor(whole_turns[:], turns[:], -1.0, turns[:], ALU.mult, ALU.max).then_inc(turns_steps, 1)

            S = lambda k: small[:, k]
            X, THETA, K, R, RHO, DT, EAR, T, OMT, EM1, E, S2, ER, EI, NR, NI, A2, Q, GR, GI, TA, TB, AR = range(23)
            dve.wait_ge(consts, CONSTS)
            step(dve.tensor_scalar(center[:], ident[:], -1.0 / DIM, None, ALU.add))
            dve.wait_ge(act_small, 2)
            step(dve.scalar_tensor_tensor(S(X), S(EAR), -1.0, S(DT), ALU.mult, ALU.mult))
            step(dve.tensor_tensor(S(THETA), par[:, 1], S(DT), ALU.mult))
            step(dve.tensor_scalar(S(K), S(THETA), INV_2PI, ROUND, ALU.mult, ALU.add))
            step(dve.tensor_scalar(S(K), S(K), ROUND, None, ALU.subtract))
            step(dve.scalar_tensor_tensor(S(R), S(K), -PI2_A, S(THETA), ALU.mult, ALU.add))
            step(dve.scalar_tensor_tensor(S(R), S(K), -PI2_B, S(R), ALU.mult, ALU.add))
            step(dve.scalar_tensor_tensor(S(R), S(K), -PI2_C, S(R), ALU.mult, ALU.add))
            step(dve.tensor_scalar(S(RHO), S(R), INV_2PI, None, ALU.mult))
            step(dve.tensor_scalar(S(R), S(R), PI_IN, -PI_IN, ALU.min, ALU.max))
            turns_first(0)
            turns_second(0)
            dve.wait_ge(act_small, 3)
            step(dve.tensor_scalar(S(OMT), S(T), -1.0, 1.0, ALU.mult, ALU.add))
            step(dve.reciprocal(S(Q), S(OMT)))
            step(dve.scalar_tensor_tensor(S(EM1), S(T), 2.0, S(Q), ALU.mult, ALU.mult))
            step(dve.tensor_scalar(S(E), S(EM1), 1.0, None, ALU.add))
            dve.wait_ge(act_small, 5)
            step(dve.tensor_tensor(S(TA), S(S2), S(S2), ALU.mult))
            step(dve.tensor_tensor(S(TA), S(TA), S(E), ALU.mult))
            step(dve.scalar_tensor_tensor(S(ER), S(TA), -2.0, S(EM1), ALU.mult, ALU.add))
            step(dve.tensor_tensor(S(EI), S(EI), S(E), ALU.mult))
            step(dve.tensor_scalar(S(AR), S(EAR), -1.0, None, ALU.mult))

            def complex_times(re, im, a_re, a_im, b_re, b_im, conj):
                one, two = (ALU.add, ALU.subtract) if conj else (ALU.subtract, ALU.add)
                step(dve.tensor_tensor(S(TA), a_re, b_re, ALU.mult))
                step(dve.tensor_tensor(S(TB), a_im, b_im, ALU.mult))
                step(dve.tensor_tensor(re, S(TA), S(TB), one))
                step(dve.tensor_tensor(S(TA), a_im, b_re, ALU.mult))
                step(dve.tensor_tensor(S(TB), a_re, b_im, ALU.mult))
                step(dve.tensor_tensor(im, S(TA), S(TB), two))

            complex_times(S(NR), S(NI), S(ER), S(EI), S(AR), par[:, 1], True)
            complex_times(S(GR), S(GI), S(NR), S(NI), par[:, 2], par[:, 3], False)
            step(dve.tensor_tensor(S(TA), S(AR), S(AR), ALU.mult))
            step(dve.tensor_tensor(S(TB), par[:, 1], par[:, 1], ALU.mult))
            step(dve.tensor_tensor(S(A2), S(TA), S(TB), ALU.add))
            step(dve.reciprocal(S(Q), S(A2)))
            step(dve.tensor_tensor(S(GR), S(GR), S(Q), ALU.mult))
            step(dve.tensor_tensor(S(GI), S(GI), S(Q), ALU.mult))
            for slot_, (dst, src, f) in enumerate(((alpha, GR, 2.0), (alpha, GI, -2.0), (beta, GI, -2.0), (beta, GR, -2.0))):
                ps = slice(slot_ % 2 * STATES, (slot_ % 2 + 1) * STATES)
                step(dve.tensor_scalar(dst[ps], small[ps, src], f, None, ALU.mult))
            dve.sem_inc(coef_made, 1)
            dve.sem_inc(vv_made, RING)
            dve.wait_ge(c_in, 64)

            def tables(q):
                hq = bass.ds(q * H_CHUNK, H_CHUNK)
                ab = slice(0, NA + NB1)
                b0 = slice(NA + NB1, NJ)
                re, im = slice(0, STATES), slice(STATES, P)
                base = q * DVE_TABLES
                dve.wait_ge(mag_made, q + 1)
                dve.wait_ge(sincos_made, 2 * q + 2)
                dve.tensor_tensor(w_re[:], mag[:, :, ab], cos[:, :, ab], ALU.mult).then_inc(dve_tables, 1)
                dve.tensor_tensor(n1[re], mag[re, :, b0], cos[re, :, b0], ALU.mult).then_inc(dve_tables, 1)
                dve.wait_ge(dve_tables, base + 1)
                dve.wait_ge(x2_made, free(BLOCKS * q))
                for k, c in ((0, alpha), (2, beta)):
                    dve.tensor_tensor(pt[:, k], w_re[:, :, 0:NA], c[:, hq].unsqueeze(2).to_broadcast([P, H_CHUNK, NA]),
                                      ALU.mult).then_inc(dve_tables, 1)
                dve.wait_ge(y2_made, free(BLOCKS * q))
                dve.tensor_tensor(n1[im], mag[im, :, b0], sin[im, :, b0], ALU.mult).then_inc(dve_tables, 1)
                dve.scalar_tensor_tensor(n2[re], mag[re, :, b0], -1.0, sin[re, :, b0], ALU.mult, ALU.mult).then_inc(dve_tables, 1)
                dve.tensor_tensor(n2[im], mag[im, :, b0], cos[im, :, b0], ALU.mult).then_inc(dve_tables, 1)
                dve.wait_ge(pool_tables, q * POOL_TABLES + 2)
                dve.wait_ge(dve_tables, base + 7)
                dve.tensor_tensor(p1[:], pt[:, 0], pt[:, 1], ALU.add).then_inc(dve_tables, 1)
                dve.wait_ge(dve_tables, base + 8)

            def slot(q, b, s4d):
                if s4d:
                    n = q * BLOCKS + b
                    r = b % RING
                    hs = slice(b * H_BLOCK, (b + 1) * H_BLOCK)
                    if b == 0:
                        tables(q)
                    dve.wait_ge(k_done, 2 * free(n))
                    dve.tensor_tensor(
                        y1[:, r], w_re[:, hs, NA:].unsqueeze(3).to_broadcast([P, H_BLOCK, NB1, NB0]),
                        n1[:, hs].unsqueeze(2).to_broadcast([P, H_BLOCK, NB1, NB0]), ALU.mult).then_inc(y1_made, 1)
                    dve.tensor_tensor(
                        x1[:, r], c_re[:, bass.ds(q * H_CHUNK + b * H_BLOCK, H_BLOCK)].unsqueeze(3).to_broadcast([P, H_BLOCK, BATCH, NA]),
                        p1[:, hs].unsqueeze(2).to_broadcast([P, H_BLOCK, BATCH, NA]), ALU.mult).then_inc(x1_made, 1)
                if isinstance(q, int) and q == N_CHUNK and b == 0:
                    scaled_rotations(dve)
                t = tile(q, b, 0)
                if t is not None:
                    dve.wait_ge(raw_in[b], 16 * q + 16)
                    for k in range(2):
                        dve.bn_stats(stats[:, b, k], raw[:, b, k * 512:(k + 1) * 512]).then_inc(stats_made, 1)
                if s4d and not is_last(q):
                    if b == 0:
                        dve.wait_ge(sincos_made, 2 * q + 2)
                        turns_first(q + 1)
                    if b == 1:
                        turns_second(q + 1)
                if t is not None:
                    dve.wait_ge(stats_made, 2 * t + 2)
                    carry(dve)
                    dve.bn_aggr(mv[:, b], stats[:, b].rearrange("p a b -> p (a b)")).then_inc(mv_made, 1)
                if s4d:
                    dve.wait_ge(y1_made, n + 1)
                    dve.wait_ge(y2_made, made(n, 1))
                    dve.tensor_tensor(vv[:, r], y1[:, r].rearrange("p h a b -> p h (a b)"),
                                      y2[:, r].rearrange("p h a b -> p h (a b)"), ALU.add).then_inc(vv_made, 1)

            slots(dve, slot)

        @block.scalar
        def _(act):
            X, THETA, K, R, RHO, DT, EAR, T, OMT, EM1, E, S2, ER, EI = range(14)
            for r in range(RING):
                act.sem_inc(rows_stored[r], 16)
            act.sem_inc(k_moved, 2)
            act.sem_inc(xhat_made, LONG_RING)
            act.sem_inc(xT_moved, 2 * RING)
            act.sem_inc(win_moved, RING)
            act.wait_ge(consts, CONSTS)
            act.wait_ge(par_in, 48)
            act.activation(small[:, DT], ldt[:], ACT.Exp).then_inc(act_small, 1)
            act.activation(small[:, EAR], par[:, 0], ACT.Exp).then_inc(act_small, 1)
            act.wait_ge(dve_small, 2)
            act.activation(small[:, T], small[:, X], ACT.Tanh, scale=0.5).then_inc(act_small, 1)

            def decay(q):
                act.wait_ge(decay_made, q + 1)
                act.activation(mag[:], mag[:], ACT.Exp).then_inc(mag_made, 1)

            def sines(q):
                act.wait_ge(turns_steps, q * TURN_STEPS + 4)
                act.activation(sin[:], turns[:], ACT.Sin, scale=TURN).then_inc(sincos_made, 1)
                act.activation(cos[:], whole_turns[:], ACT.Sin, scale=-TURN, bias=half_pi[:]).then_inc(sincos_made, 1)

            act.wait_ge(pool_small, 4)
            act.activation(rate[:], ph[:, 2], ACT.Tanh)
            decay(0)
            act.wait_ge(dve_small, 10)
            act.activation(small[:, EI], small[:, R], ACT.Sin).then_inc(act_small, 1)
            act.activation(small[:, S2], small[:, R], ACT.Sin, scale=0.5).then_inc(act_small, 1)
            sines(0)

            def slot(q, b, s4d):
                def move_rows(k):
                    n = q * BLOCKS + b
                    r = b % RING
                    act.wait_ge(k_done, 2 * n + (k + 1 + 2 * RING))
                    act.activation(rows_out[:, r, 4 * k:4 * k + 4], k_ps[k][:], ACT.Copy).then_inc(k_moved, 1)

                if s4d:
                    if b == 0 and not is_last(q):
                        decay(q + 1)
                    if b == 1 and not is_last(q):
                        act.wait_ge(pool_tables, (q + 1) * POOL_TABLES)
                        act.wait_ge(dve_tables, (q + 1) * DVE_TABLES)
                        sines(q + 1)
                    act.wait_ge(rows_stored[b % RING], q * (8 * BLOCKS) + 8 * (b - b % RING + RING))
                    move_rows(0)
                t = tile(q, b, 2)
                if t is not None:
                    at = (b - 2) % RING
                    act.wait_ge(win_done, free(t))
                    for k in range(2):
                        act.wait_ge(xT_done, 2 * t + (k + 1 + 2 * RING))
                        act.activation(xT[:, at, 4 * k:4 * k + 4], t_ps[2 * at + k][:], ACT.Copy).then_inc(xT_moved, 1)
                if s4d:
                    move_rows(1)
                t = tile(q, b, 1)
                if t is not None:
                    at = (b - 1) % LONG_RING
                    act.wait_ge(shift_made, t + 1)
                    act.wait_ge(xT_done, 2 * free(t))
                    carry(act)
                    act.activation(xhat[:, (b - 1) % RING], raw[:, at], ACT.Identity, bias=shift[:, at:at + 1],
                                   scale=rstd[:, at:at + 1]).then_inc(xhat_made, 1)
                t = tile(q, b, 3)
                if t is not None:
                    act.wait_ge(win_done, made(t))
                    carry(act)
                    act.activation(place(q, b, t, s4d), w_ps[(b - 3) % RING][:, 0:P], ACT.Identity, bias=bin_sb[:]).then_inc(win_moved, 1)

            act.wait_ge(win_in, 32)
            slots(act, slot)

        @block.tensor
        def _(pe):
            pe.sem_inc(k_done, 2 * RING)
            pe.sem_inc(xT_done, 2 * RING)
            pe.sem_inc(win_done, RING)

            def slot(q, b, s4d):
                def expand(k):
                    n = q * BLOCKS + b
                    r = b % RING
                    if k == 0:
                        pe.wait_ge(x1_made, n + 1)
                        pe.wait_ge(x2_made, made(n, 1))
                        pe.wait_ge(vv_made, made(n))
                    pe.wait_ge(k_moved, 2 * n + (k + 1))
                    for g in range(4):
                        h = 4 * k + g
                        for x in (x1, x2):
                            mm = pe.matmul(k_ps[k][:, g], x[:, r, h].rearrange("p c a -> p (c a)"), vv[:, r, h],
                                           start=(x is x1), stop=(x is x2))
                    mm.then_inc(k_done, 1)

                if s4d:
                    expand(0)
                t = tile(q, b, 2)
                if t is not None:
                    at = (b - 2) % RING
                    pe.wait_ge(xhat_made, made(t, LONG_RING))
                    pe.wait_ge(xT_moved, 2 * free(t))
                    for k in range(2):
                        for c in range(4):
                            mm = pe.transpose(t_ps[2 * at + k][:, c], xhat[:, at, (4 * k + c) * P:(4 * k + c + 1) * P], ident[:])
                        mm.then_inc(xT_done, 1)
                if s4d:
                    expand(1)
                t = tile(q, b, 3)
                if t is not None:
                    at = (b - 3) % RING
                    pe.wait_ge(xT_moved, 2 * made(t))
                    pe.wait_ge(win_moved, free(t))
                    for c in range(KC):
                        mm = pe.matmul(w_ps[at][:, 0:P], wts[:, c], xT[:, at, c], start=(c == 0), stop=(c == KC - 1))
                    mm.then_inc(win_done, 1)

            pe.wait_ge(win_in, 32)
            slots(pe, slot)


def mixer(nc, sb, psum, sem, w1_t, w2_t, experts, hT, ident, center, minus_half, vec, b1_sb, w1, w2,
          rot, rot_scaled, rate, state0, wf):
    with ExitStack() as ctx:
        def buf(name, shape, dt=F32):
            return sb(ctx, name, shape, dt)

        sq = [buf(f"sq{n}", [P, 4, P]) for n in (1, 2)]
        ss = [buf(f"ss{n}", [P, 4]) for n in (1, 2)]
        ve = [buf(f"ve{n}", [P, 4]) for n in (1, 2)]
        rstd = [buf(f"l_rstd{n}", [P, 4]) for n in (1, 2)]
        xn = [buf(f"xn{n}", [P, 4, P]) for n in (1, 2)]
        y = buf("y", [P, 2, SEQ])
        u_re = buf("u_re", [P, 2, SEQ])
        u_im = buf("u_im", [P, 2, SEQ])
        z_re = buf("z_re", [P, 2, SEQ])
        z_im = buf("z_im", [P, 2, SEQ])
        c_re = buf("conv_re", [P, 2, SEQ])
        c_im = buf("conv_im", [P, 2, SEQ])
        h_mid = buf("h_mid", [P, 2, SEQ])
        y2 = buf("y2l", [P, UNIT])
        s = buf("s", [P, FC, UNIT])
        wf_raw = buf("wf_raw", [P, RING, WF_PIECE])

        c_ps = [psum(ctx, f"c_ps{n}", [P, 4, P]) for n in (1, 2)]
        t_ps = [psum(ctx, f"tl_ps{n}", [P, 4 * P]) for n in (1, 2)]
        m_ps = [psum(ctx, f"m_ps{n}", [P, UNIT]) for n in range(3)]
        o_ps = psum(ctx, "o_ps", [P, UNIT])

        centered = [sem(ctx, f"centered{n}") for n in (1, 2)]
        squared = [sem(ctx, f"squared{n}") for n in (1, 2)]
        summed = [sem(ctx, f"summed{n}") for n in (1, 2)]
        ve_made = [sem(ctx, f"lve_made{n}") for n in (1, 2)]
        rstd_made = [sem(ctx, f"lrstd_made{n}") for n in (1, 2)]
        xn_made = [sem(ctx, f"xn_made{n}") for n in (1, 2)]
        turned = [sem(ctx, f"turned{n}") for n in (1, 2)]
        y_made = sem(ctx, "y_made")
        u_re_made = sem(ctx, "u_re_made")
        u_im_made = sem(ctx, "u_im_made")
        z_re_made = sem(ctx, "z_re_made")
        z_im_made = sem(ctx, "z_im_made")
        c_re_made = sem(ctx, "c_re_made")
        c_im_made = sem(ctx, "c_im_made")
        h_mid_made = sem(ctx, "h_mid_made")
        h1_made = sem(ctx, "h1_made")
        y2_made = sem(ctx, "y2l_made")
        m_done = sem(ctx, "m_done")
        s_made = sem(ctx, "s_made")
        o_done = sem(ctx, "o_done")
        res_made = sem(ctx, "res_made")
        waited = sem(ctx, "l_waited")
        w1_in = sem(ctx, "w1_in")
        w2_in = sem(ctx, "w2_in")
        piece_in = [sem(ctx, f"piece_in{r}") for r in range(RING)]
        hi_made = sem(ctx, "hi_made")
        lo_made = sem(ctx, "lo_made")
        block = ctx.enter_context(nc.Block())

        def slots(eng, slot):
            slot(-3, 0, -3, "N")
            slot(-2, 0, -2, "NA")
            slot(-1, 0, -1, "NAB")
            with eng.Fori(0, DEPTH - 1) as l:
                for g in range(GROUPS):
                    slot(GROUPS * l + g, l, g, "NABM")
            for g in range(GROUPS):
                slot(GROUPS * (DEPTH - 1) + g, DEPTH - 1, g, "NABM"[max(0, g + 4 - GROUPS):])

        def carry(eng):
            eng.sem_inc(waited, 1)

        def at(l, g, ahead):
            return l + (g + ahead) // GROUPS, (g + ahead) % GROUPS

        def of(l):
            return bass.ds(l, 1)

        def rows(g):
            return hT[:, 2 * g:2 * g + 2, :]

        @block.sync
        def _(sp):
            with sp.Fori(0, DEPTH - 1) as l:
                for g in range(GROUPS):
                    n = GROUPS * l + g
                    sp.wait_ge(lo_made, free(n))
                    sp.dma_start(wf_raw[:, g % RING], experts[:, bass.ds(n * WF_PIECE, WF_PIECE)]).then_inc(piece_in[g % RING], 16)
                sp.wait_ge(m_done, FC * GROUPS * l + (FC * GROUPS + FC))
                sp.dma_start(w1[:], w1_t[bass.ds(l + 1, 1)].rearrange("o p f -> (o p) f")).then_inc(w1_in, 16)
                sp.wait_ge(o_done, GROUPS * l + (GROUPS + 1))
                sp.dma_start(w2[:], w2_t[bass.ds(l + 1, 1)].rearrange("o p c f -> (o p) c f")).then_inc(w2_in, 16)

        @block.gpsimd
        def _(pool):
            for k in range(2):
                pool.sem_inc(rstd_made[k], 1)
            pool.sem_inc(u_im_made, 1)
            pool.sem_inc(c_im_made, 1)
            pool.sem_inc(lo_made, RING)

            def rstd_of(k, u):
                pool.wait_ge(summed[k], made(u, 1))
                carry(pool)
                pool.tensor_scalar(ve[k][:], ss[k][:], 1.0 / DIM, EPS, ALU.mult, ALU.add).then_inc(ve_made[k], 1)
                pool.wait_ge(ve_made[k], u + 1)
                pool.wait_ge(xn_made[k], free(u))
                pool.tensor_tensor(rstd[k][:], ve[k][:], minus_half[:], ALU.pow).then_inc(rstd_made[k], 1)

            def slot(i, l, g, stages):
                if "A" in stages:
                    u = i + 2
                    la, _ = at(l, g, 2)
                    pool.wait_ge(y_made, made(u, 1))
                    pool.wait_ge(z_im_made, 2 * free(u))
                    carry(pool)
                    pool.tensor_tensor(u_im[:], y[:], rot[:, 1, of(la)].to_broadcast([P, 2, SEQ]), ALU.mult).then_inc(u_im_made, 1)
                if "N" in stages:
                    rstd_of(0, i + 3)
                if "A" in stages:
                    pool.wait_ge(z_im_made, 2 * made(u, 1))
                    pool.wait_ge(h1_made, free(u))
                    carry(pool)
                    pool.tensor_tensor(c_im[:], z_im[:], rot_scaled[:, 1, of(la)].to_broadcast([P, 2, SEQ]), ALU.mult).then_inc(c_im_made, 1)
                if "B" in stages:
                    rstd_of(1, i + 1)
                if "M" in stages and not isinstance(l, int):
                    pool.wait_ge(hi_made, i + 1)
                    carry(pool)
                    pool.tensor_tensor(wf[:, 1, bass.ds(i * WF_PIECE, WF_PIECE)], wf_raw[:, g % RING],
                                       wf[:, 0, bass.ds(i * WF_PIECE, WF_PIECE)].bitcast(F32), ALU.subtract).then_inc(lo_made, 1)

            slots(pool, slot)

        @block.vector
        def _(dve):
            for k in range(2):
                dve.sem_inc(summed[k], 1)
                dve.sem_inc(xn_made[k], 1)
            dve.sem_inc(u_re_made, 1)
            dve.sem_inc(z_im_made, 2)
            dve.sem_inc(h1_made, 1)
            dve.sem_inc(res_made, GROUPS)

            def sum_squares(k, u):
                dve.wait_ge(squared[k], made(u, 1))
                dve.wait_ge(rstd_made[k], free(u))
                dve.tensor_reduce(ss[k][:], sq[k][:], AX.X, ALU.add).then_inc(summed[k], 1)

            def normalize(k, u):
                dve.wait_ge(rstd_made[k], made(u, 1))
                dve.wait_ge(turned[k], free(u))
                dve.tensor_tensor(xn[k][:], c_ps[k][:], rstd[k][:].unsqueeze(2).to_broadcast([P, 4, P]), ALU.mult).then_inc(xn_made[k], 1)

            def scans(u, dst, src, part, la, done):
                for n in range(2):
                    dve.tensor_tensor_scan(dst[:, n], rate[:, of(la)].to_broadcast([P, SEQ]), src[:, n],
                                           state0[:, part, of(la)], ALU.mult, ALU.add).then_inc(done, 1)

            def slot(i, l, g, stages):
                if "A" in stages:
                    u = i + 2
                    la, ga = at(l, g, 2)
                    dve.wait_ge(y_made, made(u, 1))
                    dve.tensor_tensor(u_re[:], y[:], rot[:, 0, of(la)].to_broadcast([P, 2, SEQ]), ALU.mult).then_inc(u_re_made, 1)
                    dve.wait_ge(u_re_made, made(u, 1))
                    scans(u, z_re, u_re, 0, la, z_re_made)
                if "N" in stages:
                    sum_squares(0, i + 3)
                if "A" in stages:
                    dve.wait_ge(u_im_made, made(u, 1))
                    dve.wait_ge(c_im_made, free(u))
                    scans(u, z_im, u_im, 1, la, z_im_made)
                    dve.wait_ge(z_re_made, 2 * u + 2)
                    dve.tensor_tensor(c_re[:], z_re[:], rot_scaled[:, 0, of(la)].to_broadcast([P, 2, SEQ]), ALU.mult).then_inc(c_re_made, 1)
                    dve.wait_ge(c_re_made, u + 1)
                    dve.tensor_tensor(h_mid[:], rows(ga), c_re[:], ALU.add).then_inc(h_mid_made, 1)
                if "B" in stages:
                    sum_squares(1, i + 1)
                if "A" in stages:
                    dve.wait_ge(h_mid_made, u + 1)
                    dve.wait_ge(c_im_made, made(u, 1))
                    dve.tensor_tensor(rows(ga), h_mid[:], c_im[:], ALU.add).then_inc(h1_made, 1)
                if "N" in stages:
                    normalize(0, i + 3)
                if "B" in stages:
                    normalize(1, i + 1)
                if "M" in stages:
                    dve.wait_ge(o_done, made(i, 1))
                    flat = rows(g).rearrange("p n t -> p (n t)")
                    dve.scalar_tensor_tensor(flat, o_ps[:], vec[:, of(l), B2], flat, ALU.add, ALU.add).then_inc(res_made, 1)

            slots(dve, slot)

        @block.scalar
        def _(act):
            for k in range(2):
                act.sem_inc(squared[k], 1)
            act.sem_inc(y_made, 1)
            act.sem_inc(y2_made, 1)
            act.sem_inc(s_made, 2)

            def square(k, u):
                act.wait_ge(centered[k], made(u, 1))
                act.wait_ge(summed[k], free(u))
                act.activation(sq[k][:], c_ps[k][:], ACT.Square).then_inc(squared[k], 1)

            def hidden(i, l, j):
                act.wait_ge(m_done, FC * i + (j + 1 + FC))
                act.wait_ge(o_done, free(i))
                carry(act)
                act.activation(s[:, j], m_ps[j % 3][:], ACT.Silu, bias=b1_sb[:, of(l), j]).then_inc(s_made, 1)

            def slot(i, l, g, stages):
                if "A" in stages:
                    u = i + 2
                    la, _ = at(l, g, 2)
                    act.wait_ge(turned[0], made(u, 1))
                    act.wait_ge(u_re_made, free(u))
                    act.wait_ge(u_im_made, free(u))
                    carry(act)
                    act.activation(y[:].rearrange("p n t -> p (n t)"), t_ps[0][:], ACT.Silu, bias=vec[:, of(la), LN1_B],
                                   scale=vec[:, of(la), LN1_W]).then_inc(y_made, 1)
                if "N" in stages:
                    square(0, i + 3)
                if "M" in stages:
                    hidden(i, l, 0)
                    hidden(i, l, 1)
                    if not isinstance(l, int):
                        act.wait_ge(piece_in[g % RING], 16 * (GROUPS // RING) * l + 16 * (g // RING + 1))
                        carry(act)
                        act.activation(wf[:, 0, bass.ds(i * WF_PIECE, WF_PIECE)], wf_raw[:, g % RING], ACT.Copy).then_inc(hi_made, 1)
                    hidden(i, l, 2)
                if "B" in stages:
                    square(1, i + 1)
                if "M" in stages:
                    hidden(i, l, 3)
                if "B" in stages:
                    u = i + 1
                    lb, _ = at(l, g, 1)
                    act.wait_ge(turned[1], made(u, 1))
                    act.wait_ge(m_done, FC * free(u))
                    carry(act)
                    act.activation(y2[:], t_ps[1][:], ACT.Identity, bias=vec[:, of(lb), LN2_B],
                                   scale=vec[:, of(lb), LN2_W]).then_inc(y2_made, 1)

            slots(act, slot)

        @block.tensor
        def _(pe):
            for k in range(2):
                pe.sem_inc(centered[k], 1)
                pe.sem_inc(turned[k], 1)
            pe.sem_inc(m_done, FC)
            pe.sem_inc(o_done, 1)
            pe.sem_inc(w1_in, 16)
            pe.sem_inc(w2_in, 16)

            def center_rows(k, u, g):
                if k == 0:
                    pe.wait_ge(res_made, free(u))
                else:
                    pe.wait_ge(h1_made, made(u, 1))
                pe.wait_ge(xn_made[k], free(u))
                flat = rows(g).rearrange("p n t -> p (n t)")
                for c in range(4):
                    mm = pe.matmul(c_ps[k][:, c], flat[:, c * P:(c + 1) * P], center[:], start=True, stop=True)
                mm.then_inc(centered[k], 1)

            def turn_rows(k, u):
                pe.wait_ge(xn_made[k], made(u, 1))
                pe.wait_ge((y_made, y2_made)[k], free(u))
                for c in range(4):
                    mm = pe.transpose(t_ps[k][:, c * P:(c + 1) * P], xn[k][:, c], ident[:])
                mm.then_inc(turned[k], 1)

            def first(i, j):
                if j == 0:
                    pe.wait_ge(y2_made, made(i, 1))
                if j == 0:
                    pe.wait_ge(s_made, FC * i + 2)
                if j == 3:
                    pe.wait_ge(s_made, FC * i + 3)
                pe.matmul(m_ps[j % 3][:], w1[:, j * P:(j + 1) * P], y2[:], start=True, stop=True).then_inc(m_done, 1)

            def second(i, g, k):
                if k == 0:
                    pe.wait_ge(res_made, i + GROUPS)
                pe.wait_ge(s_made, FC * i + (k + 3))
                mm = pe.matmul(o_ps[:], w2[:, k], s[:, k], start=(k == 0), stop=(k == FC - 1))
                if k == FC - 1:
                    mm.then_inc(o_done, 1)

            def slot(i, l, g, stages):
                if "A" in stages:
                    turn_rows(0, i + 2)
                if "N" in stages:
                    center_rows(0, i + 3, at(l, g, 3)[1])
                if "M" in stages:
                    if g == 0:
                        pe.wait_ge(w1_in, 16 * l + 16)
                    for j in range(3):
                        first(i, j)
                if "B" in stages:
                    center_rows(1, i + 1, at(l, g, 1)[1])
                if "M" in stages:
                    first(i, 3)
                    if g == 0:
                        pe.wait_ge(w2_in, 16 * l + 16)
                    for k in range(FC):
                        second(i, g, k)
                if "B" in stages:
                    turn_rows(1, i + 1)

            slots(pe, slot)


def experts_stage(nc, sb, psum, sem, txt, row_bias, tok_rows, hT, ident, minus_half, vec, wf, out):
    with ExitStack() as ctx:
        def buf(name, shape, dt=F32):
            return sb(ctx, name, shape, dt)

        ER = EXPERTS * RANK
        mixed = buf("mixed", [P, RING, P])
        row = buf("row", [P, RING, VOC])
        bias = buf("bias", [P, 2, VOC])
        f_stats = buf("f_stats", [P, 6])
        f_mv = buf("f_mv", [P, 2])
        f_ve = buf("f_ve", [P, 1])
        f_rstd = buf("f_rstd", [P, 1])
        zn = buf("zn", [P, P])
        z = buf("z", [P, P])
        z_hi = buf("z_hi", [P, P], F32R)
        z_lo = buf("z_lo", [P, P], F32R)
        row_b = buf("row_b", [P, VOC])
        h2 = buf("h2", [P, VOC])
        h2_b = buf("h2_b", [P, RING, VOC])
        r_stats = buf("r_stats", [P, 2, 6])
        r_mv = buf("r_mv", [P, 2])
        r_ve = buf("r_ve", [P, 1])
        r_rstd = buf("r_rstd", [P, 1])
        xhat = buf("x2hat", [P, VOC])
        x_hi = buf("x_hi", [P, RING, VOC], F32R)
        x_lo = buf("x_lo", [P, RING, VOC], F32R)
        top = buf("top", [P, EXPERTS])
        top_at = buf("top_at", [P, EXPERTS], U32)
        top_at_f = buf("top_at_f", [P, 2])
        gap = buf("gap", [P, 1])
        ratio = buf("ratio", [P, 1])
        total = buf("total", [P, 1])
        share = buf("share", [P, 2])
        picked = buf("picked", [P, 2, EXPERTS])
        weight = buf("weight", [P, EXPERTS])
        number = buf("number", [P, EXPERTS])
        ag = buf("ag", [P, AG])
        low = buf("low", [P, ER])
        low_hi = buf("low_hi", [P, P], F32R)
        low_lo = buf("low_lo", [P, P], F32R)
        result = buf("result", [P, RING, VOC])

        f_ps = psum(ctx, "f_ps", [P, 4, P])
        ag_bank = psum(ctx, "ag_bank", [P, 512])
        ag_ps = ag_bank[:, 0:2 * AG].rearrange("p (k n) -> p k n", k=2)
        y_ps = psum(ctx, "y_ps", [P, VOC])
        x_ps = psum(ctx, "x_ps", [P, VOC])
        r_ps = psum(ctx, "r_ps", [P, VOC])

        mixed_turned = sem(ctx, "x_mixed_turned")
        f_counted = sem(ctx, "x_f_counted")
        f_aggregated = sem(ctx, "x_f_aggregated")
        f_ve_made = sem(ctx, "x_f_ve_made")
        f_rstd_made = sem(ctx, "x_f_rstd_made")
        zn_made = sem(ctx, "x_zn_made")
        zn_turned = sem(ctx, "x_zn_turned")
        z_made = sem(ctx, "x_z_made")
        z_hi_made = sem(ctx, "x_z_hi_made")
        z_lo_made = sem(ctx, "x_z_lo_made")
        row_b_made = sem(ctx, "x_row_b_made")
        y_done = sem(ctx, "x_y_done")
        h2_made = sem(ctx, "x_h2_made")
        h2_b_made = sem(ctx, "x_h2_b_made")
        r_counted = sem(ctx, "x_r_counted")
        r_aggregated = sem(ctx, "x_r_aggregated")
        r_ve_made = sem(ctx, "x_r_ve_made")
        r_rstd_made = sem(ctx, "x_r_rstd_made")
        xhat_made = sem(ctx, "x_xhat_made")
        x_turned = sem(ctx, "x_x_turned")
        x_hi_made = sem(ctx, "x_x_hi_made")
        x_lo_made = sem(ctx, "x_x_lo_made")
        ag_done = sem(ctx, "x_ag_done")
        ag_base_done = sem(ctx, "x_ag_base_done")
        weight_made = sem(ctx, "x_weight_made")
        ag_half_made = sem(ctx, "x_ag_half_made")
        ag_added = sem(ctx, "x_ag_added")
        gate_steps = sem(ctx, "x_gate_steps")
        ratio_made = sem(ctx, "x_ratio_made")
        low_made = sem(ctx, "x_low_made")
        low_turned = sem(ctx, "x_low_turned")
        low_hi_made = sem(ctx, "x_low_hi_made")
        low_lo_made = sem(ctx, "x_low_lo_made")
        r_done = sem(ctx, "x_r_done")
        result_made = sem(ctx, "x_result_made")
        x_constants = sem(ctx, "x_x_constants")
        x_waited = sem(ctx, "x_x_waited")
        bias_in = sem(ctx, "x_bias_in")
        mixed_in = [sem(ctx, f"mixed_in{r}") for r in range(RING)]
        row_in = [sem(ctx, f"row_in{r}") for r in range(RING)]
        stored = [sem(ctx, f"stored{r}") for r in range(RING)]
        block = ctx.enter_context(nc.Block())
        TILES = 2 * BATCH
        GATE_STEPS = 10

        def slots(eng, slot):
            with eng.Fori(0, BATCH - 1) as c:
                for p in range(RING):
                    slot(2 * c + p, p, c, 2)
            slot(TILES - 2, 0, BATCH - 1, 1)
            slot(TILES - 1, 1, BATCH - 1, 0)

        def carry(eng):
            eng.sem_inc(x_waited, 1)

        @block.sync
        def _(sp):
            def load(t, p, c):
                sp.wait_ge(mixed_turned, free(t))
                sp.dma_start(mixed[:, p], hT[:, bass.ds(c, 1), p * P:(p + 1) * P].rearrange("d o t -> d (o t)")).then_inc(mixed_in[p], 16)
                sp.wait_ge(row_b_made, free(t))
                src = tok_rows[:, bass.ds(c, 1)] if p == 0 else txt[bass.ds(c, 1)].rearrange("o s v -> s o v")
                sp.dma_start(row[:, p], src.rearrange("s o v -> s (o v)")).then_inc(row_in[p], 16)

            def store(t, p, c):
                sp.wait_ge(result_made, made(t))
                sp.dma_start(out[bass.ds(c, 1), p * P:(p + 1) * P].rearrange("o s v -> (o s) v"), result[:, p]).then_inc(stored[p], 16)

            for k in range(2):
                sp.dma_start(bias[:, k], row_bias[k:k + 1].to_broadcast([P, VOC])).then_inc(bias_in, 16)
            for p in range(RING):
                load(p, p, 0)
            with sp.Fori(0, BATCH - 1) as c:
                for p in range(RING):
                    load(2 * c + (p + 2), p, c + 1)
                    store(2 * c + p, p, c)
            for p in range(RING):
                store(TILES - 2 + p, p, BATCH - 1)
            for p in range(RING):
                sp.wait_ge(stored[p], 16 * (BATCH + 1))

        @block.gpsimd
        def _(pool):
            pool.iota(number[:], pattern=[[1, EXPERTS]], base=0, channel_multiplier=0,
                      allow_small_or_imprecise_dtypes=True).then_inc(x_constants, 1)
            pool.sem_inc(row_b_made, RING)
            pool.sem_inc(h2_b_made, RING)
            pool.sem_inc(f_rstd_made, 1)
            pool.sem_inc(r_rstd_made, 1)
            pool.wait_ge(bias_in, 32)

            def rstd_of(t, mv, ve, rstd, aggregated, ve_made, rstd_made, used):
                pool.wait_ge(aggregated, t + 1)
                pool.wait_ge(used, free(t))
                carry(pool)
                pool.tensor_scalar(ve[:], mv[:, 1:2], EPS, None, ALU.add).then_inc(ve_made, 1)
                pool.wait_ge(ve_made, t + 1)
                pool.tensor_tensor(rstd[:], ve[:], minus_half[:, 0:1], ALU.pow).then_inc(rstd_made, 1)

            def mixed_part(t, p, c):
                pool.wait_ge(row_in[p], 16 * (c + 1))
                pool.wait_ge(h2_made, free(t))
                pool.tensor_tensor(row_b[:], row[:, p], bias[:, 0], ALU.add).then_inc(row_b_made, 1)
                rstd_of(t, f_mv, f_ve, f_rstd, f_aggregated, f_ve_made, f_rstd_made, zn_made)

            def row_part(t, p):
                rstd_of(t, r_mv, r_ve, r_rstd, r_aggregated, r_ve_made, r_rstd_made, xhat_made)
                pool.wait_ge(h2_made, made(t, 1))
                pool.wait_ge(result_made, free(t))
                pool.tensor_tensor(h2_b[:, p], h2[:], bias[:, 1], ALU.add).then_inc(h2_b_made, 1)

            def slot(t, p, c, after):
                if after > 0:
                    row_part(t + 1, 1 - p)
                if after > 1:
                    mixed_part(t + 2, p, c + 1)

            mixed_part(0, 0, 0)
            row_part(0, 0)
            mixed_part(1, 1, 0)
            slots(pool, slot)

        @block.vector
        def _(dve):
            for n in (zn_made, z_lo_made, h2_made, xhat_made, ag_added, low_made, low_lo_made):
                dve.sem_inc(n, 1)
            dve.sem_inc(x_lo_made, RING)
            dve.sem_inc(result_made, RING)
            dve.wait_ge(x_constants, 1)

            def gate_pick(t):
                g = t * GATE_STEPS
                dve.wait_ge(ag_done, made(t, 1))
                dve.wait_ge(low_made, free(t))
                dve.tensor_copy(ag[:], ag_ps[:, 1]).then_inc(ag_half_made, 1)
                dve.wait_ge(ag_half_made, t + 1)
                dve.tensor_tensor(ag[:], ag_ps[:, 0], ag[:], ALU.add).then_inc(ag_added, 1)
                dve.wait_ge(ag_added, made(t, 1))
                carry(dve)
                dve.max(top[:], ag[:, ER:AG]).then_inc(gate_steps, 1)
                dve.wait_ge(gate_steps, g + 1)
                dve.tensor_tensor(gap[:], top[:, 1:2], top[:, 0:1], ALU.subtract).then_inc(gate_steps, 1)
                dve.max_index(top_at[:], top[:], ag[:, ER:AG]).then_inc(gate_steps, 1)
                dve.wait_ge(gate_steps, g + 3)
                dve.tensor_copy(top_at_f[:], top_at[:, 0:2]).then_inc(gate_steps, 1)
                dve.wait_ge(gate_steps, g + 4)
                for k in range(2):
                    dve.tensor_scalar(picked[:, k], number[:], top_at_f[:, k:k + 1], None, ALU.is_equal).then_inc(gate_steps, 1)

            def gate_weigh(t):
                g = t * GATE_STEPS
                dve.wait_ge(ratio_made, t + 1)
                dve.tensor_scalar(total[:], ratio[:], 0.5, 0.5, ALU.mult, ALU.add).then_inc(gate_steps, 1)
                dve.wait_ge(gate_steps, g + 7)
                dve.reciprocal(share[:, 0:1], total[:]).then_inc(gate_steps, 1)
                dve.wait_ge(gate_steps, g + 8)
                dve.tensor_tensor(share[:, 1:2], share[:, 0:1], ratio[:], ALU.mult).then_inc(gate_steps, 1)
                dve.wait_ge(gate_steps, g + 9)
                dve.tensor_scalar(weight[:], picked[:, 0], share[:, 0:1], None, ALU.mult).then_inc(gate_steps, 1)

            def low_rank(t):
                g = t * GATE_STEPS
                dve.wait_ge(gate_steps, g + 10)
                dve.scalar_tensor_tensor(weight[:], picked[:, 1], share[:, 1:2], weight[:], ALU.mult, ALU.add).then_inc(weight_made, 1)
                dve.wait_ge(weight_made, t + 1)
                dve.wait_ge(low_turned, t + 1)
                dve.tensor_tensor(low[:].rearrange("p (e r) -> p e r", e=EXPERTS), ag[:, 0:ER].rearrange("p (e r) -> p e r", e=EXPERTS),
                                  weight[:].unsqueeze(2).to_broadcast([P, EXPERTS, RANK]), ALU.mult).then_inc(low_made, 1)

            def finish(t, p):
                dve.wait_ge(r_done, made(t, 1))
                dve.wait_ge(stored[p], 8 * t + (16 - 8 * p))
                dve.wait_ge(h2_b_made, made(t))
                dve.tensor_tensor(result[:, p], r_ps[:], h2_b[:, p], ALU.add).then_inc(result_made, 1)

            def mixed_stats(t):
                dve.wait_ge(mixed_turned, made(t))
                dve.bn_stats(f_stats[:], f_ps[:, 0]).then_inc(f_counted, 1)
                dve.wait_ge(f_counted, t + 1)
                dve.wait_ge(f_rstd_made, free(t))
                carry(dve)
                dve.bn_aggr(f_mv[:], f_stats[:]).then_inc(f_aggregated, 1)

            def mixed_normal(t):
                dve.wait_ge(f_rstd_made, made(t, 1))
                dve.wait_ge(zn_turned, free(t))
                dve.tensor_scalar(zn[:], f_ps[:, 0], f_mv[:, 0:1], f_rstd[:], ALU.subtract, ALU.mult).then_inc(zn_made, 1)

            def mixed_low(t):
                dve.wait_ge(z_hi_made, t + 1)
                dve.wait_ge(y_done, free(t))
                dve.tensor_tensor(z_lo[:], z[:], z_hi[:].bitcast(F32), ALU.subtract).then_inc(z_lo_made, 1)

            def residual(t):
                dve.wait_ge(y_done, made(t, 1))
                dve.wait_ge(row_b_made, made(t))
                dve.wait_ge(h2_b_made, t + RING)
                dve.tensor_tensor(h2[:], y_ps[:], row_b[:], ALU.add).then_inc(h2_made, 1)
                dve.wait_ge(h2_made, made(t, 1))
                for k in range(2):
                    dve.bn_stats(r_stats[:, k], h2[:, k * 512:(k + 1) * 512]).then_inc(r_counted, 1)
                dve.wait_ge(r_counted, 2 * t + 2)
                dve.wait_ge(r_rstd_made, free(t))
                carry(dve)
                dve.bn_aggr(r_mv[:], r_stats[:].rearrange("p a b -> p (a b)")).then_inc(r_aggregated, 1)

            def row_normal(t):
                dve.wait_ge(r_rstd_made, made(t, 1))
                dve.wait_ge(x_turned, free(t))
                dve.tensor_scalar(xhat[:], h2[:], r_mv[:, 0:1], r_rstd[:], ALU.subtract, ALU.mult).then_inc(xhat_made, 1)

            def row_low(t, p):
                dve.wait_ge(x_hi_made, made(t))
                dve.tensor_tensor(x_lo[:, p], x_ps[:], x_hi[:, p].bitcast(F32), ALU.subtract).then_inc(x_lo_made, 1)

            def low_low(t):
                dve.wait_ge(low_hi_made, t + 1)
                dve.tensor_tensor(low_lo[:], f_ps[:, 2], low_hi[:].bitcast(F32), ALU.subtract).then_inc(low_lo_made, 1)

            def slot(t, p, c, after):
                if after > 0:
                    mixed_normal(t + 1)
                gate_pick(t)
                if after > 0:
                    mixed_low(t + 1)
                gate_weigh(t)
                low_rank(t)
                if after > 0:
                    residual(t + 1)
                low_low(t)
                if after > 0:
                    row_normal(t + 1)
                    row_low(t + 1, 1 - p)
                if after > 1:
                    mixed_stats(t + 2)
                finish(t, p)

            mixed_stats(0)
            mixed_normal(0)
            mixed_low(0)
            residual(0)
            row_normal(0)
            row_low(0, 0)
            mixed_stats(1)
            slots(dve, slot)

        @block.scalar
        def _(act):
            act.sem_inc(z_made, 1)
            act.sem_inc(x_hi_made, RING)
            for p in range(RING):
                act.sem_inc(stored[p], 16)

            def ahead_z(t):
                act.wait_ge(zn_turned, made(t, 1))
                act.wait_ge(z_lo_made, free(t))
                act.activation(z[:], f_ps[:, 1], ACT.Identity, bias=vec[:, 0, LNL_B:LNL_B + 1],
                               scale=vec[:, 0, LNL_W:LNL_W + 1]).then_inc(z_made, 1)
                act.wait_ge(z_made, made(t, 1))
                act.wait_ge(y_done, free(t))
                act.activation(z_hi[:], z[:], ACT.Copy).then_inc(z_hi_made, 1)

            def ahead_x(t, p):
                act.wait_ge(x_turned, made(t, 1))
                act.wait_ge(ag_base_done, free(t))
                act.activation(x_hi[:, p], x_ps[:], ACT.Copy).then_inc(x_hi_made, 1)

            def slot(t, p, c, after):
                if after > 0:
                    ahead_z(t + 1)
                act.wait_ge(gate_steps, t * GATE_STEPS + 2)
                act.activation(ratio[:], gap[:], ACT.Exp).then_inc(ratio_made, 1)
                act.wait_ge(low_turned, made(t, 1))
                act.wait_ge(r_done, free(t))
                act.activation(low_hi[:], f_ps[:, 2], ACT.Copy).then_inc(low_hi_made, 1)
                if after > 0:
                    ahead_x(t + 1, 1 - p)

            ahead_z(0)
            ahead_x(0, 0)
            slots(act, slot)

        @block.tensor
        def _(pe):
            pe.sem_inc(mixed_turned, RING)
            for n in (zn_turned, y_done, x_turned, ag_done, low_turned, r_done):
                pe.sem_inc(n, 1)
            pe.sem_inc(ag_base_done, RING)

            def turn_mixed(t, p, c):
                pe.wait_ge(mixed_in[p], 16 * (c + 1))
                pe.wait_ge(zn_made, free(t))
                pe.wait_ge(z_made, free(t))
                pe.transpose(f_ps[:, 0], mixed[:, p], ident[:]).then_inc(mixed_turned, 1)

            def turn_zn(t):
                pe.wait_ge(zn_made, made(t, 1))
                pe.transpose(f_ps[:, 1], zn[:], ident[:]).then_inc(zn_turned, 1)

            def wide(dst, x_hi_c, x_lo_c, at, start, stop):
                for k, (x, lo) in enumerate(((x_hi_c, False), (x_hi_c, True), (x_lo_c, False))):
                    for n in range(VOC // 512):
                        w = wf[:, int(lo), at + n * 512:at + (n + 1) * 512]
                        mm = pe.matmul(dst[:, n * 512:(n + 1) * 512], x, w, start=(start and k == 0), stop=(stop and k == 2))
                return mm

            def output(t):
                pe.wait_ge(z_lo_made, made(t, 1))
                pe.wait_ge(h2_made, free(t))
                wide(y_ps, z_hi[:], z_lo[:], WF_OUT, True, True).then_inc(y_done, 1)

            def turn_rows(t):
                pe.wait_ge(xhat_made, made(t, 1))
                pe.wait_ge(x_lo_made, t + RING)
                for c in range(KC):
                    mm = pe.transpose(x_ps[:, c * P:(c + 1) * P], xhat[:, c * P:(c + 1) * P], ident[:])
                mm.then_inc(x_turned, 1)

            def low_and_gate(t, p):
                pe.wait_ge(x_lo_made, made(t))
                pe.wait_ge(ag_added, free(t))
                for c in range(KC):
                    cs = slice(c * P, (c + 1) * P)
                    w = wf[:, :, WF_AG + c * AG:WF_AG + (c + 1) * AG]
                    if c == 0:
                        pe.matmul(ag_ps, x_hi[:, p, cs], w, start=True, stop=False)
                    pe.matmul(ag_ps[:, 0], x_lo[:, p, cs], w[:, 0], start=False, stop=False)
                    if c > 0:
                        mm = pe.matmul(ag_ps, x_hi[:, p, cs], w, start=False, stop=c == KC - 1)
                mm.then_inc(ag_done, 1)

            def base(t, p, chunks):
                if chunks[0] == 0:
                    pe.wait_ge(result_made, t + RING)
                for c in chunks:
                    cs = slice(c * P, (c + 1) * P)
                    mm = wide(r_ps, x_hi[:, p, cs], x_lo[:, p, cs], WF_BASE + c * VOC, c == 0, False)
                    if c == KC - 1:
                        mm.then_inc(ag_base_done, 1)

            def turn_low(t, after):
                if after:
                    pe.wait_ge(z_made, made(t + 1, 1))
                pe.wait_ge(low_made, made(t, 1))
                pe.wait_ge(low_lo_made, free(t))
                pe.transpose(f_ps[:, 2], low[:], ident[:]).then_inc(low_turned, 1)

            def low_output(t):
                pe.wait_ge(low_lo_made, made(t, 1))
                wide(r_ps, low_hi[:], low_lo[:], WF_B, False, True).then_inc(r_done, 1)

            def slot(t, p, c, after):
                low_and_gate(t, p)
                if after > 0:
                    turn_zn(t + 1)
                base(t, p, [0, 1])
                if after > 0:
                    output(t + 1)
                base(t, p, [2])
                turn_low(t, after > 0)
                base(t, p, [3, 4, 5])
                if after > 0:
                    turn_rows(t + 1)
                base(t, p, [6, 7])
                if after > 1:
                    pe.wait_ge(low_lo_made, made(t, 1))
                    turn_mixed(t + 2, p, c + 1)
                low_output(t)

            turn_mixed(0, 0, 0)
            turn_zn(0)
            output(0)
            turn_rows(0)
            turn_mixed(1, 1, 0)
            slots(pe, slot)


def kernel(x, txt, L0_tok_log_dt, L0_tok_B, L0_tok_inv_A_real, L0_tok_A_imag, L0_attn_Win, L0_attn_bin,
           L0_attn_ln1_w, L0_attn_ln1_b, L0_attn_phz_re, L0_attn_phz_im, L0_attn_lc_re, L0_attn_lc_im,
           L0_attn_sc_lin, L0_attn_ln2_w, L0_attn_ln2_b, L0_attn_W1, L0_attn_b1, L0_attn_W2, L0_attn_b2,
           L0_attn_lnl_w, L0_attn_lnl_b, L0_attn_Wout, L0_attn_bout, L0_ffn_gate_w, L0_ffn_base_w,
           L0_ffn_base_b, L0_ffn_lora_A, L0_ffn_lora_B):
    import concourse.bacc as bacc
    from concourse.bass_utils import run_bass_kernel_spmd

    arr = np.asarray
    per_layer = [L0_attn_ln1_w, L0_attn_ln1_b, L0_attn_phz_re, L0_attn_phz_im, L0_attn_lc_re, L0_attn_lc_im,
                 L0_attn_sc_lin, L0_attn_ln2_w, L0_attn_ln2_b, L0_attn_b2]
    once = [np.broadcast_to(arr(v), (DEPTH, DIM)) for v in (L0_attn_lnl_w, L0_attn_lnl_b)]

    def chunked(w):
        w = arr(w)
        return w.reshape(-1, P, w.shape[-1]).transpose(1, 0, 2)

    low_rank = np.concatenate([arr(L0_ffn_lora_A).reshape(EXPERTS * RANK, VOC), arr(L0_ffn_gate_w)], axis=0)
    laid_out = {
        "log_dt": arr(L0_tok_log_dt).reshape(1, TOK),
        "tok_a": np.stack([arr(L0_tok_inv_A_real).T, arr(L0_tok_A_imag).T, arr(L0_tok_B)[..., 0].T,
                           arr(L0_tok_B)[..., 1].T], axis=1),
        "tok_c": arr(x).transpose(3, 2, 1, 0),
        "txt": arr(txt),
        "win_t": chunked(arr(L0_attn_Win).T),
        "bin_": arr(L0_attn_bin).reshape(DIM, 1),
        "vecs": np.stack([arr(v) for v in per_layer] + once).transpose(2, 1, 0),
        "b1": arr(L0_attn_b1).reshape(DEPTH, FC, P).transpose(2, 0, 1),
        "w1_t": arr(L0_attn_W1).transpose(0, 2, 1),
        "w2_t": np.stack([chunked(w.T) for w in arr(L0_attn_W2)]),
        "experts": np.concatenate([chunked(w).reshape(P, -1) for w in (
            arr(L0_ffn_base_w).T, low_rank.T, arr(L0_attn_Wout).T,
            arr(L0_ffn_lora_B).transpose(0, 2, 1).reshape(EXPERTS * RANK, VOC))], axis=1),
        "row_bias": np.stack([arr(L0_attn_bout), arr(L0_ffn_base_b)]),
    }
    nc = bacc.Bacc("TRN2", target_bir_lowering=False, num_devices=1)
    arrays, args = {}, []
    for name, a in laid_out.items():
        arrays["in_" + name] = np.ascontiguousarray(a)
        args.append(nc.dram_tensor("in_" + name, a.shape, mybir.dt.from_np(a.dtype), kind="ExternalInput").ap())
    args.append(nc.dram_tensor("out", (BATCH, SEQ, VOC), F32, kind="ExternalOutput").ap())
    build(nc, *args)
    return run_bass_kernel_spmd(nc, [arrays], core_ids=[0]).results[0]["out"]
```

```python
from contextlib import ExitStack

import numpy as np

import concourse.bass as bass
from concourse import mybir

F32 = mybir.dt.float32
F32R = mybir.dt.float32r
U32 = mybir.dt.uint32
ALU = mybir.AluOpType
ACT = mybir.ActivationFunctionType
AX = mybir.AxisListType

P = 128
BATCH = 16
SEQ = 256
TOK = 128
VOC = 1024
KC = VOC // P
STATES = 64
DIM = 128
DFF = 512
FC = DFF // P
DEPTH = 4
EXPERTS = 8
RANK = 16
EPS = 1e-5

NA, NB1, NB0 = 8, 8, 16
NJ = NA + NB1 + NB0
H_CHUNK = 32
H_BLOCK = 8
N_CHUNK = TOK // H_CHUNK
BLOCKS = H_CHUNK // H_BLOCK

TWO_PI = 2.0 * np.pi
INV_2PI = float(np.float32(1.0 / TWO_PI))
PI2_A = 6.28125
PI2_B = float(np.float32(round((TWO_PI - PI2_A) * 2**21) / 2**21))
PI2_C = float(np.float32(TWO_PI - PI2_A - PI2_B))
ROUND = 1.5 * 2**23
TURN = float(np.nextafter(np.float32(TWO_PI), np.float32(0)))
PI_IN = float(np.nextafter(np.float32(np.pi), np.float32(0)))

LN1_W, LN1_B, PHZ_RE, PHZ_IM, LC_RE, LC_IM, SC_LIN, LN2_W, LN2_B, B2, LNL_W, LNL_B = range(12)
N_VEC = 12
AG = EXPERTS * RANK + EXPERTS
WF_BASE, WF_AG = 0, KC * VOC
WF_OUT = WF_AG + KC * AG
WF_B = WF_OUT + VOC
N_WF = WF_B + VOC
GROUPS = BATCH // 2
UNIT = 2 * SEQ
WF_PIECE = N_WF // ((DEPTH - 1) * GROUPS)
assert WF_PIECE * (DEPTH - 1) * GROUPS == N_WF

LONG_RING = 4
RING = 2


def made(n, ring=RING):
    return n + (1 + ring)


def free(n):
    return n + 1


def build(nc, log_dt, tok_a, tok_c, txt, win_t, bin_, vecs, b1, w1_t, w2_t, experts, row_bias, out):
    with ExitStack() as whole:
        def sb(ctx, name, shape, dt=F32):
            return ctx.enter_context(nc.sbuf_tensor(name, shape, dt))

        def psum(ctx, name, shape, dt=F32):
            return ctx.enter_context(nc.psum_tensor(name, shape, dt))

        def sem(ctx, name):
            return ctx.enter_context(nc.semaphore(name))

        tok_rows = nc.dram_tensor("tok_rows", (TOK, BATCH, VOC), F32, kind="Internal").ap()

        hT = sb(whole, "hT", [P, BATCH, SEQ])
        ident = sb(whole, "ident", [P, P])
        center = sb(whole, "center", [P, P])
        minus_half = sb(whole, "minus_half", [P, 4])
        vec = sb(whole, "vec", [P, DEPTH, N_VEC])
        b1_sb = sb(whole, "b1_sb", [P, DEPTH, FC])
        w1 = sb(whole, "w1", [P, DFF])
        w2 = sb(whole, "w2", [P, FC, DIM])
        rot = sb(whole, "rot", [P, 2, DEPTH, SEQ])
        rot_scaled = sb(whole, "rot_scaled", [P, 2, DEPTH, SEQ])
        rate = sb(whole, "rate", [P, DEPTH])
        state0 = sb(whole, "state0", [P, 2, DEPTH])
        tokens_and_projection(nc, sb, psum, sem, log_dt, tok_a, tok_c, txt, win_t, bin_, vecs, b1, w1_t, w2_t,
                              tok_rows, hT, ident, center, minus_half, vec, b1_sb, w1, w2,
                              rot, rot_scaled, rate, state0)
        with ExitStack() as late:
            wf = sb(late, "wf", [P, 2, N_WF], F32R)
            mixer(nc, sb, psum, sem, w1_t, w2_t, experts, hT, ident, center, minus_half, vec, b1_sb, w1, w2,
                  rot, rot_scaled, rate, state0, wf)
            experts_stage(nc, sb, psum, sem, txt, row_bias, tok_rows, hT, ident, minus_half, vec, wf, out)


def tokens_and_projection(nc, sb, psum, sem, log_dt, tok_a, tok_c, txt, win_t, bin_, vecs, b1, w1_t, w2_t,
                          tok_rows, hT, ident, center, minus_half, vec, b1_sb, w1, w2,
                          rot, rot_scaled, rate, state0):
    with ExitStack() as ctx:
        ldt = sb(ctx, "ldt", [P, TOK])
        par = sb(ctx, "par", [P, 4, TOK])
        c_re = sb(ctx, "c_re", [P, TOK, BATCH])
        c_im = sb(ctx, "c_im", [P, TOK, BATCH])
        small = sb(ctx, "small", [P, 24, TOK])
        half = sb(ctx, "half", [P, DEPTH])
        ph = sb(ctx, "ph", [P, 5, DEPTH])
        eps = sb(ctx, "eps", [P, 1])
        half_pi = sb(ctx, "half_pi", [P, 1])
        warm = sb(ctx, "warm", [P, 1])
        alpha = sb(ctx, "alpha", [P, TOK])
        beta = sb(ctx, "beta", [P, TOK])
        powers = sb(ctx, "powers", [P, NJ])
        turns = sb(ctx, "turns", [P, H_CHUNK, NJ])
        whole_turns = sb(ctx, "whole_turns", [P, H_CHUNK, NJ])
        mag = sb(ctx, "decay", [P, H_CHUNK, NJ])
        sin = sb(ctx, "sin", [P, H_CHUNK, NJ])
        cos = sb(ctx, "cos", [P, H_CHUNK, NJ])
        w_re = sb(ctx, "w_re", [P, H_CHUNK, NA + NB1])
        w_im = sb(ctx, "w_im", [P, H_CHUNK, NA + NB1])
        n1 = sb(ctx, "n1", [P, H_CHUNK, NB0])
        n2 = sb(ctx, "n2", [P, H_CHUNK, NB0])
        pt = sb(ctx, "pt", [P, 4, H_CHUNK, NA])
        p1 = sb(ctx, "p1", [P, H_CHUNK, NA])
        p2 = sb(ctx, "p2", [P, H_CHUNK, NA])
        x1 = sb(ctx, "x1", [P, RING, H_BLOCK, BATCH, NA])
        x2 = sb(ctx, "x2", [P, RING, H_BLOCK, BATCH, NA])
        y1 = sb(ctx, "y1", [P, RING, H_BLOCK, NB1, NB0])
        y2 = sb(ctx, "y2", [P, RING, H_BLOCK, NB1, NB0])
        vv = sb(ctx, "vv", [P, RING, H_BLOCK, NB1 * NB0])
        rows_out = sb(ctx, "rows_out", [P, RING, H_BLOCK, P])
        wts = sb(ctx, "win_sb", [P, KC, DIM])
        bin_sb = sb(ctx, "bin_sb", [P, 1])
        raw = sb(ctx, "raw", [P, LONG_RING, VOC])
        stats = sb(ctx, "stats", [P, LONG_RING, 2, 6])
        mv = sb(ctx, "mv", [P, LONG_RING, 2])
        var_eps = sb(ctx, "var_eps", [P, LONG_RING])
        rstd = sb(ctx, "rstd", [P, LONG_RING])
        shift = sb(ctx, "shift", [P, LONG_RING])
        xhat = sb(ctx, "xhat", [P, RING, VOC])
        xT = sb(ctx, "xT", [P, RING, KC, P])

        k_ps = [[psum(ctx, f"k_ps{r}{k}", [P, 4, P]) for k in range(2)] for r in range(RING)]
        t_ps = [psum(ctx, f"t_ps{k}", [P, 4, P]) for k in range(2)]
        w_ps = [psum(ctx, f"w_ps{i}", [P, 512]) for i in range(RING)]

        vec_in = sem(ctx, "vec_in")
        ffn_in = sem(ctx, "ffn_in")
        first_rotations = sem(ctx, "first_rotations")
        rot_steps = sem(ctx, "rot_steps")
        pool_small = sem(ctx, "pool_small")
        par_in = sem(ctx, "par_in")
        c_in = sem(ctx, "c_in")
        win_in = sem(ctx, "win_in")
        consts = sem(ctx, "consts")
        act_small = sem(ctx, "act_small")
        dve_small = sem(ctx, "dve_small")
        turns_steps = sem(ctx, "turns_steps")
        coef_made = sem(ctx, "coef_made")
        abs_made = sem(ctx, "abs_made")
        decay_made = sem(ctx, "decay_made")
        mag_made = sem(ctx, "mag_made")
        sincos_made = sem(ctx, "sincos_made")
        dve_tables = sem(ctx, "dve_tables")
        pool_tables = sem(ctx, "pool_tables")
        x1_made = sem(ctx, "x1_made")
        x2_made = sem(ctx, "x2_made")
        y1_made = sem(ctx, "y1_made")
        y2_made = sem(ctx, "y2_made")
        vv_made = sem(ctx, "vv_made")
        k_done = sem(ctx, "k_done")
        k_moved = sem(ctx, "k_moved")
        rows_stored = [sem(ctx, f"rows_stored{i}") for i in range(RING)]
        raw_in = [sem(ctx, f"raw_in{i}") for i in range(LONG_RING)]
        stats_made = sem(ctx, "stats_made")
        waited = sem(ctx, "waited")
        mv_made = sem(ctx, "mv_made")
        ve_made = sem(ctx, "ve_made")
        rstd_made = sem(ctx, "rstd_made")
        shift_made = sem(ctx, "shift_made")
        xhat_made = sem(ctx, "xhat_made")
        xT_done = sem(ctx, "xT_done")
        xT_moved = sem(ctx, "xT_moved")
        win_done = sem(ctx, "win_done")
        win_moved = sem(ctx, "win_moved")
        block = ctx.enter_context(nc.Block())

        N_BLOCK = N_CHUNK * BLOCKS
        TILES = 2 * BATCH
        CONSTS = 9
        TURN_STEPS = 3
        DVE_TABLES = 8
        POOL_TABLES = 4

        def slots(eng, slot):
            def four(q, s4d, n=BLOCKS):
                for b in range(n):
                    slot(q, b, s4d)

            four(0, True)
            with eng.Fori(1, N_CHUNK - 1) as q:
                four(q, True)
            four(N_CHUNK - 1, True)
            four(N_CHUNK, False)
            with eng.Fori(N_CHUNK + 1, TILES // BLOCKS) as q:
                four(q, False)
            four(TILES // BLOCKS, False, 3)

        def scaled_rotations(dve):
            count = [0]

            def step(ins):
                count[0] += 1
                ins.then_inc(rot_steps, 1)
                dve.wait_ge(rot_steps, count[0])

            def mul(o, a, b):
                step(dve.tensor_tensor(o, a, b, ALU.mult))

            rt = y1[:].rearrange("p r h a b -> p (r h a b)").rearrange("p (n l t) -> p n l t", n=4, l=DEPTH)
            dve.wait_ge(first_rotations, 1)
            double(dve, mul, step, rt, EARLY, SEQ)
            for part in range(2):
                mul(rot_scaled[:, part], rot[:, part], vec[:, :, SC_LIN].unsqueeze(2).to_broadcast([P, DEPTH, SEQ]))

        def is_last(q):
            return isinstance(q, int) and q == N_CHUNK - 1

        def tile(q, b, lag):
            t = BLOCKS * q + (b - lag)
            return None if isinstance(t, int) and not 0 <= t < TILES else t

        def place(t, s4d):
            text = t < BATCH if isinstance(t, int) else s4d
            return hT[:, bass.ds(t if text else t - BATCH, 1), (P if text else 0):(2 * P if text else P)].rearrange("d o t -> d (o t)")

        def carry(eng):
            eng.sem_inc(waited, 1)

        @block.sync
        def _(sp):
            sp.dma_start(ldt[:], log_dt.to_broadcast([P, TOK])).then_inc(par_in, 16)
            for slot in range(2):
                sp.dma_start(par[slot * STATES:(slot + 1) * STATES], tok_a).then_inc(par_in, 16)
            sp.dma_start(vec[:], vecs).then_inc(vec_in, 16)
            for part, dst in enumerate((c_re, c_im)):
                for slot in range(2):
                    sp.dma_start(dst[slot * STATES:(slot + 1) * STATES], tok_c[part]).then_inc(c_in, 16)
            sp.dma_start(wts[:], win_t).then_inc(win_in, 16)
            sp.dma_start(bin_sb[:], bin_).then_inc(win_in, 16)
            def load_text(t, r):
                sp.wait_ge(xhat_made, free(t))
                sp.dma_start(raw[:, r], txt[bass.ds(t, 1)].rearrange("o s v -> (o s) v")).then_inc(raw_in[r], 16)

            def store_block(q, b):
                sp.wait_ge(k_moved, 2 * made(BLOCKS * q + b))
                sp.dma_start(tok_rows[bass.ds(q * H_CHUNK + b * H_BLOCK, H_BLOCK)].rearrange("h c (a l) -> (c a) h l", l=P),
                             rows_out[:, b % RING]).then_inc(rows_stored[b % RING], 16)

            for t in range(LONG_RING - 1):
                load_text(t, t)
            with sp.Fori(0, N_CHUNK - 1) as q:
                for b in range(BLOCKS):
                    load_text(BLOCKS * q + (b + LONG_RING - 1), (b - 1) % LONG_RING)
                    store_block(q, b)
            load_text(BATCH - 1, LONG_RING - 1)
            for b in range(BLOCKS):
                store_block(N_CHUNK - 1, b)
            for r in range(RING):
                sp.wait_ge(rows_stored[r], 16 * (N_BLOCK // RING + 1))
            with sp.Fori(0, BATCH // LONG_RING) as i:
                for b in range(LONG_RING):
                    sp.wait_ge(xhat_made, free(LONG_RING * i + (b + BATCH)))
                    sp.dma_start(raw[:, b], tok_rows[:, bass.ds(LONG_RING * i + b, 1)].rearrange("s o v -> s (o v)")).then_inc(raw_in[b], 16)
            sp.dma_start(b1_sb[:], b1).then_inc(ffn_in, 16)
            sp.dma_start(w1[:], w1_t[0]).then_inc(ffn_in, 16)
            sp.dma_start(w2[:], w2_t[0]).then_inc(ffn_in, 16)
            sp.wait_ge(ffn_in, 48)

        EARLY = 16

        def double(eng, mul, step, rt, m, end):
            while m < end:
                k = min(m, SEQ - 1 - m)
                here = lambda part: rot[:, part, :, 1:1 + k]
                turn = lambda part: rot[:, part, :, m:m + 1].to_broadcast([P, DEPTH, k])
                for n, (a, b) in enumerate(((0, 0), (1, 1), (0, 1), (1, 0))):
                    mul(rt[:, n, :, 0:k], here(a), turn(b))
                step(eng.tensor_tensor(rot[:, 0, :, m + 1:m + 1 + k], rt[:, 0, :, 0:k], rt[:, 1, :, 0:k], ALU.subtract))
                step(eng.tensor_tensor(rot[:, 1, :, m + 1:m + 1 + k], rt[:, 2, :, 0:k], rt[:, 3, :, 0:k], ALU.add))
                m *= 2

        def mixer_tables(pool):
            count = [0]

            def step(ins):
                count[0] += 1
                ins.then_inc(pool_small, 1)
                pool.wait_ge(pool_small, count[0])

            def mul(o, a, b):
                step(pool.tensor_tensor(o, a, b, ALU.mult))

            rt = y2[:].rearrange("p r h a b -> p (r h a b)").rearrange("p (n l t) -> p n l t", n=4, l=DEPTH)
            v = lambda k: vec[:, :, k]
            t = lambda k: ph[:, k]
            pool.wait_ge(vec_in, 16)
            mul(t(0), v(PHZ_RE), v(PHZ_RE))
            mul(t(1), v(PHZ_IM), v(PHZ_IM))
            step(pool.tensor_tensor(t(0), t(0), t(1), ALU.add))
            step(pool.tensor_tensor(t(2), t(0), half[:], ALU.pow))
            step(pool.tensor_scalar(t(1), t(0), 1e-37, None, ALU.max))
            step(pool.tensor_tensor(t(1), t(1), minus_half[:], ALU.pow))
            step(pool.tensor_scalar(t(3), t(2), 0.0, None, ALU.is_equal))
            pool.wait_ge(dve_small, 2)
            chunk_exponents(pool, 0)
            mul(t(4), v(PHZ_RE), t(1))
            step(pool.tensor_tensor(rot[:, 0, :, 1], t(4), t(3), ALU.add))
            mul(rot[:, 1, :, 1], v(PHZ_IM), t(1))
            step(pool.memset(rot[:, 0, :, 0], 1.0))
            step(pool.memset(rot[:, 1, :, 0], 0.0))
            double(pool, mul, step, rt, 1, EARLY)
            c, s_ = rot[:, 0, :, 1], rot[:, 1, :, 1]
            mul(t(0), c, v(LC_RE))
            mul(t(1), s_, v(LC_IM))
            step(pool.tensor_tensor(state0[:, 0], t(0), t(1), ALU.subtract))
            mul(t(0), s_, v(LC_RE))
            mul(t(1), c, v(LC_IM))
            step(pool.tensor_tensor(t(0), t(0), t(1), ALU.add))
            step(pool.tensor_scalar(state0[:, 1], t(0), -1.0, None, ALU.mult))

        def chunk_exponents(pool, q):
            pool.tensor_tensor(
                mag[:], small[:, 0, bass.ds(q * H_CHUNK, H_CHUNK)].unsqueeze(2).to_broadcast([P, H_CHUNK, NJ]),
                powers[:].unsqueeze(1).to_broadcast([P, H_CHUNK, NJ]), ALU.mult).then_inc(decay_made, 1)

        @block.gpsimd
        def _(pool):
            pool.memset(half[:], 0.5).then_inc(consts, 1)
            pool.memset(ident[:], 0.0).then_inc(consts, 1)
            pool.memset(minus_half[:], -0.5).then_inc(consts, 1)
            pool.iota(powers[:, 0:NA], pattern=[[P, NA]], base=0, channel_multiplier=0,
                      allow_small_or_imprecise_dtypes=True).then_inc(consts, 1)
            pool.iota(powers[:, NA:NA + NB1], pattern=[[NB0, NB1]], base=0, channel_multiplier=0,
                      allow_small_or_imprecise_dtypes=True).then_inc(consts, 1)
            pool.iota(powers[:, NA + NB1:NJ], pattern=[[1, NB0]], base=0, channel_multiplier=0,
                      allow_small_or_imprecise_dtypes=True).then_inc(consts, 1)
            pool.memset(eps[:], EPS).then_inc(consts, 1)
            pool.memset(half_pi[:], 0.5 * np.pi).then_inc(consts, 1)
            pool.wait_ge(consts, 2)
            pool.affine_select(out=ident[:], in_=ident[:], compare_op=ALU.not_equal, fill=1.0, base=0,
                               pattern=[[-1, P]], channel_multiplier=1).then_inc(consts, 1)
            pool.sem_inc(x2_made, 1)
            pool.sem_inc(y2_made, 1)
            pool.wait_ge(consts, CONSTS)
            mixer_tables(pool)
            pool.sem_inc(first_rotations, 1)
            pool.wait_ge(c_in, 64)
            pool.wait_ge(coef_made, 1)

            def tables(q):
                hq = bass.ds(q * H_CHUNK, H_CHUNK)
                ab = slice(0, NA + NB1)
                base = q * POOL_TABLES
                pool.wait_ge(mag_made, q + 1)
                pool.wait_ge(sincos_made, 2 * q + 2)
                if not (isinstance(q, int) and q == 0):
                    pool.wait_ge(dve_tables, q * DVE_TABLES)
                pool.tensor_tensor(w_im[:], mag[:, :, ab], sin[:, :, ab], ALU.mult).then_inc(pool_tables, 1)
                pool.wait_ge(pool_tables, base + 1)
                for k, c in ((1, beta), (3, alpha)):
                    pool.tensor_tensor(pt[:, k], w_im[:, :, 0:NA], c[:, hq].unsqueeze(2).to_broadcast([P, H_CHUNK, NA]),
                                       ALU.mult).then_inc(pool_tables, 1)
                pool.wait_ge(pool_tables, base + 3)
                pool.wait_ge(dve_tables, q * DVE_TABLES + 7)
                pool.tensor_tensor(p2[:], pt[:, 2], pt[:, 3], ALU.subtract).then_inc(pool_tables, 1)
                pool.wait_ge(pool_tables, base + 4)

            def slot(q, b, s4d):
                if s4d:
                    n = q * BLOCKS + b
                    r = b % RING
                    hs = slice(b * H_BLOCK, (b + 1) * H_BLOCK)
                    if b == 0:
                        tables(q)
                    pool.wait_ge(vv_made, free(n))
                    pool.tensor_tensor(
                        y2[:, r], w_im[:, hs, NA:].unsqueeze(3).to_broadcast([P, H_BLOCK, NB1, NB0]),
                        n2[:, hs].unsqueeze(2).to_broadcast([P, H_BLOCK, NB1, NB0]), ALU.mult).then_inc(y2_made, 1)
                    pool.wait_ge(k_done, 2 * free(n))
                    pool.tensor_tensor(
                        x2[:, r], c_im[:, bass.ds(q * H_CHUNK + b * H_BLOCK, H_BLOCK)].unsqueeze(3).to_broadcast([P, H_BLOCK, BATCH, NA]),
                        p2[:, hs].unsqueeze(2).to_broadcast([P, H_BLOCK, BATCH, NA]), ALU.mult).then_inc(x2_made, 1)
                t = tile(q, b, 1)
                if t is not None:
                    at = (b - 1) % LONG_RING
                    pool.wait_ge(mv_made, t + 1)
                    pool.tensor_tensor(var_eps[:, at:at + 1], mv[:, at, 1:2], eps[:], ALU.add).then_inc(ve_made, 1)
                    pool.wait_ge(ve_made, t + 1)
                    pool.tensor_tensor(rstd[:, at:at + 1], var_eps[:, at:at + 1], minus_half[:, 0:1], ALU.pow).then_inc(rstd_made, 1)
                    pool.wait_ge(rstd_made, t + 1)
                    carry(pool)
                    pool.tensor_scalar(shift[:, at:at + 1], mv[:, at, 0:1], rstd[:, at:at + 1], -1.0, ALU.mult, ALU.mult).then_inc(shift_made, 1)
                if s4d and b == 0 and not is_last(q):
                    pool.wait_ge(dve_tables, (q + 1) * DVE_TABLES)
                    chunk_exponents(pool, q + 1)

            slots(pool, slot)

        @block.vector
        def _(dve):
            count = [0]

            def step(*several):
                for ins in several:
                    count[0] += 1
                    ins.then_inc(dve_small, 1)
                dve.wait_ge(dve_small, count[0])

            def turns_first(q):
                hq = bass.ds(q * H_CHUNK, H_CHUNK)
                dve.tensor_tensor(turns[:], small[:, RHO, hq].unsqueeze(2).to_broadcast([P, H_CHUNK, NJ]),
                                  powers[:].unsqueeze(1).to_broadcast([P, H_CHUNK, NJ]), ALU.mult).then_inc(turns_steps, 1)
                dve.wait_ge(turns_steps, q * TURN_STEPS + 1)
                dve.tensor_scalar(whole_turns[:], turns[:], ROUND, ROUND, ALU.add, ALU.subtract).then_inc(turns_steps, 1)

            def turns_second(q):
                dve.wait_ge(turns_steps, q * TURN_STEPS + 2)
                dve.tensor_tensor(turns[:], turns[:], whole_turns[:], ALU.subtract).then_inc(turns_steps, 1)

            S = lambda k: small[:, k]
            X, THETA, K, R, RHO, DT, EAR, T, OMT, EM1, E, S2, ER, EI, NR, NI, A2, Q, GR, GI, TA, TB, AR, TC = range(24)
            TD = K
            dve.wait_ge(consts, CONSTS)
            step(dve.tensor_scalar(center[:], ident[:], -1.0 / DIM, None, ALU.add))
            dve.wait_ge(act_small, 2)
            step(dve.scalar_tensor_tensor(S(X), S(EAR), -1.0, S(DT), ALU.mult, ALU.mult),
                 dve.tensor_tensor(S(THETA), par[:, 1], S(DT), ALU.mult))
            step(dve.tensor_scalar(S(K), S(THETA), INV_2PI, ROUND, ALU.mult, ALU.add))
            step(dve.tensor_scalar(S(K), S(K), ROUND, None, ALU.subtract),
                 dve.tensor_scalar(S(AR), S(EAR), -1.0, None, ALU.mult))
            step(dve.scalar_tensor_tensor(S(R), S(K), -PI2_A, S(THETA), ALU.mult, ALU.add))
            step(dve.scalar_tensor_tensor(S(R), S(K), -PI2_B, S(R), ALU.mult, ALU.add))
            step(dve.scalar_tensor_tensor(S(R), S(K), -PI2_C, S(R), ALU.mult, ALU.add))
            step(dve.tensor_scalar(S(RHO), S(R), INV_2PI, None, ALU.mult))
            step(dve.tensor_scalar(S(R), S(R), PI_IN, -PI_IN, ALU.min, ALU.max))
            turns_first(0)
            turns_second(0)
            dve.wait_ge(act_small, 5)
            step(dve.tensor_scalar(S(OMT), S(T), -1.0, 1.0, ALU.mult, ALU.add),
                 dve.tensor_tensor(S(TA), S(S2), S(S2), ALU.mult),
                 dve.tensor_tensor(S(TC), S(AR), S(AR), ALU.mult),
                 dve.tensor_tensor(S(TD), par[:, 1], par[:, 1], ALU.mult))
            step(dve.reciprocal(S(Q), S(OMT)),
                 dve.tensor_tensor(S(A2), S(TC), S(TD), ALU.add))
            step(dve.scalar_tensor_tensor(S(EM1), S(T), 2.0, S(Q), ALU.mult, ALU.mult))
            step(dve.tensor_scalar(S(E), S(EM1), 1.0, None, ALU.add),
                 dve.reciprocal(S(Q), S(A2)))
            step(dve.tensor_tensor(S(TA), S(TA), S(E), ALU.mult),
                 dve.tensor_tensor(S(EI), S(EI), S(E), ALU.mult))
            step(dve.scalar_tensor_tensor(S(ER), S(TA), -2.0, S(EM1), ALU.mult, ALU.add))

            def complex_times(re, im, a_re, a_im, b_re, b_im, conj):
                one, two = (ALU.add, ALU.subtract) if conj else (ALU.subtract, ALU.add)
                step(dve.tensor_tensor(S(TA), a_re, b_re, ALU.mult),
                     dve.tensor_tensor(S(TB), a_im, b_im, ALU.mult),
                     dve.tensor_tensor(S(TC), a_im, b_re, ALU.mult),
                     dve.tensor_tensor(S(TD), a_re, b_im, ALU.mult))
                step(dve.tensor_tensor(re, S(TA), S(TB), one),
                     dve.tensor_tensor(im, S(TC), S(TD), two))

            complex_times(S(NR), S(NI), S(ER), S(EI), S(AR), par[:, 1], True)
            complex_times(S(GR), S(GI), S(NR), S(NI), par[:, 2], par[:, 3], False)
            step(dve.tensor_tensor(S(GR), S(GR), S(Q), ALU.mult),
                 dve.tensor_tensor(S(GI), S(GI), S(Q), ALU.mult))
            upper, lower = slice(0, STATES), slice(STATES, P)
            step(*(dve.tensor_scalar(dst[ps], small[ps, src], f, None, ALU.mult) for dst, ps, src, f in (
                (alpha, upper, GR, 2.0), (alpha, lower, GI, -2.0), (beta, upper, GI, -2.0), (beta, lower, GR, -2.0))))
            dve.sem_inc(coef_made, 1)
            dve.sem_inc(vv_made, RING)
            dve.wait_ge(c_in, 64)

            def tables(q):
                hq = bass.ds(q * H_CHUNK, H_CHUNK)
                ab = slice(0, NA + NB1)
                b0 = slice(NA + NB1, NJ)
                re, im = slice(0, STATES), slice(STATES, P)
                base = q * DVE_TABLES
                dve.wait_ge(mag_made, q + 1)
                dve.wait_ge(sincos_made, 2 * q + 2)
                dve.tensor_tensor(w_re[:], mag[:, :, ab], cos[:, :, ab], ALU.mult).then_inc(dve_tables, 1)
                dve.tensor_tensor(n1[re], mag[re, :, b0], cos[re, :, b0], ALU.mult).then_inc(dve_tables, 1)
                dve.wait_ge(dve_tables, base + 1)
                dve.wait_ge(x2_made, free(BLOCKS * q))
                for k, c in ((0, alpha), (2, beta)):
                    dve.tensor_tensor(pt[:, k], w_re[:, :, 0:NA], c[:, hq].unsqueeze(2).to_broadcast([P, H_CHUNK, NA]),
                                      ALU.mult).then_inc(dve_tables, 1)
                dve.wait_ge(y2_made, free(BLOCKS * q))
                dve.tensor_tensor(n1[im], mag[im, :, b0], sin[im, :, b0], ALU.mult).then_inc(dve_tables, 1)
                dve.scalar_tensor_tensor(n2[re], mag[re, :, b0], -1.0, sin[re, :, b0], ALU.mult, ALU.mult).then_inc(dve_tables, 1)
                dve.tensor_tensor(n2[im], mag[im, :, b0], cos[im, :, b0], ALU.mult).then_inc(dve_tables, 1)
                dve.wait_ge(pool_tables, q * POOL_TABLES + 2)
                dve.wait_ge(dve_tables, base + 7)
                dve.tensor_tensor(p1[:], pt[:, 0], pt[:, 1], ALU.add).then_inc(dve_tables, 1)
                dve.wait_ge(dve_tables, base + 8)

            def slot(q, b, s4d):
                if s4d:
                    n = q * BLOCKS + b
                    r = b % RING
                    hs = slice(b * H_BLOCK, (b + 1) * H_BLOCK)
                    if b == 0:
                        tables(q)
                    dve.wait_ge(k_done, 2 * free(n))
                    dve.tensor_tensor(
                        y1[:, r], w_re[:, hs, NA:].unsqueeze(3).to_broadcast([P, H_BLOCK, NB1, NB0]),
                        n1[:, hs].unsqueeze(2).to_broadcast([P, H_BLOCK, NB1, NB0]), ALU.mult).then_inc(y1_made, 1)
                    dve.tensor_tensor(
                        x1[:, r], c_re[:, bass.ds(q * H_CHUNK + b * H_BLOCK, H_BLOCK)].unsqueeze(3).to_broadcast([P, H_BLOCK, BATCH, NA]),
                        p1[:, hs].unsqueeze(2).to_broadcast([P, H_BLOCK, BATCH, NA]), ALU.mult).then_inc(x1_made, 1)
                    dve.wait_ge(y1_made, n + 1)
                    dve.wait_ge(y2_made, made(n, 1))
                    dve.tensor_tensor(vv[:, r], y1[:, r].rearrange("p h a b -> p h (a b)"),
                                      y2[:, r].rearrange("p h a b -> p h (a b)"), ALU.add).then_inc(vv_made, 1)
                if isinstance(q, int) and q == N_CHUNK and b == 0:
                    scaled_rotations(dve)
                t = tile(q, b, 0)
                if t is not None:
                    dve.wait_ge(raw_in[b], 16 * q + 16)
                    for k in range(2):
                        dve.bn_stats(stats[:, b, k], raw[:, b, k * 512:(k + 1) * 512]).then_inc(stats_made, 1)
                if s4d and not is_last(q):
                    if b == 0:
                        dve.wait_ge(sincos_made, 2 * q + 2)
                        turns_first(q + 1)
                    if b == 1:
                        turns_second(q + 1)
                if t is not None:
                    dve.wait_ge(stats_made, 2 * t + 2)
                    carry(dve)
                    dve.bn_aggr(mv[:, b], stats[:, b].rearrange("p a b -> p (a b)")).then_inc(mv_made, 1)

            slots(dve, slot)

        @block.scalar
        def _(act):
            X, THETA, K, R, RHO, DT, EAR, T, OMT, EM1, E, S2, ER, EI = range(14)
            for r in range(RING):
                act.sem_inc(rows_stored[r], 16)
            act.sem_inc(k_moved, 2 * RING)
            act.sem_inc(xhat_made, LONG_RING)
            act.sem_inc(xT_moved, 2)
            act.sem_inc(win_moved, RING)
            act.wait_ge(consts, CONSTS)
            act.activation(warm[:], half_pi[:], ACT.Exp)
            act.wait_ge(par_in, 48)
            act.activation(small[:, DT], ldt[:], ACT.Exp).then_inc(act_small, 1)
            act.activation(small[:, EAR], par[:, 0], ACT.Exp).then_inc(act_small, 1)
            act.wait_ge(dve_small, 2)
            act.activation(small[:, T], small[:, X], ACT.Tanh, scale=0.5).then_inc(act_small, 1)

            def decay(q):
                act.wait_ge(decay_made, q + 1)
                act.activation(mag[:], mag[:], ACT.Exp).then_inc(mag_made, 1)

            def sines(q):
                act.wait_ge(turns_steps, (q + 1) * TURN_STEPS)
                act.activation(whole_turns[:], turns[:], ACT.Abs).then_inc(abs_made, 1)
                act.activation(sin[:], turns[:], ACT.Sin, scale=TURN).then_inc(sincos_made, 1)
                act.wait_ge(abs_made, q + 1)
                act.activation(cos[:], whole_turns[:], ACT.Sin, scale=-TURN, bias=half_pi[:]).then_inc(sincos_made, 1)

            act.wait_ge(pool_small, 4)
            act.activation(rate[:], ph[:, 2], ACT.Tanh)
            decay(0)
            act.wait_ge(dve_small, 11)
            act.activation(small[:, EI], small[:, R], ACT.Sin).then_inc(act_small, 1)
            act.activation(small[:, S2], small[:, R], ACT.Sin, scale=0.5).then_inc(act_small, 1)
            sines(0)

            def slot(q, b, s4d):
                def move_rows(k):
                    n = q * BLOCKS + b
                    r = b % RING
                    act.wait_ge(k_done, 2 * n + (k + 1 + 2 * RING))
                    act.activation(rows_out[:, r, 4 * k:4 * k + 4], k_ps[r][k][:], ACT.Copy).then_inc(k_moved, 1)

                def normalize():
                    t = tile(q, b, 1)
                    if t is not None:
                        at = (b - 1) % LONG_RING
                        act.wait_ge(shift_made, t + 1)
                        act.wait_ge(xT_done, 2 * free(t))
                        carry(act)
                        act.activation(xhat[:, (b - 1) % RING], raw[:, at], ACT.Identity, bias=shift[:, at:at + 1],
                                       scale=rstd[:, at:at + 1]).then_inc(xhat_made, 1)

                if not s4d:
                    normalize()
                if s4d:
                    if b == 0 and not is_last(q):
                        decay(q + 1)
                    if b == 1 and not is_last(q):
                        act.wait_ge(pool_tables, (q + 1) * POOL_TABLES)
                        act.wait_ge(dve_tables, (q + 1) * DVE_TABLES)
                        sines(q + 1)
                    act.wait_ge(rows_stored[b % RING], q * (8 * BLOCKS) + 8 * (b - b % RING + RING))
                    move_rows(0)
                t = tile(q, b, 2)
                if t is not None:
                    at = (b - 2) % RING
                    act.wait_ge(win_done, free(t))
                    for k in range(2):
                        act.wait_ge(xT_done, 2 * t + (k + 1 + 2 * RING))
                        act.activation(xT[:, at, 4 * k:4 * k + 4], t_ps[k][:], ACT.Copy).then_inc(xT_moved, 1)
                if s4d:
                    move_rows(1)
                if s4d:
                    normalize()
                t = tile(q, b, 3)
                if t is not None:
                    act.wait_ge(win_done, made(t))
                    carry(act)
                    act.activation(place(t, s4d), w_ps[(b - 3) % RING][:, 0:P], ACT.Identity, bias=bin_sb[:]).then_inc(win_moved, 1)

            act.wait_ge(win_in, 32)
            slots(act, slot)

        @block.tensor
        def _(pe):
            pe.sem_inc(k_done, 2 * RING)
            pe.sem_inc(xT_done, 2 * RING)
            pe.sem_inc(win_done, RING)

            def slot(q, b, s4d):
                def expand(k):
                    n = q * BLOCKS + b
                    r = b % RING
                    if k == 0:
                        pe.wait_ge(x1_made, n + 1)
                        pe.wait_ge(x2_made, made(n, 1))
                        pe.wait_ge(vv_made, made(n))
                    pe.wait_ge(k_moved, 2 * n + (k + 1))
                    for g in range(4):
                        h = 4 * k + g
                        for x in (x1, x2):
                            mm = pe.matmul(k_ps[r][k][:, g], x[:, r, h].rearrange("p c a -> p (c a)"), vv[:, r, h],
                                           start=(x is x1), stop=(x is x2))
                    mm.then_inc(k_done, 1)

                if s4d:
                    expand(0)
                t = tile(q, b, 2)
                if t is not None:
                    at = (b - 2) % RING
                    pe.wait_ge(xhat_made, made(t, LONG_RING))
                    for k in range(2):
                        pe.wait_ge(xT_moved, 2 * t + (k + 1))
                        for c in range(4):
                            mm = pe.transpose(t_ps[k][:, c], xhat[:, at, (4 * k + c) * P:(4 * k + c + 1) * P], ident[:])
                        mm.then_inc(xT_done, 1)
                if s4d:
                    expand(1)
                t = tile(q, b, 3)
                if t is not None:
                    at = (b - 3) % RING
                    pe.wait_ge(xT_moved, 2 * made(t, 1))
                    pe.wait_ge(win_moved, free(t))
                    for c in range(KC):
                        mm = pe.matmul(w_ps[at][:, 0:P], wts[:, c], xT[:, at, c], start=(c == 0), stop=(c == KC - 1))
                    mm.then_inc(win_done, 1)

            pe.wait_ge(win_in, 32)
            slots(pe, slot)


def mixer(nc, sb, psum, sem, w1_t, w2_t, experts, hT, ident, center, minus_half, vec, b1_sb, w1, w2,
          rot, rot_scaled, rate, state0, wf):
    with ExitStack() as ctx:
        def buf(name, shape, dt=F32):
            return sb(ctx, name, shape, dt)

        sq = [buf(f"sq{n}", [P, 4, P]) for n in (1, 2)]
        ss = [buf(f"ss{n}", [P, 4]) for n in (1, 2)]
        ve = [buf(f"ve{n}", [P, 4]) for n in (1, 2)]
        rstd = [buf(f"l_rstd{n}", [P, 4]) for n in (1, 2)]
        xn = [buf(f"xn{n}", [P, 4, P]) for n in (1, 2)]
        y = buf("y", [P, 2, SEQ])
        u_re = buf("u_re", [P, 2, SEQ])
        u_im = buf("u_im", [P, 2, SEQ])
        z_re = buf("z_re", [P, 2, SEQ])
        z_im = buf("z_im", [P, 2, SEQ])
        warm = buf("mixer_warm", [P, 1])
        c_re = buf("conv_re", [P, 2, SEQ])
        c_im = buf("conv_im", [P, 2, SEQ])
        h_mid = buf("h_mid", [P, 2, SEQ])
        y2 = buf("y2l", [P, UNIT])
        y2_hi = buf("y2_hi", [P, UNIT], F32R)
        y2_lo = buf("y2_lo", [P, UNIT], F32R)
        w1_hi = buf("w1_hi", [P, DFF], F32R)
        w1_lo = buf("w1_lo", [P, DFF], F32R)
        s = buf("s", [P, FC, UNIT])
        wf_raw = buf("wf_raw", [P, RING, WF_PIECE])

        c_ps = [psum(ctx, f"c_ps{n}", [P, 4, P]) for n in (1, 2)]
        t_ps = psum(ctx, "tl_ps", [P, 4 * P])
        m_ps = [psum(ctx, f"m_ps{n}", [P, UNIT]) for n in range(FC)]
        o_ps = psum(ctx, "o_ps", [P, UNIT])

        centered = [sem(ctx, f"centered{n}") for n in (1, 2)]
        squared = [sem(ctx, f"squared{n}") for n in (1, 2)]
        summed = [sem(ctx, f"summed{n}") for n in (1, 2)]
        ve_made = [sem(ctx, f"lve_made{n}") for n in (1, 2)]
        rstd_made = [sem(ctx, f"lrstd_made{n}") for n in (1, 2)]
        xn_made = [sem(ctx, f"xn_made{n}") for n in (1, 2)]
        turned = [sem(ctx, f"turned{n}") for n in (1, 2)]
        y_made = sem(ctx, "y_made")
        u_re_made = sem(ctx, "u_re_made")
        u_im_made = sem(ctx, "u_im_made")
        z_re_made = sem(ctx, "z_re_made")
        z_im_made = sem(ctx, "z_im_made")
        c_re_made = sem(ctx, "c_re_made")
        c_im_made = sem(ctx, "c_im_made")
        h_mid_made = sem(ctx, "h_mid_made")
        h1_made = sem(ctx, "h1_made")
        y2_made = sem(ctx, "y2l_made")
        y2_hi_made = sem(ctx, "y2_hi_made")
        y2_lo_made = sem(ctx, "y2_lo_made")
        w1_hi_made = sem(ctx, "w1_hi_made")
        w1_lo_made = sem(ctx, "w1_lo_made")
        m_done = sem(ctx, "m_done")
        s_made = sem(ctx, "s_made")
        o_done = sem(ctx, "o_done")
        res_made = sem(ctx, "res_made")
        waited = sem(ctx, "l_waited")
        w1_in = sem(ctx, "w1_in")
        w2_in = sem(ctx, "w2_in")
        piece_in = [sem(ctx, f"piece_in{r}") for r in range(RING)]
        hi_made = sem(ctx, "hi_made")
        lo_made = sem(ctx, "lo_made")
        block = ctx.enter_context(nc.Block())

        def slots(eng, slot):
            slot(-3, 0, -3, "N")
            slot(-2, 0, -2, "NA")
            slot(-1, 0, -1, "NAB")
            with eng.Fori(0, DEPTH - 1) as l:
                for g in range(GROUPS):
                    slot(GROUPS * l + g, l, g, "NABM")
            for g in range(GROUPS):
                slot(GROUPS * (DEPTH - 1) + g, DEPTH - 1, g, "NABM"[max(0, g + 4 - GROUPS):])

        def carry(eng):
            eng.sem_inc(waited, 1)

        def norms(stages):
            both = [(0, 3)] * ("N" in stages) + [(1, 1)] * ("B" in stages)
            return both if "M" in stages else both[::-1]

        def at(l, g, ahead):
            return l + (g + ahead) // GROUPS, (g + ahead) % GROUPS

        def of(l):
            return bass.ds(l, 1)

        def rows(g):
            return hT[:, 2 * g:2 * g + 2, :]

        @block.sync
        def _(sp):
            with sp.Fori(0, DEPTH - 1) as l:
                sp.wait_ge(w1_lo_made, l + 1)
                sp.dma_start(w1[:], w1_t[bass.ds(l + 1, 1)].rearrange("o p f -> (o p) f")).then_inc(w1_in, 16)
                for g in range(GROUPS):
                    n = GROUPS * l + g
                    sp.wait_ge(lo_made, free(n))
                    sp.dma_start(wf_raw[:, g % RING], experts[:, bass.ds(n * WF_PIECE, WF_PIECE)]).then_inc(piece_in[g % RING], 16)
                sp.wait_ge(o_done, GROUPS * l + (GROUPS + 1))
                sp.dma_start(w2[:], w2_t[bass.ds(l + 1, 1)].rearrange("o p c f -> (o p) c f")).then_inc(w2_in, 16)

        @block.gpsimd
        def _(pool):
            for k in range(2):
                pool.sem_inc(rstd_made[k], 1)
            pool.sem_inc(u_im_made, 1)
            pool.sem_inc(c_im_made, 1)
            pool.sem_inc(lo_made, RING)

            def split_w1(l):
                pool.wait_ge(w1_hi_made, l + 1)
                pool.tensor_tensor(w1_lo[:], w1[:], w1_hi[:].bitcast(F32), ALU.subtract).then_inc(w1_lo_made, 1)

            def rstd_of(k, u):
                pool.wait_ge(summed[k], made(u, 1))
                carry(pool)
                pool.tensor_scalar(ve[k][:], ss[k][:], 1.0 / DIM, EPS, ALU.mult, ALU.add).then_inc(ve_made[k], 1)
                pool.wait_ge(ve_made[k], u + 1)
                pool.wait_ge(xn_made[k], free(u))
                pool.tensor_tensor(rstd[k][:], ve[k][:], minus_half[:], ALU.pow).then_inc(rstd_made[k], 1)

            def slot(i, l, g, stages):
                if "A" in stages:
                    u = i + 2
                    la, _ = at(l, g, 2)
                    pool.wait_ge(y_made, made(u, 1))
                    pool.wait_ge(z_im_made, 2 * free(u))
                    carry(pool)
                    pool.tensor_tensor(u_im[:], y[:], rot[:, 1, of(la)].to_broadcast([P, 2, SEQ]), ALU.mult).then_inc(u_im_made, 1)
                for k, ahead in norms(stages):
                    rstd_of(k, i + ahead)
                if "A" in stages:
                    pool.wait_ge(z_im_made, 2 * made(u, 1))
                    pool.wait_ge(h1_made, free(u))
                    carry(pool)
                    pool.tensor_tensor(c_im[:], z_im[:], rot_scaled[:, 1, of(la)].to_broadcast([P, 2, SEQ]), ALU.mult).then_inc(c_im_made, 1)
                if "M" in stages and not isinstance(l, int):
                    pool.wait_ge(hi_made, i + 1)
                    carry(pool)
                    pool.tensor_tensor(wf[:, 1, bass.ds(i * WF_PIECE, WF_PIECE)], wf_raw[:, g % RING],
                                       wf[:, 0, bass.ds(i * WF_PIECE, WF_PIECE)].bitcast(F32), ALU.subtract).then_inc(lo_made, 1)
                    if g == GROUPS - 1:
                        split_w1(l + 1)

            split_w1(0)
            slots(pool, slot)

        @block.vector
        def _(dve):
            for k in range(2):
                dve.sem_inc(summed[k], 1)
                dve.sem_inc(xn_made[k], 1)
            dve.sem_inc(u_re_made, 1)
            dve.sem_inc(z_im_made, 2)
            dve.sem_inc(h1_made, 1)
            dve.sem_inc(y2_lo_made, 1)
            dve.sem_inc(res_made, GROUPS)

            def sum_squares(k, u):
                dve.wait_ge(squared[k], made(u, 1))
                dve.wait_ge(rstd_made[k], free(u))
                dve.tensor_reduce(ss[k][:], sq[k][:], AX.X, ALU.add).then_inc(summed[k], 1)

            def normalize(k, u):
                dve.wait_ge(rstd_made[k], made(u, 1))
                dve.wait_ge(turned[k], free(u))
                dve.tensor_tensor(xn[k][:], c_ps[k][:], rstd[k][:].unsqueeze(2).to_broadcast([P, 4, P]), ALU.mult).then_inc(xn_made[k], 1)

            def scans(dst, src, part, la, done):
                for n in range(2):
                    dve.tensor_tensor_scan(dst[:, n], rate[:, of(la)].to_broadcast([P, SEQ]), src[:, n],
                                           state0[:, part, of(la)], ALU.mult, ALU.add).then_inc(done, 1)

            def slot(i, l, g, stages):
                if "A" in stages:
                    u = i + 2
                    la, ga = at(l, g, 2)
                    dve.wait_ge(y_made, made(u, 1))
                    dve.tensor_tensor(u_re[:], y[:], rot[:, 0, of(la)].to_broadcast([P, 2, SEQ]), ALU.mult).then_inc(u_re_made, 1)
                    dve.wait_ge(u_re_made, made(u, 1))
                    scans(z_re, u_re, 0, la, z_re_made)
                if "M" in stages:
                    dve.wait_ge(y2_made, made(i, 1))
                    dve.wait_ge(m_done, FC * free(i))
                    carry(dve)
                    dve.tensor_tensor(y2_lo[:], y2[:], y2_hi[:].bitcast(F32), ALU.subtract).then_inc(y2_lo_made, 1)
                    for k, ahead in norms(stages):
                        sum_squares(k, i + ahead)
                if "A" in stages:
                    dve.wait_ge(u_im_made, made(u, 1))
                    dve.wait_ge(c_im_made, free(u))
                    scans(z_im, u_im, 1, la, z_im_made)
                if "M" not in stages:
                    for k, ahead in norms(stages):
                        sum_squares(k, i + ahead)
                    for k, ahead in norms(stages):
                        normalize(k, i + ahead)
                elif "N" in stages:
                    normalize(0, i + 3)
                if "A" in stages:
                    dve.wait_ge(z_re_made, 2 * u + 2)
                    dve.tensor_tensor(c_re[:], z_re[:], rot_scaled[:, 0, of(la)].to_broadcast([P, 2, SEQ]), ALU.mult).then_inc(c_re_made, 1)
                    dve.wait_ge(c_re_made, u + 1)
                    dve.tensor_tensor(h_mid[:], rows(ga), c_re[:], ALU.add).then_inc(h_mid_made, 1)
                if "M" in stages and "B" in stages:
                    normalize(1, i + 1)
                if "A" in stages:
                    dve.wait_ge(h_mid_made, u + 1)
                    dve.wait_ge(c_im_made, made(u, 1))
                    dve.tensor_tensor(rows(ga), h_mid[:], c_im[:], ALU.add).then_inc(h1_made, 1)
                if "M" in stages:
                    dve.wait_ge(o_done, made(i, 1))
                    flat = rows(g).rearrange("p n t -> p (n t)")
                    dve.scalar_tensor_tensor(flat, o_ps[:], vec[:, of(l), B2], flat, ALU.add, ALU.add).then_inc(res_made, 1)

            slots(dve, slot)

        @block.scalar
        def _(act):
            for k in range(2):
                act.sem_inc(squared[k], 1)
            act.sem_inc(y_made, 1)
            act.sem_inc(y2_made, 1)
            act.sem_inc(s_made, FC)

            def split_w1(l):
                act.wait_ge(w1_in, 16 * l + 16)
                act.wait_ge(m_done, FC * GROUPS * l + FC)
                act.activation(w1_hi[:], w1[:], ACT.Copy).then_inc(w1_hi_made, 1)

            def square(k, u):
                act.wait_ge(centered[k], made(u, 1))
                act.wait_ge(summed[k], free(u))
                act.activation(sq[k][:], c_ps[k][:], ACT.Square).then_inc(squared[k], 1)

            def hidden(i, l, j):
                act.wait_ge(m_done, FC * i + (j + 1 + FC))
                act.wait_ge(o_done, free(i))
                carry(act)
                act.activation(s[:, j], m_ps[j][:], ACT.Silu, bias=b1_sb[:, of(l), j]).then_inc(s_made, 1)

            def silu_rows(i, l, g):
                u = i + 3
                la, _ = at(l, g, 3)
                act.wait_ge(turned[0], made(u, 1))
                act.wait_ge(u_re_made, free(u))
                act.wait_ge(u_im_made, free(u))
                carry(act)
                act.activation(y[:].rearrange("p n t -> p (n t)"), t_ps[:], ACT.Silu, bias=vec[:, of(la), LN1_B],
                               scale=vec[:, of(la), LN1_W]).then_inc(y_made, 1)

            def ffn_input(i, l, g):
                u = i + 1
                lb, _ = at(l, g, 1)
                act.wait_ge(turned[1], made(u, 1))
                act.wait_ge(m_done, FC * free(u))
                for dst, done in ((y2_hi, y2_hi_made), (y2, y2_made)):
                    carry(act)
                    act.activation(dst[:], t_ps[:], ACT.Identity, bias=vec[:, of(lb), LN2_B],
                                   scale=vec[:, of(lb), LN2_W]).then_inc(done, 1)

            def slot(i, l, g, stages):
                for k, ahead in norms(stages):
                    square(k, i + ahead)
                if "M" in stages:
                    for j in range(FC):
                        hidden(i, l, j)
                    if g == GROUPS - 1 and not isinstance(l, int):
                        split_w1(l + 1)
                if "B" in stages and "M" not in stages:
                    ffn_input(i, l, g)
                if "N" in stages:
                    silu_rows(i, l, g)
                if "M" in stages and not isinstance(l, int):
                    act.wait_ge(piece_in[g % RING], 16 * (GROUPS // RING) * l + 16 * (g // RING + 1))
                    carry(act)
                    act.activation(wf[:, 0, bass.ds(i * WF_PIECE, WF_PIECE)], wf_raw[:, g % RING], ACT.Copy).then_inc(hi_made, 1)
                if "B" in stages and "M" in stages:
                    ffn_input(i, l, g)

            act.activation(warm[:], minus_half[:, 0:1], ACT.Silu)
            split_w1(0)
            slots(act, slot)

        @block.tensor
        def _(pe):
            for k in range(2):
                pe.sem_inc(centered[k], 1)
                pe.sem_inc(turned[k], 1)
            pe.sem_inc(m_done, FC)
            pe.sem_inc(o_done, 1)
            pe.sem_inc(w1_in, 16)
            pe.sem_inc(w2_in, 16)

            def center_rows(k, u, g):
                if k == 0:
                    pe.wait_ge(res_made, free(u))
                else:
                    pe.wait_ge(h1_made, made(u, 1))
                pe.wait_ge(xn_made[k], free(u))
                flat = rows(g).rearrange("p n t -> p (n t)")
                for c in range(4):
                    mm = pe.matmul(c_ps[k][:, c], flat[:, c * P:(c + 1) * P], center[:], start=True, stop=True)
                mm.then_inc(centered[k], 1)

            def turn_rows(k, u, other):
                pe.wait_ge(xn_made[k], made(u, 1))
                pe.wait_ge((y_made, y2_made)[k], free(u))
                if other is not None:
                    pe.wait_ge((y2_made, y_made)[k], made(other, 1))
                for c in range(4):
                    mm = pe.transpose(t_ps[:, c * P:(c + 1) * P], xn[k][:, c], ident[:])
                mm.then_inc(turned[k], 1)

            def first(i, j, high):
                w_hi, w_lo = (w[:, j * P:(j + 1) * P] for w in (w1_hi, w1_lo))
                if high:
                    if j == 0:
                        pe.wait_ge(y2_hi_made, i + 1)
                        pe.wait_ge(s_made, FC * i + FC)
                    pe.matmul(m_ps[j][:], w_hi, y2_hi[:], start=True, stop=False)
                    pe.matmul(m_ps[j][:], w_lo, y2_hi[:], start=False, stop=False)
                else:
                    if j == 0:
                        pe.wait_ge(y2_lo_made, made(i, 1))
                    pe.matmul(m_ps[j][:], w_hi, y2_lo[:], start=False, stop=True).then_inc(m_done, 1)

            def second(i, k):
                if k == 0:
                    pe.wait_ge(res_made, i + GROUPS)
                pe.wait_ge(s_made, FC * i + (k + 1 + FC))
                mm = pe.matmul(o_ps[:], w2[:, k], s[:, k], start=(k == 0), stop=(k == FC - 1))
                if k == FC - 1:
                    mm.then_inc(o_done, 1)

            def slot(i, l, g, stages):
                for k, ahead in norms(stages):
                    center_rows(k, i + ahead, at(l, g, ahead)[1])
                if "M" in stages:
                    if g == 0:
                        pe.wait_ge(w1_lo_made, l + 1)
                        pe.wait_ge(w2_in, 16 * l + 16)
                    for j, high in ((0, True), (1, True), (2, True), (0, False), (1, False), (3, True), (2, False), (3, False)):
                        first(i, j, high)
                    second(i, 0)
                    second(i, 1)
                if "B" in stages and "M" not in stages:
                    turn_rows(1, i + 1, i + 2)
                    turn_rows(0, i + 3, i + 1)
                elif "N" in stages:
                    turn_rows(0, i + 3, i if "M" in stages else None)
                if "M" in stages:
                    second(i, 2)
                    second(i, 3)
                if "B" in stages and "M" in stages:
                    turn_rows(1, i + 1, i + 3 if "N" in stages else None)

            slots(pe, slot)


def experts_stage(nc, sb, psum, sem, txt, row_bias, tok_rows, hT, ident, minus_half, vec, wf, out):
    with ExitStack() as ctx:
        def buf(name, shape, dt=F32):
            return sb(ctx, name, shape, dt)

        ER = EXPERTS * RANK
        mixed = buf("mixed", [P, RING, P])
        row = buf("row", [P, RING, VOC])
        bias = buf("bias", [P, 2, VOC])
        f_stats = buf("f_stats", [P, 6])
        f_mv = buf("f_mv", [P, 2])
        f_ve = buf("f_ve", [P, 1])
        f_rstd = buf("f_rstd", [P, 1])
        zn = buf("zn", [P, P])
        z = buf("z", [P, P])
        z_hi = buf("z_hi", [P, P], F32R)
        z_lo = buf("z_lo", [P, P], F32R)
        row_b = buf("row_b", [P, VOC])
        h2 = buf("h2", [P, VOC])
        h2_b = buf("h2_b", [P, RING, VOC])
        r_stats = buf("r_stats", [P, 2, 6])
        r_mv = buf("r_mv", [P, 2])
        r_ve = buf("r_ve", [P, 1])
        r_rstd = buf("r_rstd", [P, 1])
        xhat = buf("x2hat", [P, VOC])
        x_hi = buf("x_hi", [P, RING, VOC], F32R)
        x_lo = buf("x_lo", [P, RING, VOC], F32R)
        top = buf("top", [P, EXPERTS])
        top_at = buf("top_at", [P, EXPERTS], U32)
        top_at_f = buf("top_at_f", [P, 2])
        gap = buf("gap", [P, 1])
        warm = buf("experts_warm", [P, 1])
        ratio = buf("ratio", [P, 1])
        total = buf("total", [P, 1])
        share = buf("share", [P, 2])
        picked = buf("picked", [P, 2, EXPERTS])
        weight = buf("weight", [P, EXPERTS])
        number = buf("number", [P, EXPERTS])
        ag = buf("ag", [P, AG])
        low = buf("low", [P, ER])
        low_hi = buf("low_hi", [P, P], F32R)
        low_lo = buf("low_lo", [P, P], F32R)
        result = buf("result", [P, RING, VOC])

        f_ps = psum(ctx, "f_ps", [P, 4, P])
        ag_bank = psum(ctx, "ag_bank", [P, 512])
        ag_ps = ag_bank[:, 0:2 * AG].rearrange("p (k n) -> p k n", k=2)
        y_ps = psum(ctx, "y_ps", [P, VOC])
        x_ps = psum(ctx, "x_ps", [P, VOC])
        r_ps = psum(ctx, "r_ps", [P, VOC])

        mixed_turned = sem(ctx, "x_mixed_turned")
        f_counted = sem(ctx, "x_f_counted")
        f_aggregated = sem(ctx, "x_f_aggregated")
        f_ve_made = sem(ctx, "x_f_ve_made")
        f_rstd_made = sem(ctx, "x_f_rstd_made")
        zn_made = sem(ctx, "x_zn_made")
        zn_turned = sem(ctx, "x_zn_turned")
        z_made = sem(ctx, "x_z_made")
        z_hi_made = sem(ctx, "x_z_hi_made")
        z_lo_made = sem(ctx, "x_z_lo_made")
        row_b_made = sem(ctx, "x_row_b_made")
        y_done = sem(ctx, "x_y_done")
        h2_made = sem(ctx, "x_h2_made")
        h2_b_made = sem(ctx, "x_h2_b_made")
        r_counted = sem(ctx, "x_r_counted")
        r_aggregated = sem(ctx, "x_r_aggregated")
        r_ve_made = sem(ctx, "x_r_ve_made")
        r_rstd_made = sem(ctx, "x_r_rstd_made")
        xhat_made = sem(ctx, "x_xhat_made")
        x_turned = sem(ctx, "x_x_turned")
        x_hi_made = sem(ctx, "x_x_hi_made")
        x_lo_made = sem(ctx, "x_x_lo_made")
        ag_done = sem(ctx, "x_ag_done")
        ag_base_done = sem(ctx, "x_ag_base_done")
        weight_made = sem(ctx, "x_weight_made")
        ag_half_made = sem(ctx, "x_ag_half_made")
        ag_added = sem(ctx, "x_ag_added")
        gate_steps = sem(ctx, "x_gate_steps")
        ratio_made = sem(ctx, "x_ratio_made")
        low_made = sem(ctx, "x_low_made")
        low_turned = sem(ctx, "x_low_turned")
        low_hi_made = sem(ctx, "x_low_hi_made")
        low_lo_made = sem(ctx, "x_low_lo_made")
        r_done = sem(ctx, "x_r_done")
        result_made = sem(ctx, "x_result_made")
        x_constants = sem(ctx, "x_x_constants")
        x_waited = sem(ctx, "x_x_waited")
        bias_in = sem(ctx, "x_bias_in")
        mixed_in = [sem(ctx, f"mixed_in{r}") for r in range(RING)]
        row_in = [sem(ctx, f"row_in{r}") for r in range(RING)]
        stored = [sem(ctx, f"stored{r}") for r in range(RING)]
        block = ctx.enter_context(nc.Block())
        TILES = 2 * BATCH
        GATE_STEPS = 10

        def slots(eng, slot):
            with eng.Fori(0, BATCH - 1) as c:
                for p in range(RING):
                    slot(2 * c + p, p, c, 2)
            slot(TILES - 2, 0, BATCH - 1, 1)
            slot(TILES - 1, 1, BATCH - 1, 0)

        def carry(eng):
            eng.sem_inc(x_waited, 1)

        @block.sync
        def _(sp):
            def load(t, p, c):
                if not (isinstance(c, int) and c == 0):
                    sp.wait_ge(mixed_turned, free(t))
                    sp.dma_start(mixed[:, p], hT[:, bass.ds(c, 1), p * P:(p + 1) * P].rearrange("d o t -> d (o t)")).then_inc(mixed_in[p], 16)
                sp.wait_ge(row_b_made, free(t))
                src = tok_rows[:, bass.ds(c, 1)] if p == 0 else txt[bass.ds(c, 1)].rearrange("o s v -> s o v")
                sp.dma_start(row[:, p], src.rearrange("s o v -> s (o v)")).then_inc(row_in[p], 16)

            def store(t, p, c):
                sp.wait_ge(result_made, made(t))
                sp.dma_start(out[bass.ds(c, 1), p * P:(p + 1) * P].rearrange("o s v -> (o s) v"), result[:, p]).then_inc(stored[p], 16)

            load(0, 0, 0)
            for k in range(2):
                sp.dma_start(bias[:, k], row_bias[k:k + 1].to_broadcast([P, VOC])).then_inc(bias_in, 16)
            load(1, 1, 0)
            with sp.Fori(0, BATCH - 1) as c:
                for p in range(RING):
                    load(2 * c + (p + 2), p, c + 1)
                    store(2 * c + p, p, c)
            for p in range(RING):
                store(TILES - 2 + p, p, BATCH - 1)
            for p in range(RING):
                sp.wait_ge(stored[p], 16 * (BATCH + 1))

        @block.gpsimd
        def _(pool):
            pool.iota(number[:], pattern=[[1, EXPERTS]], base=0, channel_multiplier=0,
                      allow_small_or_imprecise_dtypes=True).then_inc(x_constants, 1)
            pool.sem_inc(row_b_made, RING)
            pool.sem_inc(h2_b_made, RING)
            pool.sem_inc(f_rstd_made, 1)
            pool.sem_inc(r_rstd_made, 1)

            def rstd_of(t, mv, ve, rstd, aggregated, ve_made, rstd_made, used):
                pool.wait_ge(aggregated, t + 1)
                pool.wait_ge(used, free(t))
                carry(pool)
                pool.tensor_scalar(ve[:], mv[:, 1:2], EPS, None, ALU.add).then_inc(ve_made, 1)
                pool.wait_ge(ve_made, t + 1)
                pool.tensor_tensor(rstd[:], ve[:], minus_half[:, 0:1], ALU.pow).then_inc(rstd_made, 1)

            def biased_row(t, p, c):
                pool.wait_ge(row_in[p], 16 * (c + 1))
                pool.wait_ge(h2_made, free(t))
                pool.tensor_tensor(row_b[:], row[:, p], bias[:, 0], ALU.add).then_inc(row_b_made, 1)

            def mixed_part(t):
                rstd_of(t, f_mv, f_ve, f_rstd, f_aggregated, f_ve_made, f_rstd_made, zn_made)

            def row_part(t, p):
                rstd_of(t, r_mv, r_ve, r_rstd, r_aggregated, r_ve_made, r_rstd_made, xhat_made)
                pool.wait_ge(h2_made, made(t, 1))
                pool.wait_ge(result_made, free(t))
                pool.tensor_tensor(h2_b[:, p], h2[:], bias[:, 1], ALU.add).then_inc(h2_b_made, 1)

            def slot(t, p, c, after):
                if after > 0:
                    row_part(t + 1, 1 - p)
                if after > 1:
                    biased_row(t + 2, p, c + 1)
                    mixed_part(t + 2)

            mixed_part(0)
            pool.wait_ge(bias_in, 32)
            biased_row(0, 0, 0)
            row_part(0, 0)
            biased_row(1, 1, 0)
            mixed_part(1)
            slots(pool, slot)

        @block.vector
        def _(dve):
            for n in (zn_made, z_lo_made, h2_made, xhat_made, ag_added, low_made, low_lo_made):
                dve.sem_inc(n, 1)
            dve.sem_inc(x_lo_made, RING)
            dve.sem_inc(result_made, RING)
            dve.wait_ge(x_constants, 1)

            def gate_pick(t):
                g = t * GATE_STEPS
                dve.wait_ge(ag_done, made(t, 1))
                dve.wait_ge(low_made, free(t))
                dve.tensor_copy(ag[:], ag_ps[:, 1]).then_inc(ag_half_made, 1)
                dve.wait_ge(ag_half_made, t + 1)
                dve.tensor_tensor(ag[:], ag_ps[:, 0], ag[:], ALU.add).then_inc(ag_added, 1)
                dve.wait_ge(ag_added, made(t, 1))
                carry(dve)
                dve.max(top[:], ag[:, ER:AG]).then_inc(gate_steps, 1)
                dve.wait_ge(gate_steps, g + 1)
                dve.tensor_tensor(gap[:], top[:, 1:2], top[:, 0:1], ALU.subtract).then_inc(gate_steps, 1)
                dve.max_index(top_at[:], top[:], ag[:, ER:AG]).then_inc(gate_steps, 1)
                dve.wait_ge(gate_steps, g + 3)
                dve.tensor_copy(top_at_f[:], top_at[:, 0:2]).then_inc(gate_steps, 1)
                dve.wait_ge(gate_steps, g + 4)
                for k in range(2):
                    dve.tensor_scalar(picked[:, k], number[:], top_at_f[:, k:k + 1], None, ALU.is_equal).then_inc(gate_steps, 1)

            def gate_weigh(t):
                g = t * GATE_STEPS
                dve.wait_ge(ratio_made, t + 1)
                dve.tensor_scalar(total[:], ratio[:], 0.5, 0.5, ALU.mult, ALU.add).then_inc(gate_steps, 1)
                dve.wait_ge(gate_steps, g + 7)
                dve.reciprocal(share[:, 0:1], total[:]).then_inc(gate_steps, 1)
                dve.wait_ge(gate_steps, g + 8)
                dve.tensor_tensor(share[:, 1:2], share[:, 0:1], ratio[:], ALU.mult).then_inc(gate_steps, 1)
                dve.wait_ge(gate_steps, g + 9)
                dve.tensor_scalar(weight[:], picked[:, 0], share[:, 0:1], None, ALU.mult).then_inc(gate_steps, 1)

            def low_rank(t):
                g = t * GATE_STEPS
                dve.wait_ge(gate_steps, g + 10)
                dve.scalar_tensor_tensor(weight[:], picked[:, 1], share[:, 1:2], weight[:], ALU.mult, ALU.add).then_inc(weight_made, 1)
                dve.wait_ge(weight_made, t + 1)
                dve.wait_ge(low_turned, t + 1)
                dve.tensor_tensor(low[:].rearrange("p (e r) -> p e r", e=EXPERTS), ag[:, 0:ER].rearrange("p (e r) -> p e r", e=EXPERTS),
                                  weight[:].unsqueeze(2).to_broadcast([P, EXPERTS, RANK]), ALU.mult).then_inc(low_made, 1)

            def finish(t, p):
                dve.wait_ge(r_done, made(t, 1))
                dve.wait_ge(stored[p], 8 * t + (16 - 8 * p))
                dve.wait_ge(h2_b_made, made(t))
                dve.tensor_tensor(result[:, p], r_ps[:], h2_b[:, p], ALU.add).then_inc(result_made, 1)

            def mixed_stats(t):
                dve.wait_ge(mixed_turned, made(t))
                dve.bn_stats(f_stats[:], f_ps[:, 0]).then_inc(f_counted, 1)
                dve.wait_ge(f_counted, t + 1)
                dve.wait_ge(f_rstd_made, free(t))
                carry(dve)
                dve.bn_aggr(f_mv[:], f_stats[:]).then_inc(f_aggregated, 1)

            def mixed_normal(t):
                dve.wait_ge(f_rstd_made, made(t, 1))
                dve.wait_ge(zn_turned, free(t))
                dve.tensor_scalar(zn[:], f_ps[:, 0], f_mv[:, 0:1], f_rstd[:], ALU.subtract, ALU.mult).then_inc(zn_made, 1)

            def mixed_low(t):
                dve.wait_ge(z_hi_made, t + 1)
                dve.wait_ge(y_done, free(t))
                dve.tensor_tensor(z_lo[:], z[:], z_hi[:].bitcast(F32), ALU.subtract).then_inc(z_lo_made, 1)

            def residual(t):
                dve.wait_ge(y_done, made(t, 1))
                dve.wait_ge(row_b_made, made(t))
                dve.wait_ge(h2_b_made, t + RING)
                dve.tensor_tensor(h2[:], y_ps[:], row_b[:], ALU.add).then_inc(h2_made, 1)
                dve.wait_ge(h2_made, made(t, 1))
                for k in range(2):
                    dve.bn_stats(r_stats[:, k], h2[:, k * 512:(k + 1) * 512]).then_inc(r_counted, 1)
                dve.wait_ge(r_counted, 2 * t + 2)
                dve.wait_ge(r_rstd_made, free(t))
                carry(dve)
                dve.bn_aggr(r_mv[:], r_stats[:].rearrange("p a b -> p (a b)")).then_inc(r_aggregated, 1)

            def row_normal(t):
                dve.wait_ge(r_rstd_made, made(t, 1))
                dve.wait_ge(x_turned, free(t))
                dve.tensor_scalar(xhat[:], h2[:], r_mv[:, 0:1], r_rstd[:], ALU.subtract, ALU.mult).then_inc(xhat_made, 1)

            def row_low(t, p):
                dve.wait_ge(x_hi_made, made(t))
                dve.tensor_tensor(x_lo[:, p], x_ps[:], x_hi[:, p].bitcast(F32), ALU.subtract).then_inc(x_lo_made, 1)

            def low_low(t):
                dve.wait_ge(low_hi_made, t + 1)
                dve.tensor_tensor(low_lo[:], f_ps[:, 2], low_hi[:].bitcast(F32), ALU.subtract).then_inc(low_lo_made, 1)

            def slot(t, p, c, after):
                gate_pick(t)
                if after > 0:
                    mixed_low(t + 1)
                gate_weigh(t)
                low_rank(t)
                if after > 0:
                    residual(t + 1)
                low_low(t)
                if after > 0:
                    row_normal(t + 1)
                    row_low(t + 1, 1 - p)
                if after > 1:
                    mixed_stats(t + 2)
                    mixed_normal(t + 2)
                finish(t, p)

            mixed_stats(0)
            mixed_normal(0)
            mixed_low(0)
            residual(0)
            row_normal(0)
            row_low(0, 0)
            mixed_stats(1)
            mixed_normal(1)
            slots(dve, slot)

        @block.scalar
        def _(act):
            act.sem_inc(z_made, 1)
            act.sem_inc(x_hi_made, RING)
            for p in range(RING):
                act.sem_inc(stored[p], 16)

            def ahead_z(t):
                act.wait_ge(zn_turned, made(t, 1))
                act.wait_ge(z_lo_made, free(t))
                act.activation(z[:], f_ps[:, 1], ACT.Identity, bias=vec[:, 0, LNL_B:LNL_B + 1],
                               scale=vec[:, 0, LNL_W:LNL_W + 1]).then_inc(z_made, 1)
                act.wait_ge(z_made, made(t, 1))
                act.wait_ge(y_done, free(t))
                act.activation(z_hi[:], z[:], ACT.Copy).then_inc(z_hi_made, 1)

            def ahead_x(t, p):
                act.wait_ge(x_turned, made(t, 1))
                act.wait_ge(ag_base_done, free(t))
                act.activation(x_hi[:, p], x_ps[:], ACT.Copy).then_inc(x_hi_made, 1)

            def slot(t, p, c, after):
                if p == 0:
                    act.activation(warm[:], minus_half[:, 0:1], ACT.Exp)
                if after > 0:
                    ahead_z(t + 1)
                act.wait_ge(gate_steps, t * GATE_STEPS + 2)
                act.activation(ratio[:], gap[:], ACT.Exp).then_inc(ratio_made, 1)
                act.wait_ge(low_turned, made(t, 1))
                act.wait_ge(r_done, free(t))
                act.activation(low_hi[:], f_ps[:, 2], ACT.Copy).then_inc(low_hi_made, 1)
                if after > 0:
                    ahead_x(t + 1, 1 - p)

            ahead_z(0)
            ahead_x(0, 0)
            slots(act, slot)

        @block.tensor
        def _(pe):
            pe.sem_inc(mixed_turned, RING)
            for n in (zn_turned, y_done, x_turned, ag_done, low_turned, r_done):
                pe.sem_inc(n, 1)
            pe.sem_inc(ag_base_done, RING)

            def turn_mixed(t, p, c):
                if isinstance(c, int) and c == 0:
                    src = hT[:, 0, p * P:(p + 1) * P]
                else:
                    src = mixed[:, p]
                    pe.wait_ge(mixed_in[p], 16 * c)
                pe.wait_ge(zn_made, free(t))
                pe.wait_ge(z_made, free(t))
                pe.transpose(f_ps[:, 0], src, ident[:]).then_inc(mixed_turned, 1)

            def turn_zn(t):
                pe.wait_ge(zn_made, made(t, 1))
                pe.transpose(f_ps[:, 1], zn[:], ident[:]).then_inc(zn_turned, 1)

            def wide(dst, x_hi_c, x_lo_c, at, start, stop):
                for k, (x, lo) in enumerate(((x_hi_c, False), (x_hi_c, True), (x_lo_c, False))):
                    for n in range(VOC // 512):
                        w = wf[:, int(lo), at + n * 512:at + (n + 1) * 512]
                        mm = pe.matmul(dst[:, n * 512:(n + 1) * 512], x, w, start=(start and k == 0), stop=(stop and k == 2))
                return mm

            def output(t):
                pe.wait_ge(z_lo_made, made(t, 1))
                pe.wait_ge(h2_made, free(t))
                wide(y_ps, z_hi[:], z_lo[:], WF_OUT, True, True).then_inc(y_done, 1)

            def turn_rows(t):
                pe.wait_ge(xhat_made, made(t, 1))
                pe.wait_ge(x_lo_made, t + RING)
                for c in range(KC):
                    mm = pe.transpose(x_ps[:, c * P:(c + 1) * P], xhat[:, c * P:(c + 1) * P], ident[:])
                mm.then_inc(x_turned, 1)

            def low_and_gate(t, p):
                pe.wait_ge(x_lo_made, made(t))
                pe.wait_ge(ag_added, free(t))
                for c in range(KC):
                    cs = slice(c * P, (c + 1) * P)
                    w = wf[:, :, WF_AG + c * AG:WF_AG + (c + 1) * AG]
                    if c == 0:
                        pe.matmul(ag_ps, x_hi[:, p, cs], w, start=True, stop=False)
                    pe.matmul(ag_ps[:, 0], x_lo[:, p, cs], w[:, 0], start=False, stop=False)
                    if c > 0:
                        mm = pe.matmul(ag_ps, x_hi[:, p, cs], w, start=False, stop=c == KC - 1)
                mm.then_inc(ag_done, 1)

            def base(t, p, chunks):
                if chunks[0] == 0:
                    pe.wait_ge(result_made, t + RING)
                for c in chunks:
                    cs = slice(c * P, (c + 1) * P)
                    mm = wide(r_ps, x_hi[:, p, cs], x_lo[:, p, cs], WF_BASE + c * VOC, c == 0, False)
                    if c == KC - 1:
                        mm.then_inc(ag_base_done, 1)

            def turn_low(t, after):
                if after:
                    pe.wait_ge(z_made, made(t + 1, 1))
                pe.wait_ge(low_made, made(t, 1))
                pe.wait_ge(low_lo_made, free(t))
                pe.transpose(f_ps[:, 2], low[:], ident[:]).then_inc(low_turned, 1)

            def low_output(t):
                pe.wait_ge(low_lo_made, made(t, 1))
                wide(r_ps, low_hi[:], low_lo[:], WF_B, False, True).then_inc(r_done, 1)

            def slot(t, p, c, after):
                low_and_gate(t, p)
                if after > 0:
                    turn_zn(t + 1)
                base(t, p, [0, 1])
                if after > 0:
                    output(t + 1)
                base(t, p, [2])
                turn_low(t, after > 0)
                base(t, p, [3, 4, 5])
                if after > 0:
                    turn_rows(t + 1)
                base(t, p, [6])
                if after > 1:
                    pe.wait_ge(low_lo_made, made(t, 1))
                    turn_mixed(t + 2, p, c + 1)
                base(t, p, [7])
                low_output(t)

            turn_mixed(0, 0, 0)
            turn_zn(0)
            output(0)
            turn_rows(0)
            turn_mixed(1, 1, 0)
            slots(pe, slot)


def kernel(x, txt, L0_tok_log_dt, L0_tok_B, L0_tok_inv_A_real, L0_tok_A_imag, L0_attn_Win, L0_attn_bin,
           L0_attn_ln1_w, L0_attn_ln1_b, L0_attn_phz_re, L0_attn_phz_im, L0_attn_lc_re, L0_attn_lc_im,
           L0_attn_sc_lin, L0_attn_ln2_w, L0_attn_ln2_b, L0_attn_W1, L0_attn_b1, L0_attn_W2, L0_attn_b2,
           L0_attn_lnl_w, L0_attn_lnl_b, L0_attn_Wout, L0_attn_bout, L0_ffn_gate_w, L0_ffn_base_w,
           L0_ffn_base_b, L0_ffn_lora_A, L0_ffn_lora_B):
    import concourse.bacc as bacc
    from concourse.bass_utils import run_bass_kernel_spmd

    arr = np.asarray
    per_layer = [L0_attn_ln1_w, L0_attn_ln1_b, L0_attn_phz_re, L0_attn_phz_im, L0_attn_lc_re, L0_attn_lc_im,
                 L0_attn_sc_lin, L0_attn_ln2_w, L0_attn_ln2_b, L0_attn_b2]
    once = [np.broadcast_to(arr(v), (DEPTH, DIM)) for v in (L0_attn_lnl_w, L0_attn_lnl_b)]

    def chunked(w):
        w = arr(w)
        return w.reshape(-1, P, w.shape[-1]).transpose(1, 0, 2)

    low_rank = np.concatenate([arr(L0_ffn_lora_A).reshape(EXPERTS * RANK, VOC), arr(L0_ffn_gate_w)], axis=0)
    laid_out = {
        "log_dt": arr(L0_tok_log_dt).reshape(1, TOK),
        "tok_a": np.stack([arr(L0_tok_inv_A_real).T, arr(L0_tok_A_imag).T, arr(L0_tok_B)[..., 0].T,
                           arr(L0_tok_B)[..., 1].T], axis=1),
        "tok_c": arr(x).transpose(3, 2, 1, 0),
        "txt": arr(txt),
        "win_t": chunked(arr(L0_attn_Win).T),
        "bin_": arr(L0_attn_bin).reshape(DIM, 1),
        "vecs": np.stack([arr(v) for v in per_layer] + once).transpose(2, 1, 0),
        "b1": arr(L0_attn_b1).reshape(DEPTH, FC, P).transpose(2, 0, 1),
        "w1_t": arr(L0_attn_W1).transpose(0, 2, 1),
        "w2_t": np.stack([chunked(w.T) for w in arr(L0_attn_W2)]),
        "experts": np.concatenate([chunked(w).reshape(P, -1) for w in (
            arr(L0_ffn_base_w).T, low_rank.T, arr(L0_attn_Wout).T,
            arr(L0_ffn_lora_B).transpose(0, 2, 1).reshape(EXPERTS * RANK, VOC))], axis=1),
        "row_bias": np.stack([arr(L0_attn_bout), arr(L0_ffn_base_b)]),
    }
    nc = bacc.Bacc("TRN2", target_bir_lowering=False, num_devices=1)
    arrays, args = {}, []
    for name, a in laid_out.items():
        arrays["in_" + name] = np.ascontiguousarray(a)
        args.append(nc.dram_tensor("in_" + name, a.shape, mybir.dt.from_np(a.dtype), kind="ExternalInput").ap())
    args.append(nc.dram_tensor("out", (BATCH, SEQ, VOC), F32, kind="ExternalOutput").ap())
    build(nc, *args)
    return run_bass_kernel_spmd(nc, [arrays], core_ids=[0]).results[0]["out"]
```
